# Optimizing a Trainium2 kernel written in Bass

```python
import numpy as np
import jax
import jax.numpy as jnp

def _softmax(x, axis=-1):
    return jax.nn.softmax(x, axis=axis)

def _gelu(x):
    return jax.nn.gelu(x, approximate=True)

def _silu(x):
    return jax.nn.silu(x)

def _sigmoid(x):
    return jax.nn.sigmoid(x)

def _layernorm(x, axis=-1, eps=1e-05):
    m = jnp.mean(x, axis=axis, keepdims=True)
    v = jnp.var(x, axis=axis, keepdims=True)
    return (x - m) / jnp.sqrt(v + eps)

def _scatter_add(tgt, idx, src, axis=0):
    return tgt.at[idx].add(src)

def _segment_sum(src, seg, n):
    return jax.ops.segment_sum(src, seg, n)
kernel_name = 'mk_gnn_preln_d2_gnn_r32_e48a27'

def setup_inputs(seed: int=0):
    np.random.seed(seed)
    _w = jnp.asarray

    def _rec_inputs():
        import jax
        import jax.numpy as jnp
        _gk = jax.random.key(seed)
        x = -0.000202 + 1 * jax.random.normal(jax.random.fold_in(_gk, 1), (50000, 128), jnp.float32)
        src = jax.random.randint(jax.random.fold_in(_gk, 2), (25000,), 0, 50000, jnp.int32)
        dst = jnp.minimum((50000 * jax.random.uniform(jax.random.fold_in(_gk, 3), (25000,)) ** 2.0).astype(jnp.int32), 49999)
        _o = jnp.argsort(dst, stable=True)
        src = src[_o]
        dst = dst[_o]
        edge_attr_128 = -8.16379e-05 + 0.999858 * jax.random.normal(jax.random.fold_in(_gk, 12), (25000, 128), jnp.float32)
        return (x, src, dst, edge_attr_128)
    x, src, dst, edge_attr_128 = _rec_inputs()

    def _L0_gnn_setup():
        import jax, jax.numpy as jnp
        import numpy as np
        N_NODES = 50000
        N_EDGES = 25000
        IN_FEAT = 128
        HEADS = 8
        HEAD_DIM = 16
        NEG_SLOPE = 0.2
        key = jax.random.key(seed)
        ks = jax.random.split(key, 8)
        g = 1.0 / np.sqrt(IN_FEAT)
        return {'x': jax.random.normal(ks[0], (N_NODES, IN_FEAT), jnp.float32), 'efeat': jax.random.normal(ks[1], (N_EDGES, IN_FEAT), jnp.float32), 'src': jax.random.randint(ks[2], (N_EDGES,), 0, N_NODES), 'dst': jax.random.randint(ks[3], (N_EDGES,), 0, N_NODES), 'W_src': jax.random.normal(ks[4], (HEADS * HEAD_DIM, IN_FEAT), jnp.float32) * g, 'b_src': jnp.zeros((HEADS * HEAD_DIM,), jnp.float32), 'W_dst': jax.random.normal(ks[5], (HEADS * HEAD_DIM, IN_FEAT), jnp.float32) * g, 'b_dst': jnp.zeros((HEADS * HEAD_DIM,), jnp.float32), 'W_edge': jax.random.normal(ks[6], (HEADS * HEAD_DIM, IN_FEAT), jnp.float32) * g, 'attn': jax.random.normal(ks[7], (HEADS, HEAD_DIM), jnp.float32) * (1.0 / np.sqrt(HEAD_DIM))}
    _L0_gnn_all = _L0_gnn_setup()
    _L0_gnn_in = {k: v for k, v in _L0_gnn_all.items() if k in ('W_src', 'b_src', 'W_dst', 'b_dst', 'W_edge', 'attn')}
    del _L0_gnn_all

    def _L1_gnn_setup():
        import jax, jax.numpy as jnp
        import numpy as np
        N_NODES = 50000
        N_EDGES = 25000
        NFEAT = 128
        NHID = 128
        BN_EPS = 1e-05
        key = jax.random.key(seed)
        ks = jax.random.split(key, 8)
        x = jax.random.normal(ks[0], (N_NODES, NFEAT), dtype=jnp.float32)
        edge_index = jax.random.randint(ks[1], (2, N_EDGES), 0, N_NODES, dtype=jnp.int64)
        W1 = jax.random.normal(ks[2], (NHID, NFEAT), dtype=jnp.float32) / np.sqrt(NFEAT)
        b1 = jax.random.normal(ks[3], (NHID,), dtype=jnp.float32) * 0.01
        gamma = jnp.ones((NHID,), dtype=jnp.float32)
        beta = jnp.zeros((NHID,), dtype=jnp.float32)
        W2 = jax.random.normal(ks[4], (NHID, NHID), dtype=jnp.float32) / np.sqrt(NHID)
        b2 = jax.random.normal(ks[5], (NHID,), dtype=jnp.float32) * 0.01
        return {'x': x, 'edge_index': edge_index, 'W1': W1, 'b1': b1, 'gamma': gamma, 'beta': beta, 'W2': W2, 'b2': b2}
    _L1_gnn_all = _L1_gnn_setup()
    _L1_gnn_in = {k: v for k, v in _L1_gnn_all.items() if k in ('W1', 'b1', 'gamma', 'beta', 'W2', 'b2')}
    del _L1_gnn_all
    return {'x': x, 'src': src, 'dst': dst, 'edge_attr_128': edge_attr_128, 'L0_gnn_W_src': _L0_gnn_in['W_src'], 'L0_gnn_b_src': _L0_gnn_in['b_src'], 'L0_gnn_W_dst': _L0_gnn_in['W_dst'], 'L0_gnn_b_dst': _L0_gnn_in['b_dst'], 'L0_gnn_W_edge': _L0_gnn_in['W_edge'], 'L0_gnn_attn': _L0_gnn_in['attn'], 'L1_gnn_W1': _L1_gnn_in['W1'], 'L1_gnn_b1': _L1_gnn_in['b1'], 'L1_gnn_gamma': _L1_gnn_in['gamma'], 'L1_gnn_beta': _L1_gnn_in['beta'], 'L1_gnn_W2': _L1_gnn_in['W2'], 'L1_gnn_b2': _L1_gnn_in['b2']}

def reference(x, src, dst, edge_attr_128, L0_gnn_W_src, L0_gnn_b_src, L0_gnn_W_dst, L0_gnn_b_dst, L0_gnn_W_edge, L0_gnn_attn, L1_gnn_W1, L1_gnn_b1, L1_gnn_gamma, L1_gnn_beta, L1_gnn_W2, L1_gnn_b2):
    import jax
    import jax.numpy as jnp

    def _L0_gnn_ref(x, efeat, src, dst, W_src, b_src, W_dst, b_dst, W_edge, attn):
        import jax, jax.numpy as jnp
        import numpy as np
        N_NODES = 50000
        N_EDGES = 25000
        IN_FEAT = 128
        HEADS = 8
        HEAD_DIM = 16
        NEG_SLOPE = 0.2
        H, D = (HEADS, HEAD_DIM)
        feat_src = (x @ W_src.T + b_src).reshape(-1, H, D)
        feat_dst = (x @ W_dst.T + b_dst).reshape(-1, H, D)
        feat_edge = (efeat @ W_edge.T).reshape(-1, H, D)
        fs = feat_src[src]
        tmp = fs + feat_dst[dst] + feat_edge
        e = jnp.where(tmp >= 0, tmp, NEG_SLOPE * tmp)
        score = jnp.einsum('ehd,hd->eh', e, attn)
        m = jax.ops.segment_max(score, dst, num_segments=N_NODES)
        ex = jnp.exp(score - jax.lax.stop_gradient(m)[dst])
        z = jax.ops.segment_sum(ex, dst, num_segments=N_NODES)
        a = ex / z[dst]
        msg = (fs + feat_edge) * a[:, :, None]
        h = jax.ops.segment_sum(msg, dst, num_segments=N_NODES)
        h = jax.nn.relu(h)
        return h.reshape(N_NODES, H * D)

    def _L1_gnn_ref(x, edge_index, W1, b1, gamma, beta, W2, b2):
        import jax, jax.numpy as jnp
        import numpy as np
        N_NODES = 50000
        N_EDGES = 25000
        NFEAT = 128
        NHID = 128
        BN_EPS = 1e-05
        src, dst = (edge_index[0], edge_index[1])
        agg = x + jax.ops.segment_sum(x[src], dst, num_segments=N_NODES)
        h = jnp.maximum(agg @ W1.T + b1, 0.0)
        mean = jnp.mean(h, axis=0)
        var = jnp.var(h, axis=0)
        h = (h - mean) * jax.lax.rsqrt(var + BN_EPS) * gamma + beta
        return h @ W2.T + b2
    edge_index = jnp.stack([src, dst])
    h = jnp.maximum(_layernorm(x, axis=-1), 0.0)
    x = x + _L0_gnn_ref(h, edge_attr_128, src, dst, L0_gnn_W_src, L0_gnn_b_src, L0_gnn_W_dst, L0_gnn_b_dst, L0_gnn_W_edge, L0_gnn_attn)
    h = jnp.maximum(_layernorm(x, axis=-1), 0.0)
    x = x + _L1_gnn_ref(h, edge_index, L1_gnn_W1, L1_gnn_b1, L1_gnn_gamma, L1_gnn_beta, L1_gnn_W2, L1_gnn_b2)
    return x

_drawn_inputs = setup_inputs


def setup_inputs(seed=0):
    import zlib

    import numpy as np

    out = dict(_drawn_inputs(seed))
    spreads = {'L0_gnn_b_src': (0.0, 0.1),
     'L0_gnn_b_dst': (0.0, 2.0),
     'L1_gnn_gamma': (1.0, 0.2),
     'L1_gnn_beta': (0.0, 0.1)}
    factors = {'L1_gnn_b1': 8.0, 'L1_gnn_b2': 7.398, 'L0_gnn_W_dst': 2.735}
    for name, (base, spread) in spreads.items():
        noise = np.random.default_rng([zlib.crc32(name.encode()), seed]).standard_normal(out[name].shape)
        drawn = base * np.exp(spread * noise) if base else spread * noise
        out[name] = jnp.asarray(drawn.astype(out[name].dtype))
    for name, factor in factors.items():
        out[name] = (out[name] * factor).astype(out[name].dtype)
    return out
```

```python
from contextlib import ExitStack

import numpy as np

import concourse.bass as bass
from concourse import mybir

F32 = mybir.dt.float32
BF16 = mybir.dt.bfloat16
I32 = mybir.dt.int32
ALU = mybir.AluOpType
ACT = mybir.ActivationFunctionType
AX = mybir.AxisListType

P = 128
N, E = 50000, 25000
HEADS, HEAD_DIM = 8, 16
SLOPE = 0.2
EPS = 1e-5
EQ, EG = 4, 512
NEG = -(-E // EG)
EPAD = NEG * EG
DQ, DG = 8, 1024
ND = -(-N // DG)
DTAIL = (N - (ND - 1) * DG) // DQ
ETAIL = E - (NEG - 1) * EG
STAGE_LAG = 10
SCATTER_LAG = 12
FAR = float(2 ** 127)
NOWHERE = 65536
RSQRT_SEED = float(0x5F3759DF)
assert (ND - 1) * DG + DTAIL * DQ == N and ETAIL % EQ == 0 and NEG == ND


class Allocator:

    def __init__(self, nc, ctx, tag):
        self.nc, self.ctx, self.tag = nc, ctx, tag

    def sb(self, name, shape, dt=F32):
        return self.ctx.enter_context(self.nc.sbuf_tensor(f"{self.tag}_{name}", shape, dt))

    def ps(self, name, shape=(P, 512), dt=F32):
        return self.ctx.enter_context(self.nc.psum_tensor(f"{self.tag}_{name}", list(shape), dt))

    def sem(self, name):
        return self.ctx.enter_context(self.nc.semaphore(f"{self.tag}_{name}"))


class Group:

    def __init__(self, t, k):
        self.t, self.k = t, k

    def __add__(self, n):
        return Group(self.t, self.k + n)

    def __sub__(self, n):
        return self + -n

    def times(self, a, b=0):
        return self.t * (4 * a) + (a * self.k + b)

    def use(self, a, b):
        m = a * self.k + b
        return m % 2, self.t * (2 * a) + m // 2

    @property
    def known(self):
        return isinstance(self.t, int)

    @property
    def g(self):
        return self.times(1)

    @property
    def half(self):
        return self.t * 2 + self.k // 2

    @property
    def quarter(self):
        return self.t + self.k // 4


def group(g):
    return Group(g // 4, g % 4)


def loop(eng, start, stop, body, by_hand=0):
    lo = -(-(start + by_hand) // 4) * 4
    hi = max(stop // 4 * 4, lo)
    for g in range(start, min(lo, stop)):
        body(group(g))
    if hi > lo:
        with eng.Fori(lo // 4, hi // 4) as t:
            for k in range(4):
                body(Group(t, k))
    for g in range(hi, stop):
        body(group(g))


def wait(eng, sem, value):
    if not isinstance(value, int):
        eng.wait_ge(sem, value)
        if eng.engine in (mybir.EngineType.SP, mybir.EngineType.Pool):
            eng.nop(nofuse=True)
    elif value > 0:
        eng.wait_ge(sem, value)


class Own:

    def __init__(self, engine, sem):
        self.engine, self.sem, self.base, self.k = engine, sem, 0, 0

    def start(self, base):
        self.base, self.k = base, 0

    def step(self, instruction):
        self.k += 1
        instruction.then_inc(self.sem, 1)
        self.engine.wait_ge(self.sem, self.base + self.k)


def rows(view, g):
    return view[bass.ds(g, 1)].rearrange("a p n -> (a p) n")


FLAT = "p q f -> p (q f)"




def constants(nc, t, w):
    with ExitStack() as ctx:
        a = Allocator(nc, ctx, "const")
        names = ("W_src", "W_dst", "W_edge", "W1", "W2")
        raw = [a.sb(f"raw_{n}", [P, P]) for n in names]
        heads = a.sb("heads", [P, P])
        bank = [a.ps(f"bank{i}", (P, P)) for i in range(len(names))]
        loaded, columns = a.sem("loaded"), a.sem("columns")
        pool_step, made, turned, copied, v_step = (a.sem(n) for n in ("pool_step", "made", "turned", "copied", "v_step"))
        block = ctx.enter_context(nc.Block())
        cols = (("b_src", t.b_src), ("b_dst", t.b_dst), ("attn", t.attn), ("b1", t.b1), ("gamma", t.gamma),
                ("beta", t.beta))

        @block.sync
        def _(sp):
            for n, r in zip(names, raw):
                sp.dma_start(r[:, :], w[n]).then_inc(loaded, 16)
            for n, c in cols:
                sp.dma_start(c[:, :], w[n]).then_inc(columns, 16)
            sp.dma_start(t.b2_row[:, :], w["b2"]).then_inc(columns, 16)

        @block.gpsimd
        def _(pool):
            nc.gpsimd.memset(t.ident[:, :], 0.0).then_inc(pool_step, 1)
            nc.gpsimd.memset(t.pick[:, :], 0.0).then_inc(pool_step, 1)
            nc.gpsimd.memset(heads[:, :], 1.0).then_inc(pool_step, 1)
            nc.gpsimd.memset(t.ones_row[:, :], 1.0).then_inc(pool_step, 1)
            nc.gpsimd.memset(t.ones_row_bf[:, :], 1.0).then_inc(pool_step, 1)
            pool.wait_ge(pool_step, 5)
            nc.gpsimd.affine_select(out=t.ident[:, :], in_=t.ident[:, :], compare_op=ALU.not_equal, fill=1.0,
                                    base=0, pattern=[[-1, P]], channel_multiplier=1).then_inc(made, 1)
            nc.gpsimd.affine_select(out=t.pick[:, :], in_=t.pick[:, :], compare_op=ALU.not_equal, fill=1.0,
                                    base=0, pattern=[[-HEAD_DIM, HEADS]], channel_multiplier=1).then_inc(made, 1)
            nc.gpsimd.affine_select(out=heads[:, :], in_=heads[:, :], compare_op=ALU.is_ge, fill=0.0, base=0,
                                    pattern=[[-HEAD_DIM, HEADS], [0, HEAD_DIM]],
                                    channel_multiplier=1).then_inc(made, 1)
            pool.wait_ge(made, 3)
            nc.gpsimd.affine_select(out=heads[:, :], in_=heads[:, :], compare_op=ALU.is_ge, fill=0.0,
                                    base=HEAD_DIM - 1, pattern=[[HEAD_DIM, HEADS], [0, HEAD_DIM]],
                                    channel_multiplier=-1).then_inc(made, 1)

        @block.tensor
        def _(pe):
            pe.wait_ge(made, 1)
            pe.wait_ge(loaded, 16 * len(names))
            for r, b in zip(raw, bank):
                nc.tensor.transpose(b[:, :], r[:, :], t.ident[:, :]).then_inc(turned, 1)

        @block.scalar
        def _(act):
            for i, o in enumerate((t.W_srcT, t.W_dstT, t.W_edgeT, t.W1T, t.W2T)):
                act.wait_ge(turned, i + 1)
                nc.scalar.copy(o[:, :], bank[i][:, :]).then_inc(copied, 1)

        @block.vector
        def _(dve):
            dve.wait_ge(columns, 16 * (len(cols) + 1))
            dve.wait_ge(made, 4)
            nc.vector.tensor_scalar(t.A_pos[:, :], heads[:, :], t.attn[:, 0:1], None, ALU.mult).then_inc(v_step, 1)
            dve.wait_ge(v_step, 1)
            nc.vector.tensor_scalar(t.A_neg[:, :], t.A_pos[:, :], -SLOPE, None, ALU.mult)
            nc.vector.tensor_tensor(t.b_sum[:, :], t.b_src[:, :], t.b_dst[:, :], ALU.add).then_inc(v_step, 1)
            dve.wait_ge(v_step, 2)
            nc.vector.tensor_scalar(t.b_sum_neg[:, :], t.b_sum[:, :], -1.0, None, ALU.mult)
            nc.vector.memset(t.sums[:, :], 0.0)




def edge_tables(nc, d, src, dst):
    w = 256
    r = EPAD // w
    full = E // w
    with ExitStack() as ctx:
        a = Allocator(nc, ctx, "tables")
        cur, nxt, prv, s, gd, si = (a.sb(n, [r, w], I32) for n in ("cur", "nxt", "prv", "src", "gdst", "sidx"))
        end, keep, start, last = a.sb("end", [r, w]), a.sb("keep", [r, w], BF16), a.sb("start", [r, w], BF16), \
            a.sb("last", [r, w], BF16)
        filled, loaded, step, done, stored = (a.sem(n) for n in ("filled", "loaded", "step", "done", "stored"))
        block = ctx.enter_context(nc.Block())

        @block.gpsimd
        def _(pool):
            nc.gpsimd.memset(cur[:, :], N).then_inc(filled, 1)
            nc.gpsimd.memset(nxt[:, :], N).then_inc(filled, 1)
            nc.gpsimd.memset(prv[:, :], -1).then_inc(filled, 1)
            nc.gpsimd.memset(s[:, :], 0).then_inc(filled, 1)

        @block.sync
        def _(sp):
            def load(tile, shift):
                values = src if tile is s else dst
                lead = 0
                if shift < 0:
                    sp.dma_start(tile[0:1, 1:w], values[0:w - 1].unsqueeze(0)).then_inc(loaded, 16)
                    lead = 1
                sp.dma_start(tile[lead:full, :],
                             values[lead * w + shift:full * w + shift].rearrange("(p e) -> p e", e=w)
                             ).then_inc(loaded, 16)
                rest = E - full * w - shift
                sp.dma_start(tile[full:full + 1, 0:rest], values[full * w + shift:E].unsqueeze(0)
                             ).then_inc(loaded, 16)

            sp.wait_ge(filled, 4)
            load(cur, 0)
            load(nxt, 1)
            load(prv, -1)
            load(s, 0)
            sp.wait_ge(done, 4)
            for tile, o in ((s, d.gather[0]), (gd, d.gather[1]), (si, d.scatter), (keep, d.keep), (start, d.start),
                            (last, d.last)):
                sp.dma_start(o.rearrange("(p e) -> p e", e=w), tile[:, :]).then_inc(stored, 16)
            sp.wait_ge(stored, 6 * 16)

        @block.vector
        def _(dve):
            dve.wait_ge(loaded, 9 * 16)
            nc.vector.tensor_tensor(end[:, :], cur[:, :], nxt[:, :], ALU.is_equal).then_inc(step, 1)
            nc.vector.tensor_tensor(keep[:, :], cur[:, :], prv[:, :], ALU.is_equal).then_inc(step, 1)
            nc.vector.tensor_scalar(gd[:, :], cur[:, :], float(N - 1), None, ALU.min).then_inc(done, 1)
            dve.wait_ge(step, 2)
            nc.vector.tensor_scalar(start[:, :], keep[:, :], -1.0, FAR, ALU.add, ALU.mult).then_inc(done, 1)
            nc.vector.tensor_scalar(last[:, :], end[:, :], -FAR, None, ALU.mult).then_inc(done, 1)
            nc.vector.tensor_scalar(end[:, :], end[:, :], float(NOWHERE), None, ALU.mult).then_inc(step, 1)
            dve.wait_ge(step, 3)
            nc.vector.tensor_tensor(si[:, :], end[:, :], cur[:, :], ALU.add).then_inc(done, 1)





class Tiny:

    def __init__(self, a, n):
        self.v, self.x, self.rstd, self.z, self.mean = (a.sb(f"tiny_{k}", [P, n]) for k in
                                                         ("v", "x", "rstd", "z", "mean"))


NORM_STEPS = 14


def norm_scale(nc, own, stats, lo, hi, tiny, r=P):
    def c(tile):
        return tile[0:r, lo:hi]

    def s(i):
        return stats[0:r, lo:hi, i:i + 1].rearrange("p a b -> p (a b)")

    v, x, y, z = c(tiny.v), c(tiny.x), c(tiny.rstd), c(tiny.z)
    nc.vector.tensor_tensor(x, s(1), s(4), ALU.subtract)
    nc.vector.tensor_tensor(z, s(1), s(4), ALU.add)
    own.step(nc.vector.tensor_tensor(v, s(2), s(5), ALU.add))
    nc.vector.scalar_tensor_tensor(x, x, 0.25, x, ALU.mult, ALU.mult)
    nc.vector.tensor_scalar(c(tiny.mean), z, 0.5, None, ALU.mult)
    own.step(nc.vector.tensor_scalar(v, v, 1.0 / P, EPS, ALU.mult, ALU.add))
    own.step(nc.vector.tensor_tensor(v, v, x, ALU.add))
    nc.vector.tensor_scalar(x, v, -0.5, None, ALU.mult)
    own.step(nc.vector.tensor_scalar(z.bitcast(I32), v.bitcast(I32), 1, None, ALU.logical_shift_right))
    own.step(nc.vector.tensor_scalar(y.bitcast(I32), z.bitcast(I32), -1.0, RSQRT_SEED, ALU.mult, ALU.add))
    for _ in range(3):
        own.step(nc.vector.tensor_tensor(z, y, y, ALU.mult))
        own.step(nc.vector.tensor_tensor(z, z, x, ALU.mult))
        own.step(nc.vector.scalar_tensor_tensor(y, z, 1.5, y, ALU.add, ALU.mult))




def attention(nc, t, d, x, edge_attr, out):
    with ExitStack() as ctx:
        a = Allocator(nc, ctx, "att")
        sb, ps, sem = a.sb, a.ps, a.sem

        def sems(name, n=2):
            return [sem(f"{name}{i}") for i in range(n)]

        idx = [sb(f"idx{i}", [P, 2, EQ], I32) for i in range(4)]
        sidx = [sb(f"sidx{i}", [P, EQ], I32) for i in range(2)]
        xs = [sb(f"xs{i}", [P, EQ, P]) for i in range(2)]
        xd = [sb(f"xd{i}", [P, EQ, P]) for i in range(4)]
        er = [sb(f"er{i}", [P, EQ, P]) for i in range(2)]
        xn = sb("xn", [P, 2 * EQ, P])
        xr = [sb(f"xr{i}", [P, DQ, P]) for i in range(2)]
        xrn = sb("xrn", [P, DQ, P])
        new = sb("new", [P, EG])
        staged = [sb(f"staged{i}", [P, EG]) for i in range(2)]
        stats, tiny = sb("stats", [P, 2 * EQ + DQ, 6]), Tiny(a, 2 * EQ + DQ)
        eT, hsT, hdT, hrT = sb("eT", [P, EG]), sb("hsT", [P, EG]), sb("hdT", [P, EG]), sb("hrT", [P, DG])
        pos, neg = sb("pos", [P, EG]), sb("neg", [P, EG])
        start = [sb(f"start{i}", [P, EG], BF16) for i in range(2)]
        last = [sb(f"last{i}", [1, EG], BF16) for i in range(2)]
        before, gap, rise, fall = (sb(n, [P, EG]) for n in ("before", "gap", "rise", "fall"))
        decay, weight, z, msg, h = (sb(n, [P, EG]) for n in ("decay", "weight", "z", "msg", "h"))
        carry, rz = sb("carry", [P, 1]), sb("rz", [P, EQ * HEADS])
        yd, junk = sb("yd", [P, EG]), sb("junk", [P, EG])
        y0 = [sb(f"y0{i}", [P, DG]) for i in range(2)]
        TP = [ps("TP0"), ps("TP1")]
        T, G, S, R, Y, ZT = (ps(n) for n in ("T", "G", "S", "R", "Y", "ZT"))

        s_idx, s_xd = sems("idx", 4), sems("xd", 4)
        s_xs, s_er, s_start, s_last, s_xr = sems("xs"), sems("er"), sems("start"), sems("last"), sems("xr")
        s_staged, s_sidx, s_scattered, s_y0_stored = sems("staged"), sems("sidx"), sems("scattered"), sems("y0_stored")
        copied = sem("x_copied")
        src_normed, dst_normed, node_normed = sem("src_normed"), sem("dst_normed"), sem("node_normed")
        tp_full, tp_free = sems("tp_full"), sems("tp_free")
        logits, signs, scores, before_done, gaps, exps = (sem(n) for n in ("logits", "signs", "scores", "before_done",
                                                                           "gaps", "exps"))
        g_full, msg_done, h_done, back, x1_done = (sem(n) for n in ("g_full", "msg_done", "h_done", "back", "x1_done"))
        y_full, y_free, y0_done = sem("y_full"), sem("y_free"), sem("y0_done")
        v_step, a_step = sem("v_step"), sem("a_step")

        gather_v = d.gather.rearrange("t (g p q) -> g p t q", p=P, q=EQ)
        scatter_v = d.scatter.rearrange("(g p q) -> g p q", p=P, q=EQ)
        e_full = edge_attr[0:(NEG - 1) * EG, :].rearrange("(g p q) f -> g p (q f)", p=P, q=EQ)
        e_tail = edge_attr[(NEG - 1) * EG:E, :].rearrange("(p q) f -> p (q f)", q=EQ)
        x_full = x[0:(ND - 1) * DG, :].rearrange("(g p q) f -> g p (q f)", p=P, q=DQ)
        x_tail = x[(ND - 1) * DG:N, :].rearrange("(p q) f -> p (q f)", q=DQ)

        FIRST_TP = [(0, 0), (1, 0), (0, 1)]
        TAIL = group(NEG - 1)

        def edge_tp(i):
            return [i.use(5, 3 + j) for j in range(3)]

        def node_tp(i):
            return [i.use(5, 6 + j - 3 * (i is TAIL)) for j in range(2)]

        block = ctx.enter_context(nc.Block())

        @block.sync
        def _(sp):
            def load_idx(g):
                k = g.k % 4
                sp.dma_start(idx[k][:, :, :], gather_v[bass.ds(g.g, 1)].rearrange("a p t q -> (a p) t q")
                             ).then_inc(s_idx[k], 16)

            def load_edges(g):
                k = g.k % 2
                if g.known and g.g == NEG - 1:
                    sp.dma_start(er[k][0:ETAIL // EQ].rearrange(FLAT), e_tail).then_inc(s_er[k], 16)
                else:
                    sp.dma_start(er[k][:, :, :].rearrange(FLAT), rows(e_full, g.g)).then_inc(s_er[k], 16)
                sp.dma_start(start[k][:, :], d.start[bass.ds(g.times(EG), EG)].partition_broadcast(P)
                             ).then_inc(s_start[k], 16)
                sp.dma_start(last[k][:, :], d.last[bass.ds(g.times(EG), EG)].unsqueeze(0)).then_inc(s_last[k], 16)

            def load_nodes(g):
                k = g.k % 2
                if g.known and g.g == ND - 1:
                    sp.dma_start(xr[k][0:DTAIL].rearrange(FLAT), x_tail).then_inc(s_xr[k], 16)
                else:
                    sp.dma_start(xr[k][:, :, :].rearrange(FLAT), rows(x_full, g.g)).then_inc(s_xr[k], 16)

            def stage(g):
                k = g.k % 2
                wait(sp, s_scattered[k], g.half * 64)
                wait(sp, x1_done, g.g + 1)
                sp.dma_start(staged[k][:, :], t.x1[:, bass.ds(g.times(EG), EG)]).then_inc(s_staged[k], 16)
                sp.dma_start(sidx[k][:, :], rows(scatter_v, g.g)).then_inc(s_sidx[k], 16)

            def body(i, lag=True):
                known = i.known
                if not known or i.g + 4 < NEG:
                    wait(sp, s_xs[i.k % 2], i.half * 64 + 64)
                    wait(sp, s_xd[i.k % 4], i.quarter * 64 + 64)
                    load_idx(i + 4)
                if not known or i.g + 2 < NEG:
                    j = group(i.g + 2) if known else i + 2
                    wait(sp, before_done, i.g + 1)
                    wait(sp, y_full, i.times(3, 1))
                    load_edges(j)
                    wait(sp, node_normed, i.g + 1)
                    load_nodes(j)
                w = DG if not known or i.g < ND - 1 else DTAIL * DQ
                wait(sp, y0_done, i.g + 1)
                sp.dma_start(d.y0[:, bass.ds(i.times(DG), w)], y0[i.k % 2][:, 0:w]).then_inc(s_y0_stored[i.k % 2], 16)
                if lag:
                    stage(i - STAGE_LAG)

            for g in range(4):
                load_idx(group(g))
            for g in range(2):
                load_edges(group(g))
                load_nodes(group(g))
            loop(sp, 0, STAGE_LAG, lambda i: body(i, lag=False))
            loop(sp, STAGE_LAG, NEG - 5, body, by_hand=2)
            for g in range(NEG - 5, NEG):
                body(group(g))
            for g in range(NEG - STAGE_LAG, NEG):
                stage(group(g))
            for i in range(2):
                wait(sp, s_y0_stored[i], 16 + 16 * len(range(i, ND, 2)))

        @block.gpsimd
        def _(pool):
            def gather(j):
                k2, k4 = j.k % 2, j.k % 4
                wait(pool, s_idx[k4], j.quarter * 16 + 16)
                wait(pool, src_normed, j.g - 1)
                for q in range(EQ):
                    pool.indirect_dma_start(
                        out=xs[k2][:, q, :], out_offset=None, in_=x[:, :],
                        in_offset=bass.IndirectOffsetOnAxis(ap=idx[k4][:, 0, q:q + 1], axis=0)
                    ).then_inc(s_xs[k2], 16)
                wait(pool, x1_done, j.g - 3)
                for q in range(EQ):
                    pool.indirect_dma_start(
                        out=xd[k4][:, q, :], out_offset=None, in_=x[:, :],
                        in_offset=bass.IndirectOffsetOnAxis(ap=idx[k4][:, 1, q:q + 1], axis=0)
                    ).then_inc(s_xd[k4], 16)

            def scatter(g):
                k = g.k % 2
                wait(pool, s_staged[k], g.half * 16 + 16)
                wait(pool, s_sidx[k], g.half * 16 + 16)
                for q in range(EQ):
                    pool.indirect_dma_start(
                        out=out[:, :], out_offset=bass.IndirectOffsetOnAxis(ap=sidx[k][:, q:q + 1], axis=0),
                        in_=staged[k][:, q * P:(q + 1) * P], in_offset=None, bounds_check=N - 1, oob_is_err=False
                    ).then_inc(s_scattered[k], 16)

            def both(j):
                gather(j)
                scatter(j - SCATTER_LAG)

            loop(pool, 0, SCATTER_LAG, gather, by_hand=4)
            wait(pool, copied, 16 * 5)
            loop(pool, SCATTER_LAG, NEG, both)
            for g in range(NEG - SCATTER_LAG, NEG):
                scatter(group(g))
            for i in range(2):
                wait(pool, s_scattered[i], 64 * len(range(i, NEG, 2)))

        @block.vector
        def _(dve):
            own = Own(dve, v_step)
            nc.vector.memset(before[:, :], 0.0)
            nc.vector.memset(z[:, :], 0.0)
            nc.vector.memset(h[:, :], 0.0)
            own.step(nc.vector.memset(carry[:, :], 0.0))

            def edge_stats(g):
                dve.wait_ge(s_xs[g.k % 2], g.half * 64 + 64)
                for q in range(EQ):
                    nc.vector.bn_stats(stats[:, q, :], xs[g.k % 2][:, q, :])
                dve.wait_ge(s_xd[g.k % 4], g.quarter * 64 + 64)
                for q in range(EQ):
                    ins = nc.vector.bn_stats(stats[:, EQ + q, :], xd[g.k % 4][:, q, :])
                return ins

            def edge_norm(g):
                for m, tile, done in ((0, xs[g.k % 2], src_normed), (EQ, xd[g.k % 4], dst_normed)):
                    for q in range(EQ):
                        ins = nc.vector.tensor_scalar(xn[:, m + q, :], tile[:, q, :], tiny.mean[:, m + q:m + q + 1],
                                                      tiny.rstd[:, m + q:m + q + 1], ALU.subtract, ALU.mult)
                    ins.then_inc(done, 1)

            def node_stats(i, r=P):
                dve.wait_ge(s_xr[i.k % 2], i.half * 16 + 16)
                for q in range(DQ):
                    ins = nc.vector.bn_stats(stats[0:r, 2 * EQ + q, :], xr[i.k % 2][0:r, q, :])
                return ins

            def node_norm(i, r=P):
                b, n = i.use(5, 2)
                dve.wait_ge(tp_full[b], n + 1)
                for q in range(DQ):
                    m = 2 * EQ + q
                    ins = nc.vector.tensor_scalar(xrn[0:r, q, :], xr[i.k % 2][0:r, q, :], tiny.mean[0:r, m:m + 1],
                                                  tiny.rstd[0:r, m:m + 1], ALU.subtract, ALU.mult)
                ins.then_inc(node_normed, 1)

            def score_scan(g):
                k = g.k % 2
                dve.wait_ge(s_start[k], g.half * 16 + 16)
                own.step(nc.vector.tensor_tensor(before[:, 0:1], carry[:, :], start[k][:, 0:1], ALU.add))
                dve.wait_ge(scores, g.g + 1)
                nc.vector.tensor_tensor_scan(before[:, 1:EG], S[:, 0:EG - 1], start[k][:, 1:EG],
                                             before[:, 0:1], ALU.max, ALU.add).then_inc(before_done, 1)
                dve.wait_ge(before_done, g.g + 1)
                nc.vector.tensor_tensor(gap[:, :], S[:, :], before[:, :], ALU.subtract)
                own.step(nc.vector.tensor_tensor(carry[:, :], S[:, EG - 1:EG], before[:, EG - 1:EG], ALU.max))
                nc.vector.tensor_scalar(rise[:, :], gap[:, :], 0.0, None, ALU.max)
                nc.vector.tensor_scalar(fall[:, :], gap[:, :], 0.0, None, ALU.min).then_inc(gaps, 1)

            def sum_scan(g):
                dve.wait_ge(exps, g.g + 1)
                nc.vector.tensor_tensor_scan(z[:, :], decay[:, :], weight[:, :], z[:, EG - 1:EG], ALU.mult, ALU.add)
                dve.wait_ge(g_full, g.g + 1)
                nc.vector.scalar_tensor_tensor(msg[:, :], G[:, :], t.b_src[:, 0:1], weight[:, :],
                                               ALU.add, ALU.mult).then_inc(msg_done, 1)
                dve.wait_ge(msg_done, g.g + 1)
                nc.vector.tensor_tensor_scan(h[:, :], decay[:, :], msg[:, :], h[:, EG - 1:EG],
                                             ALU.mult, ALU.add).then_inc(h_done, 1)

            def new_rows(g):
                dve.wait_ge(back, g.g + 1)
                own.step(nc.vector.reciprocal(rz[:, :], ZT[:, 0:EQ * HEADS]))
                own.step(nc.vector.scalar_tensor_tensor(
                    new[:, :].rearrange("p (a c) -> p a c", c=HEAD_DIM),
                    R[:, :].rearrange("p (a c) -> p a c", c=HEAD_DIM), 0.0,
                    rz[:, :].unsqueeze(2).to_broadcast([P, EQ * HEADS, HEAD_DIM]), ALU.max, ALU.mult))
                nc.vector.tensor_tensor(t.x1[:, bass.ds(g.times(EG), EG)], new[:, :],
                                        xd[g.k % 4][:, :, :].rearrange(FLAT), ALU.add).then_inc(x1_done, 1)

            own.step(edge_stats(group(0)))
            norm_scale(nc, own, stats, 0, 2 * EQ, tiny)
            edge_norm(group(0))
            first, per = own.k, NORM_STEPS + 5

            def body(i):
                own.start(i.times(per, first))
                score_scan(i)
                edge_stats(i + 1)
                own.step(node_stats(i))
                norm_scale(nc, own, stats, 0, 2 * EQ + DQ, tiny)
                edge_norm(i + 1)
                sum_scan(i)
                node_norm(i)
                new_rows(i)
                assert own.k == per

            loop(dve, 0, NEG - 1, body)
            own.start(TAIL.times(per, first))
            score_scan(TAIL)
            own.step(node_stats(TAIL, DTAIL))
            norm_scale(nc, own, stats, 2 * EQ, 2 * EQ + DQ, tiny, DTAIL)
            sum_scan(TAIL)
            node_norm(TAIL, DTAIL)
            new_rows(TAIL)

        @block.tensor
        def _(pe):
            def turn(tile, first, use, r=P, strided=True):
                b, n = use
                wait(pe, tp_free[b], n)
                for q in range(EQ):
                    o = TP[b][:, q:EG:EQ] if strided else TP[b][:, q * r:(q + 1) * r]
                    ins = nc.tensor.transpose(o, tile[0:r, first + q, :], t.ident[0:r, 0:r])
                ins.then_inc(tp_full[b], 1)

            def front(g, uses):
                pe.wait_ge(s_er[g.k % 2], g.half * 16 + 16)
                turn(er[g.k % 2], 0, uses[0])
                pe.wait_ge(src_normed, g.g + 1)
                turn(xn, 0, uses[1])
                pe.wait_ge(dst_normed, g.g + 1)
                turn(xn, EQ, uses[2])
                for b, n in uses[1:]:
                    pe.wait_ge(tp_free[b], n + 1)
                nc.tensor.matmul(T[:, :], t.W_srcT[:, :], hsT[:, :], start=True, stop=False)
                nc.tensor.matmul(T[:, :], t.W_edgeT[:, :], eT[:, :], start=False, stop=False)
                nc.tensor.matmul(T[:, :], t.W_dstT[:, :], hdT[:, :], start=False, stop=True).then_inc(logits, 1)
                wait(pe, msg_done, g.g)
                nc.tensor.matmul(G[:, :], t.W_srcT[:, :], hsT[:, :], start=True, stop=False)
                nc.tensor.matmul(G[:, :], t.W_edgeT[:, :], eT[:, :], start=False, stop=True).then_inc(g_full, 1)
                pe.wait_ge(signs, g.g + 1)
                nc.tensor.matmul(S[:, :], t.A_pos[:, :], pos[:, :], start=True, stop=False)
                nc.tensor.matmul(S[:, :], t.A_neg[:, :], neg[:, :], start=False, stop=True).then_inc(scores, 1)

            def own_part(g):
                wait(pe, y_free, g.times(3))
                pe.wait_ge(s_last[g.k % 2], g.half * 16 + 16)
                nc.tensor.matmul(Y[:, :], t.W1T[:, :], hdT[:, :], start=True, stop=False)
                nc.tensor.matmul(Y[:, :], t.ones_row_bf[:, :], last[g.k % 2][:, :], start=False,
                                 stop=True).then_inc(y_full, 1)

            def back_rows(g):
                pe.wait_ge(h_done, g.g + 1)
                for q in range(EQ):
                    nc.tensor.transpose(R[:, q * P:(q + 1) * P], h[:, q:EG:EQ], t.ident[:, :])
                for q in range(EQ):
                    ins = nc.tensor.matmul(ZT[:, q * HEADS:(q + 1) * HEADS], z[:, q:EG:EQ], t.pick[:, :],
                                           start=True, stop=True)
                ins.then_inc(back, 1)

            def nodes(i, r=P):
                pe.wait_ge(node_normed, i.g + 1)
                for m, use in enumerate(node_tp(i)):
                    turn(xrn, m * EQ, use, r=r, strided=False)
                for m, (b, n) in enumerate(node_tp(i)):
                    pe.wait_ge(tp_free[b], n + 1)
                    pe.wait_ge(y_free, i.times(3, 1 + m))
                    nc.tensor.matmul(Y[:, 0:EQ * r], t.W1T[:, :], hrT[:, m * EQ * r:(m + 1) * EQ * r],
                                     start=True, stop=True).then_inc(y_full, 1)

            front(group(0), FIRST_TP)
            own_part(group(0))

            def body(i):
                front(i + 1, edge_tp(i))
                back_rows(i)
                nodes(i)
                own_part(i + 1)

            loop(pe, 0, NEG - 1, body)
            back_rows(TAIL)
            nodes(TAIL, DTAIL)

        @block.scalar
        def _(act):
            own = Own(act, a_step)
            for c in range(5):
                n = N // 5
                act.dma_start(out[c * n:(c + 1) * n, :].rearrange("(a b) f -> a (b f)", b=25),
                              x[c * n:(c + 1) * n, :].rearrange("(a b) f -> a (b f)", b=25)).then_inc(copied, 16)
            for i in range(2):
                act.sem_inc(s_y0_stored[i], 16)

            def evacuate(o, func, use, w=EG):
                b, n = use
                act.wait_ge(tp_full[b], n + 1)
                nc.scalar.activation(o, TP[b][:, 0:w], func).then_inc(tp_free[b], 1)

            def front(g, uses):
                for o, func, use in ((eT, ACT.Copy, uses[0]), (hsT, ACT.Relu, uses[1]), (hdT, ACT.Relu, uses[2])):
                    evacuate(o[:, :], func, use)
                act.wait_ge(logits, g.g + 1)
                nc.scalar.activation(pos[:, :], T[:, :], ACT.Relu, bias=t.b_sum[:, 0:1])
                nc.scalar.activation(neg[:, :], T[:, :], ACT.Relu, bias=t.b_sum_neg[:, 0:1],
                                     scale=-1.0).then_inc(signs, 1)

            def softmax(g):
                act.wait_ge(gaps, g.g + 1)
                nc.scalar.activation(decay[:, :], rise[:, :], ACT.Exp, scale=-1.0)
                nc.scalar.activation(weight[:, :], fall[:, :], ACT.Exp).then_inc(exps, 1)

            def own_sums(g):
                act.wait_ge(y_full, g.times(3, 1))
                nc.scalar.activation(yd[:, :], Y[:, :], ACT.Relu, bias=t.b1[:, 0:1],
                                     accum_out=t.col("edge_old", g.g)).then_inc(y_free, 1)
                act.wait_ge(y_free, g.times(3, 1))
                own.step(nc.scalar.activation(junk[:, :], yd[:, :], ACT.Square, accum_out=t.col("edge_old_sq", g.g)))

            def nodes(i, r=P):
                k, w = i.k % 2, EQ * r
                for m, use in enumerate(node_tp(i)):
                    evacuate(hrT[:, m * w:(m + 1) * w], ACT.Relu, use, w)
                act.wait_ge(s_y0_stored[k], i.half * 16 + 16)
                for m in range(2):
                    act.wait_ge(y_full, i.times(3, 2 + m))
                    nc.scalar.activation(y0[k][:, m * w:(m + 1) * w], Y[:, 0:w], ACT.Relu, bias=t.b1[:, 0:1],
                                         accum_out=t.col("node", i.times(2, m))).then_inc(y_free, 1)
                act.wait_ge(y_free, i.times(3, 3))
                own.step(nc.scalar.activation(junk[:, 0:w], y0[k][:, 0:w], ACT.Square,
                                              accum_out=t.col("node_sq", i.times(2))))
                nc.scalar.activation(junk[:, 0:w], y0[k][:, w:2 * w], ACT.Square,
                                     accum_out=t.col("node_sq", i.times(2, 1))).then_inc(y0_done, 1)
                act.wait_ge(y0_done, i.g + 1)

            front(group(0), FIRST_TP)
            own_sums(group(0))

            def body(i):
                own.start(i.times(2, 1))
                softmax(i)
                front(i + 1, edge_tp(i))
                nodes(i)
                own_sums(i + 1)

            loop(act, 0, NEG - 1, body)
            own.start(TAIL.times(2, 1))
            softmax(TAIL)
            nodes(TAIL, DTAIL)




def aggregation(nc, t, d, out):
    with ExitStack() as ctx:
        a = Allocator(nc, ctx, "agg")
        sb, ps, sem = a.sb, a.ps, a.sem

        def sems(name, n=2):
            return [sem(f"{name}{i}") for i in range(n)]

        def two(name, shape, dt=F32):
            return [sb(f"{name}{i}", shape, dt) for i in range(2)]

        idx = [sb(f"idx{i}", [P, EQ], I32) for i in range(4)]
        xs = [sb(f"xs{i}", [P, EQ, P]) for i in range(4)]
        xn, hsT, hdT, agg, y = (two("xn", [P, 2 * EQ, P]), two("hsT", [P, EG]), two("hdT", [P, EG]),
                                two("agg", [P, EG]), two("y", [P, EG]))
        keep, last, junk = two("keep", [P, EG], BF16), two("last", [1, EG], BF16), sb("junk", [P, EG])
        stats, tiny = sb("stats", [P, 2 * EQ, 6]), Tiny(a, 2 * EQ)
        TS, TD, Y = [ps("TS0"), ps("TS1")], [ps("TD0"), ps("TD1")], [ps("Y0"), ps("Y1")]
        s_idx, s_xs, s_keep, s_last, s_stored = sems("idx", 4), sems("xs", 4), sems("keep"), sems("last"), sems("stored")
        normed, turned, hs_done, hd_done, agg_done, y_full, y_done, squared, v_step = (
            sem(n) for n in ("normed", "turned", "hs_done", "hd_done", "agg_done", "y_full", "y_done", "squared",
                             "v_step"))
        gather_v = d.gather[0].rearrange("(g p q) -> g p q", p=P, q=EQ)
        block = ctx.enter_context(nc.Block())

        @block.sync
        def _(sp):
            def load_idx(g):
                sp.dma_start(idx[g.k % 4][:, :], rows(gather_v, g.g)).then_inc(s_idx[g.k % 4], 16)

            def load_masks(g):
                k = g.k % 2
                sp.dma_start(keep[k][:, :], d.keep[bass.ds(g.times(EG), EG)].partition_broadcast(P)
                             ).then_inc(s_keep[k], 16)
                sp.dma_start(last[k][:, :], d.last[bass.ds(g.times(EG), EG)].unsqueeze(0)).then_inc(s_last[k], 16)

            def body(i):
                known = i.known
                if not known or i.g + 4 < NEG:
                    wait(sp, s_xs[i.k % 4], i.quarter * 64 + 64)
                    load_idx(i + 4)
                wait(sp, y_done, i.g + 1)
                if not known or i.g + 2 < NEG:
                    load_masks(i + 2)
                sp.dma_start(d.y1[:, bass.ds(i.times(EG), EG)], y[i.k % 2][:, :]).then_inc(s_stored[i.k % 2], 16)

            for g in range(4):
                load_idx(group(g))
            for g in range(2):
                load_masks(group(g))
            loop(sp, 0, NEG - 5, body)
            for g in range(NEG - 5, NEG):
                body(group(g))
            for i in range(2):
                wait(sp, s_stored[i], 16 + 16 * len(range(i, NEG, 2)))

        @block.gpsimd
        def _(pool):
            def gather(j):
                k = j.k % 4
                wait(pool, s_idx[k], j.quarter * 16 + 16)
                wait(pool, normed, j.g - 3)
                for q in range(EQ):
                    pool.indirect_dma_start(
                        out=xs[k][:, q, :], out_offset=None, in_=out[:, :],
                        in_offset=bass.IndirectOffsetOnAxis(ap=idx[k][:, q:q + 1], axis=0)).then_inc(s_xs[k], 16)

            loop(pool, 0, NEG, gather, by_hand=4)

        @block.vector
        def _(dve):
            own = Own(dve, v_step)

            def front(g):
                for q in range(EQ):
                    nc.vector.bn_stats(stats[:, EQ + q, :], t.x1[:, bass.ds(g.times(EG, q * P), P)])
                dve.wait_ge(s_xs[g.k % 4], g.quarter * 64 + 64)
                for q in range(EQ):
                    ins = nc.vector.bn_stats(stats[:, q, :], xs[g.k % 4][:, q, :])
                own.step(ins)
                norm_scale(nc, own, stats, 0, 2 * EQ, tiny)
                for q in range(2 * EQ):
                    v = xs[g.k % 4][:, q, :] if q < EQ else t.x1[:, bass.ds(g.times(EG, (q - EQ) * P), P)]
                    ins = nc.vector.tensor_scalar(xn[g.k % 2][:, q, :], v, tiny.mean[:, q:q + 1],
                                                  tiny.rstd[:, q:q + 1], ALU.subtract, ALU.mult)
                ins.then_inc(normed, 1)

            per = NORM_STEPS + 1

            def scan(g):
                k = g.k % 2
                dve.wait_ge(s_keep[k], g.half * 16 + 16)
                dve.wait_ge(hs_done, g.g + 1)
                dve.wait_ge(hd_done, g.g + 1)
                wait(dve, agg_done, g.g)
                nc.vector.tensor_tensor_scan(agg[k][:, :], keep[k][:, :], hsT[k][:, :], agg[1 - k][:, EG - 1:EG],
                                             ALU.mult, ALU.add).then_inc(agg_done, 1)

            nc.vector.memset(agg[1][:, :], 0.0)
            front(group(0))

            def body(i):
                own.start(i.times(per, per))
                front(i + 1)
                scan(i)

            loop(dve, 0, NEG - 1, body)
            scan(group(NEG - 1))

        @block.tensor
        def _(pe):
            def turn(g):
                pe.wait_ge(normed, g.g + 1)
                for m, bank in ((0, TS), (EQ, TD)):
                    for q in range(EQ):
                        ins = nc.tensor.transpose(bank[g.k % 2][:, q:EG:EQ], xn[g.k % 2][:, m + q, :], t.ident[:, :])
                    ins.then_inc(turned, 1)

            def product(g):
                k = g.k % 2
                pe.wait_ge(s_last[k], g.half * 16 + 16)
                pe.wait_ge(hd_done, g.g + 1)
                nc.tensor.matmul(Y[k][:, :], t.W1T[:, :], hdT[k][:, :], start=True, stop=False)
                nc.tensor.matmul(Y[k][:, :], t.ones_row_bf[:, :], last[k][:, :], start=False, stop=False)
                pe.wait_ge(agg_done, g.g + 1)
                nc.tensor.matmul(Y[k][:, :], t.W1T[:, :], agg[k][:, :], start=False, stop=True).then_inc(y_full, 1)

            turn(group(0))

            def body(i):
                turn(i + 1)
                product(i)

            loop(pe, 0, NEG - 1, body)
            product(group(NEG - 1))

        @block.scalar
        def _(act):
            for i in range(2):
                act.sem_inc(s_stored[i], 16)

            def evacuate(g):
                k = g.k % 2
                act.wait_ge(turned, g.times(2, 1))
                nc.scalar.activation(hsT[k][:, :], TS[k][:, :], ACT.Relu).then_inc(hs_done, 1)
                act.wait_ge(turned, g.times(2, 2))
                nc.scalar.activation(hdT[k][:, :], TD[k][:, :], ACT.Relu).then_inc(hd_done, 1)

            def sums(g):
                k = g.k % 2
                act.wait_ge(s_stored[k], g.half * 16 + 16)
                act.wait_ge(y_full, g.g + 1)
                nc.scalar.activation(y[k][:, :], Y[k][:, :], ACT.Relu, bias=t.b1[:, 0:1],
                                     accum_out=t.col("edge_new", g.g)).then_inc(y_done, 1)
                act.wait_ge(y_done, g.g + 1)
                nc.scalar.activation(junk[:, :], y[k][:, :], ACT.Square,
                                     accum_out=t.col("edge_new_sq", g.g)).then_inc(squared, 1)
                act.wait_ge(squared, g.g + 1)

            evacuate(group(0))

            def body(i):
                evacuate(i + 1)
                sums(i)

            loop(act, 0, NEG - 1, body)
            sums(group(NEG - 1))




def batch_norm(nc, t):
    with ExitStack() as ctx:
        a = Allocator(nc, ctx, "bn")
        part, tot, c = a.sb("part", [P, 6]), a.sb("tot", [P, 2]), a.sb("c", [P, 8])
        ones, shift = a.sb("ones", [P, P]), a.sb("shift", [P, P])
        bank = a.ps("bank", (P, P))
        v_step, var_done, root, folded, product, done = (a.sem(n) for n in ("v_step", "var_done", "root", "folded",
                                                                            "product", "done"))
        block = ctx.enter_context(nc.Block())

        @block.vector
        def _(dve):
            own = Own(dve, v_step)
            for i, n in enumerate(("node", "edge_old", "edge_new", "node_sq", "edge_old_sq", "edge_new_sq")):
                o, w = t.cols[n]
                ins = nc.vector.reduce_sum(part[:, i:i + 1], t.sums[:, o:o + w], axis=AX.X)
            nc.vector.memset(ones[:, :], 1.0)
            own.step(nc.vector.memset(c[:, :], 0.0))
            for i in range(2):
                nc.vector.tensor_tensor(tot[:, i:i + 1], part[:, 3 * i + 2:3 * i + 3], part[:, 3 * i + 1:3 * i + 2],
                                        ALU.subtract)
            own.step(nc.vector.memset(c[:, :], 0.0))
            for i in range(2):
                ins = nc.vector.tensor_tensor(tot[:, i:i + 1], tot[:, i:i + 1], part[:, 3 * i:3 * i + 1], ALU.add)
            own.step(ins)
            mean, sq, var, rstd, s, sh = (c[:, i:i + 1] for i in range(6))
            own.step(nc.vector.tensor_scalar(c[:, 0:2], tot[:, 0:2], 1.0 / N, None, ALU.mult))
            own.step(nc.vector.tensor_tensor(var, mean, mean, ALU.mult))
            own.step(nc.vector.tensor_tensor(var, sq, var, ALU.subtract))
            nc.vector.tensor_scalar(var, var, 0.0, EPS, ALU.max, ALU.add).then_inc(var_done, 1)
            dve.wait_ge(root, 1)
            own.step(nc.vector.reciprocal(rstd, rstd))
            own.step(nc.vector.tensor_tensor(s, rstd, t.gamma[:, :], ALU.mult))
            nc.vector.tensor_scalar(t.W2s[:, :], t.W2T[:, :], s, None, ALU.mult)
            own.step(nc.vector.tensor_tensor(sh, mean, s, ALU.mult))
            own.step(nc.vector.tensor_tensor(sh, t.beta[:, :], sh, ALU.subtract))
            nc.vector.tensor_scalar(shift[:, :], ones[:, :], sh, None, ALU.mult).then_inc(folded, 1)
            dve.wait_ge(product, 1)
            nc.vector.tensor_copy(t.b_row[:, :], bank[:, :])

        @block.scalar
        def _(act):
            act.wait_ge(var_done, 1)
            nc.scalar.activation(c[:, 3:4], c[:, 2:3], ACT.Sqrt).then_inc(root, 1)

        @block.tensor
        def _(pe):
            pe.wait_ge(folded, 1)
            nc.tensor.matmul(bank[:, :], shift[:, :], t.W2T[:, :], start=True, stop=False)
            nc.tensor.matmul(bank[:, :], t.ones_row[:, :], t.b2_row[:, :], start=False, stop=True).then_inc(product, 1)




def result(nc, t, d, x, out):
    with ExitStack() as ctx:
        a = Allocator(nc, ctx, "out")
        sb, ps, sem = a.sb, a.ps, a.sem

        def sems(name, n=2):
            return [sem(f"{name}{i}") for i in range(n)]

        xr = [sb(f"xr{i}", [P, DQ * P]) for i in range(4)]
        y0 = [sb(f"y0{i}", [P, DG]) for i in range(4)]
        y1 = [sb(f"y1{i}", [P, EG]) for i in range(4)]
        staged = [sb(f"staged{i}", [P, EG]) for i in range(2)]
        sidx = [sb(f"sidx{i}", [P, EQ], I32) for i in range(2)]
        D, Z = [ps(f"D{i}") for i in range(4)], [ps(f"Z{i}") for i in range(2)]
        s_xr, s_y0, s_y1, s_out = sems("xr", 4), sems("y0", 4), sems("y1", 4), sems("stored", 4)
        s_staged, s_sidx, s_scattered = sems("staged"), sems("sidx"), sems("scattered")
        node_full, edge_full, node_done, edge_done, biased, nodes_written = (
            sem(n) for n in ("node_full", "edge_full", "node_done", "edge_done", "biased", "nodes_written"))
        scatter_v = d.scatter.rearrange("(g p q) -> g p q", p=P, q=EQ)
        x_full = x[0:(ND - 1) * DG, :].rearrange("(g p q) f -> g p (q f)", p=P, q=DQ)
        x_tail = x[(ND - 1) * DG:N, :].rearrange("(p q) f -> p (q f)", q=DQ)
        o_full = out[0:(ND - 1) * DG, :].rearrange("(g p q) f -> g p (q f)", p=P, q=DQ)
        o_tail = out[(ND - 1) * DG:N, :].rearrange("(p q) f -> p (q f)", q=DQ)
        TAIL = group(ND - 1)
        block = ctx.enter_context(nc.Block())

        @block.sync
        def _(sp):
            def load(g):
                k = g.k % 4
                if g.known and g.g == ND - 1:
                    w = DTAIL * DQ
                    sp.dma_start(xr[k][0:DTAIL, :], x_tail).then_inc(s_xr[k], 16)
                    sp.dma_start(y0[k][:, 0:w], d.y0[:, (ND - 1) * DG:N]).then_inc(s_y0[k], 16)
                else:
                    sp.dma_start(xr[k][:, :], rows(x_full, g.g)).then_inc(s_xr[k], 16)
                    sp.dma_start(y0[k][:, :], d.y0[:, bass.ds(g.times(DG), DG)]).then_inc(s_y0[k], 16)
                sp.dma_start(y1[k][:, :], d.y1[:, bass.ds(g.times(EG), EG)]).then_inc(s_y1[k], 16)

            def body(i):
                k = i.k % 4
                known = i.known
                wait(sp, node_done, i.g + 1)
                if known and i.g == ND - 1:
                    sp.dma_start(o_tail, xr[k][0:DTAIL, :]).then_inc(s_out[k], 16)
                else:
                    sp.dma_start(rows(o_full, i.g), xr[k][:, :]).then_inc(s_out[k], 16)
                if not known or i.g >= 1:
                    wait(sp, s_out[(i.k - 1) % 4], (i - 1).quarter * 16 + 16)
                    if not known or i.g + 3 < ND:
                        wait(sp, edge_done, i.g)
                        load(group(i.g + 3) if known else i + 3)

            for g in range(4):
                load(group(g))
            loop(sp, 0, ND - 5, body, by_hand=4)
            for g in range(ND - 5, ND):
                body(group(g))
            wait(sp, s_out[(ND - 1) % 4], TAIL.quarter * 16 + 16)
            sp.sem_inc(nodes_written, 1)

        @block.vector
        def _(dve):
            def nodes(i, r=P):
                k, w = i.k % 4, DQ * P // 2
                dve.wait_ge(s_xr[k], i.quarter * 16 + 16)
                v = xr[k][0:r, :].rearrange("p (q f) -> p q f", f=P)
                nc.vector.tensor_tensor(v, v, t.b_row[0:r, :].unsqueeze(1).to_broadcast([r, DQ, P]),
                                        ALU.add).then_inc(biased, 1)
                dve.wait_ge(biased, i.times(2, 1))
                for m in range(2):
                    dve.wait_ge(node_full, i.times(2, m + 1))
                    o = xr[k][0:r, m * w:(m + 1) * w]
                    ins = nc.vector.tensor_tensor(o, D[(2 * i.k + m) % 4][0:r, :], o, ALU.add)
                ins.then_inc(node_done, 1)

            def edges(i):
                o = t.x1[:, bass.ds(i.times(EG), EG)]
                v = o.rearrange("p (q f) -> p q f", f=P)
                nc.vector.tensor_tensor(v, v, t.b_row[:, :].unsqueeze(1).to_broadcast([P, EQ, P]),
                                        ALU.add).then_inc(biased, 1)
                dve.wait_ge(biased, i.times(2, 2))
                dve.wait_ge(edge_full, i.g + 1)
                nc.vector.tensor_tensor(o, Z[i.k % 2][:, :], o, ALU.add).then_inc(edge_done, 1)

            def body(i):
                nodes(i)
                edges(i)

            loop(dve, 0, ND - 1, body)
            nodes(TAIL, DTAIL)
            edges(TAIL)

        @block.tensor
        def _(pe):
            def body(i, r=P):
                k = i.k % 4
                pe.wait_ge(s_y0[k], i.quarter * 16 + 16)
                for m in range(2):
                    wait(pe, node_done, i.g - 1)
                    for q in range(EQ):
                        c = (m * EQ + q) * r
                        ins = nc.tensor.matmul(D[(2 * i.k + m) % 4][0:r, q * P:(q + 1) * P], y0[k][:, c:c + r],
                                               t.W2s[:, :], start=True, stop=True)
                    ins.then_inc(node_full, 1)
                pe.wait_ge(s_y1[k], i.quarter * 16 + 16)
                wait(pe, edge_done, i.g - 1)
                for q in range(EQ):
                    ins = nc.tensor.matmul(Z[i.k % 2][:, q * P:(q + 1) * P], y1[k][:, q:EG:EQ], t.W2s[:, :],
                                           start=True, stop=True)
                ins.then_inc(edge_full, 1)

            loop(pe, 0, ND - 1, body, by_hand=2)
            body(TAIL, DTAIL)

        @block.scalar
        def _(act):
            def stage(g):
                k = g.k % 2
                wait(act, s_scattered[k], g.half * 64)
                act.wait_ge(edge_done, g.g + 1)
                act.dma_start(staged[k][:, :], t.x1[:, bass.ds(g.times(EG), EG)]).then_inc(s_staged[k], 16)
                act.dma_start(sidx[k][:, :], rows(scatter_v, g.g)).then_inc(s_sidx[k], 16)

            loop(act, 0, NEG, stage, by_hand=2)

        @block.gpsimd
        def _(pool):
            wait(pool, nodes_written, 1)

            def scatter(g):
                k = g.k % 2
                wait(pool, s_staged[k], g.half * 16 + 16)
                wait(pool, s_sidx[k], g.half * 16 + 16)
                for q in range(EQ):
                    pool.indirect_dma_start(
                        out=out[:, :], out_offset=bass.IndirectOffsetOnAxis(ap=sidx[k][:, q:q + 1], axis=0),
                        in_=staged[k][:, q * P:(q + 1) * P], in_offset=None, bounds_check=N - 1, oob_is_err=False
                    ).then_inc(s_scattered[k], 16)

            loop(pool, 0, NEG, scatter)
            for i in range(2):
                wait(pool, s_scattered[i], 64 * len(range(i, NEG, 2)))




class Tiles:

    def __init__(self, a):
        self.x1 = a.sb("x1", [P, EPAD])
        (self.W_srcT, self.W_dstT, self.W_edgeT, self.W1T, self.W2T, self.W2s, self.A_pos, self.A_neg, self.ident,
         self.b_row) = (a.sb(n, [P, P]) for n in ("W_srcT", "W_dstT", "W_edgeT", "W1T", "W2T", "W2s", "A_pos", "A_neg",
                                                  "ident", "b_row"))
        self.pick = a.sb("pick", [P, HEADS])
        self.ones_row, self.ones_row_bf, self.b2_row = a.sb("ones_row", [1, P]), a.sb("ones_row_bf", [1, P], BF16), \
            a.sb("b2_row", [1, P])
        (self.b_src, self.b_dst, self.attn, self.b1, self.gamma, self.beta, self.b_sum, self.b_sum_neg) = (
            a.sb(n, [P, 1]) for n in ("b_src", "b_dst", "attn", "b1", "gamma", "beta", "b_sum", "b_sum_neg"))
        self.cols, o = {}, 0
        for n, w in (("node", 2 * ND), ("node_sq", 2 * ND), ("edge_old", NEG), ("edge_old_sq", NEG),
                     ("edge_new", NEG), ("edge_new_sq", NEG)):
            self.cols[n] = (o, w)
            o += w
        self.sums = a.sb("sums", [P, o])

    def col(self, name, i):
        return self.sums[:, bass.ds(self.cols[name][0] + i, 1)]


class Scratch:

    def __init__(self, nc):
        def dram(name, shape, dt=F32):
            return nc.dram_tensor(name, list(shape), dt, kind="Internal").ap()

        self.gather = dram("gather_rows", (2, EPAD), I32)
        self.scatter = dram("scatter_rows", (EPAD,), I32)
        self.keep, self.start, self.last = (dram(n, (EPAD,), BF16) for n in ("keep", "start", "last"))
        self.y0 = dram("y_nodes", (P, N))
        self.y1 = dram("y_edges", (P, EPAD))


def program(nc, x, src, dst, edge_attr, W_src, b_src, W_dst, b_dst, W_edge, attn, W1, b1, gamma, beta, W2, b2, out):
    d = Scratch(nc)

    def column(v):
        return v.rearrange("(f o) -> f o", o=1)

    w = {"W_src": W_src, "W_dst": W_dst, "W_edge": W_edge, "W1": W1, "W2": W2, "b_src": column(b_src),
         "b_dst": column(b_dst), "attn": attn.rearrange("h (f o) -> (h f) o", o=1), "b1": column(b1),
         "gamma": column(gamma), "beta": column(beta), "b2": b2.unsqueeze(0)}
    with ExitStack() as ctx:
        t = Tiles(Allocator(nc, ctx, "t"))
        constants(nc, t, w)
        edge_tables(nc, d, src, dst)
        attention(nc, t, d, x, edge_attr, out)
        aggregation(nc, t, d, out)
        batch_norm(nc, t)
        result(nc, t, d, x, out)


_INS = ['x', 'src', 'dst', 'edge_attr_128', 'L0_gnn_W_src', 'L0_gnn_b_src', 'L0_gnn_W_dst', 'L0_gnn_b_dst',
        'L0_gnn_W_edge', 'L0_gnn_attn', 'L1_gnn_W1', 'L1_gnn_b1', 'L1_gnn_gamma', 'L1_gnn_beta', 'L1_gnn_W2',
        'L1_gnn_b2']


def kernel(**inputs):
    import concourse.bacc as _bacc
    from concourse.bass_utils import run_bass_kernel_spmd as _run

    nc = _bacc.Bacc("TRN2", target_bir_lowering=False, num_devices=1)
    arrays, args = {}, []
    for name in _INS:
        v = np.ascontiguousarray(inputs[name])
        arrays[f"in_{name}"] = v
        args.append(nc.dram_tensor(f"in_{name}", v.shape, mybir.dt.from_np(v.dtype), kind="ExternalInput").ap())
    args.append(nc.dram_tensor("out_0", (N, P), F32, kind="ExternalOutput").ap())
    program(nc, *args)
    return _run(nc, [arrays], core_ids=[0]).results[0]["out_0"]
```

```python
from contextlib import ExitStack

import numpy as np

import concourse.bass as bass
from concourse import mybir

F32 = mybir.dt.float32
BF16 = mybir.dt.bfloat16
I32 = mybir.dt.int32
ALU = mybir.AluOpType
ACT = mybir.ActivationFunctionType
AX = mybir.AxisListType

P = 128
N, E = 50000, 25000
HEADS, HEAD_DIM = 8, 16
SLOPE = 0.2
EPS = 1e-5
EQ, EG = 4, 512
NEG = -(-E // EG)
EPAD = NEG * EG
DQ, DG = 8, 1024
ND = -(-N // DG)
DTAIL = (N - (ND - 1) * DG) // DQ
ETAIL = E - (NEG - 1) * EG
COPIES, COPY_ROWS = 10, 25
STAGE_LAG = COPIES + 2
SCATTER_LAG = STAGE_LAG + 6
CATCH_UP = 40
FAR = float(2 ** 127)
NOWHERE = 65536
RSQRT_SEED = float(0x5F3759DF)
assert (ND - 1) * DG + DTAIL * DQ == N and ETAIL % EQ == 0 and NEG == ND


class Allocator:

    def __init__(self, nc, ctx, tag):
        self.nc, self.ctx, self.tag = nc, ctx, tag

    def sb(self, name, shape, dt=F32):
        return self.ctx.enter_context(self.nc.sbuf_tensor(f"{self.tag}_{name}", shape, dt))

    def ps(self, name, shape=(P, 512), dt=F32):
        return self.ctx.enter_context(self.nc.psum_tensor(f"{self.tag}_{name}", list(shape), dt))

    def sem(self, name):
        return self.ctx.enter_context(self.nc.semaphore(f"{self.tag}_{name}"))


class Group:

    def __init__(self, t, k):
        self.t, self.k = t, k

    def __add__(self, n):
        return Group(self.t, self.k + n)

    def __sub__(self, n):
        return self + -n

    def times(self, a, b=0):
        return self.t * (4 * a) + (a * self.k + b)

    def use(self, a, b):
        m = a * self.k + b
        return m % 2, self.t * (2 * a) + m // 2

    @property
    def known(self):
        return isinstance(self.t, int)

    @property
    def g(self):
        return self.times(1)

    @property
    def half(self):
        return self.t * 2 + self.k // 2

    @property
    def quarter(self):
        return self.t + self.k // 4


def group(g):
    return Group(g // 4, g % 4)


def is_group(g):
    return not g.known or 0 <= g.g < NEG


def loop(eng, start, stop, body, by_hand=0):
    lo = -(-(start + by_hand) // 4) * 4
    hi = max(stop // 4 * 4, lo)
    for g in range(start, min(lo, stop)):
        body(group(g))
    if hi > lo:
        with eng.Fori(lo // 4, hi // 4) as t:
            for k in range(4):
                body(Group(t, k))
    for g in range(hi, stop):
        body(group(g))


def unrolled(eng, start, lo, hi, stop, body):
    for g in range(start, lo):
        body(group(g))
    with eng.Fori(lo // 4, hi // 4) as t:
        for k in range(4):
            body(Group(t, k))
    for g in range(hi, stop):
        body(group(g))


def wait(eng, sem, value):
    if not isinstance(value, int):
        eng.wait_ge(sem, value)
        if eng.engine in (mybir.EngineType.SP, mybir.EngineType.Pool):
            eng.nop(nofuse=True)
    elif value > 0:
        eng.wait_ge(sem, value)


class Own:

    def __init__(self, engine, sem):
        self.engine, self.sem, self.base, self.k = engine, sem, 0, 0

    def start(self, base):
        self.base, self.k = base, 0

    def step(self, instruction, meanwhile=iter(())):
        self.k += 1
        instruction.then_inc(self.sem, 1)
        next(meanwhile, None)
        self.engine.wait_ge(self.sem, self.base + self.k)


def rows(view, g):
    return view[bass.ds(g, 1)].rearrange("a p n -> (a p) n")


FLAT = "p q f -> p (q f)"




TW = 256
TR = EPAD // TW
TF = E // TW
assert TR <= P and EPAD % TW == 0 and TR == TF + 1


def constants(nc, t, w, d, src, dst):
    with ExitStack() as ctx:
        a = Allocator(nc, ctx, "const")
        names = ("W_src", "W_dst", "W_edge", "W1", "W2")
        raw = [a.sb(f"raw_{n}", [P, P]) for n in names]
        heads = a.sb("heads", [P, P])
        bank = [a.ps(f"bank{i}", (P, P)) for i in range(len(names))]
        cur, nxt = a.sb("cur", [TR, TW], I32), a.sb("nxt", [TR, TW], I32)
        falls, count, ones = a.sb("falls", [TR, TW]), a.sb("count", [TR, 1]), a.sb("ones", [TR, 1])
        total = a.ps("total", (P, P))
        loaded, columns, filled, ends, copies = (a.sem(n) for n in ("loaded", "columns", "filled", "ends", "copies"))
        f_step, counted, summed = a.sem("f_step"), a.sem("counted"), a.sem("summed")
        pool_step, made, turned, copied, v_step = (a.sem(n) for n in ("pool_step", "made", "turned", "copied", "v_step"))
        block = ctx.enter_context(nc.Block())
        cols = (("b_src", t.b_src), ("b_dst", t.b_dst), ("attn", t.attn), ("b1", t.b1), ("gamma", t.gamma),
                ("beta", t.beta))

        @block.sync
        def _(sp):
            sp.wait_ge(filled, 2)
            for shift, tile in enumerate((cur, nxt)):
                n = E - TF * TW - shift
                sp.dma_start(tile[0:TF, :], dst[shift:TF * TW + shift].rearrange("(p e) -> p e", e=TW)).then_inc(ends, 16)
                sp.dma_start(tile[TF:TR, 0:n], dst[TF * TW + shift:E].unsqueeze(0)).then_inc(ends, 16)
            sp.dma_start(d.src.rearrange("(a e) o -> a (e o)", a=1), src.unsqueeze(0)).then_inc(copies, 16)
            sp.dma_start(d.dst.rearrange("(a e) o -> a (e o)", a=1), dst.unsqueeze(0)).then_inc(copies, 16)
            for n, r in zip(names, raw):
                sp.dma_start(r[:, :], w[n]).then_inc(loaded, 16)
            for n, c in cols:
                sp.dma_start(c[:, :], w[n]).then_inc(columns, 16)
            sp.dma_start(t.b2_row[:, :], w["b2"]).then_inc(columns, 16)
            sp.wait_ge(copies, 2 * 16)

        @block.gpsimd
        def _(pool):
            nc.gpsimd.memset(cur[:, :], N).then_inc(filled, 1)
            nc.gpsimd.memset(nxt[:, :], N).then_inc(filled, 1)
            nc.gpsimd.memset(ones[:, :], 1.0)
            nc.gpsimd.memset(t.ident[:, :], 0.0).then_inc(pool_step, 1)
            nc.gpsimd.memset(t.pick[:, :], 0.0).then_inc(pool_step, 1)
            nc.gpsimd.memset(heads[:, :], 1.0).then_inc(pool_step, 1)
            nc.gpsimd.memset(t.ones_row[:, :], 1.0).then_inc(pool_step, 1)
            nc.gpsimd.memset(t.ones_row_bf[:, :], 1.0).then_inc(pool_step, 1)
            pool.wait_ge(pool_step, 5)
            nc.gpsimd.affine_select(out=t.ident[:, :], in_=t.ident[:, :], compare_op=ALU.not_equal, fill=1.0,
                                    base=0, pattern=[[-1, P]], channel_multiplier=1).then_inc(made, 1)
            nc.gpsimd.affine_select(out=t.pick[:, :], in_=t.pick[:, :], compare_op=ALU.not_equal, fill=1.0,
                                    base=0, pattern=[[-HEAD_DIM, HEADS]], channel_multiplier=1).then_inc(made, 1)
            nc.gpsimd.affine_select(out=heads[:, :], in_=heads[:, :], compare_op=ALU.is_ge, fill=0.0, base=0,
                                    pattern=[[-HEAD_DIM, HEADS], [0, HEAD_DIM]],
                                    channel_multiplier=1).then_inc(made, 1)
            pool.wait_ge(made, 3)
            nc.gpsimd.affine_select(out=heads[:, :], in_=heads[:, :], compare_op=ALU.is_ge, fill=0.0,
                                    base=HEAD_DIM - 1, pattern=[[HEAD_DIM, HEADS], [0, HEAD_DIM]],
                                    channel_multiplier=-1).then_inc(made, 1)

        @block.tensor
        def _(pe):
            pe.wait_ge(made, 1)
            pe.wait_ge(loaded, 16 * len(names))
            for r, b in zip(raw, bank):
                nc.tensor.transpose(b[:, :], r[:, :], t.ident[:, :]).then_inc(turned, 1)
            pe.wait_ge(counted, 1)
            nc.tensor.matmul(total[0:1, 0:1], count[:, :], ones[:, :], start=True, stop=True).then_inc(summed, 1)

        @block.scalar
        def _(act):
            for i, o in enumerate((t.W_srcT, t.W_dstT, t.W_edgeT, t.W1T, t.W2T)):
                act.wait_ge(turned, i + 1)
                nc.scalar.copy(o[:, :], bank[i][:, :]).then_inc(copied, 1)

        @block.vector
        def _(dve):
            dve.wait_ge(columns, 16 * (len(cols) + 1))
            dve.wait_ge(made, 4)
            nc.vector.tensor_scalar(t.A_pos[:, :], heads[:, :], t.attn[:, 0:1], None, ALU.mult).then_inc(v_step, 1)
            dve.wait_ge(v_step, 1)
            nc.vector.tensor_scalar(t.A_neg[:, :], t.A_pos[:, :], -SLOPE, None, ALU.mult)
            nc.vector.tensor_tensor(t.b_sum[:, :], t.b_src[:, :], t.b_dst[:, :], ALU.add).then_inc(v_step, 1)
            dve.wait_ge(v_step, 2)
            nc.vector.tensor_scalar(t.b_sum_neg[:, :], t.b_sum[:, :], -1.0, None, ALU.mult)
            nc.vector.memset(t.sums[:, :], 0.0)
            dve.wait_ge(ends, 4 * 16)
            nc.vector.tensor_tensor(falls[:, :], cur[:, :], nxt[:, :], ALU.is_gt).then_inc(f_step, 1)
            dve.wait_ge(f_step, 1)
            nc.vector.reduce_sum(count[:, :], falls[:, :], axis=AX.X).then_inc(counted, 1)
            dve.wait_ge(summed, 1)
            nc.vector.tensor_copy(t.unsorted[:, :], total[0:1, 0:1])




def sort_edges(nc, t, d, src, dst, edge_attr):
    parts = 4
    with ExitStack() as ctx:
        a = Allocator(nc, ctx, "sort")
        key_of = t.x1
        ahead, behind, own_block = a.sb("ahead", [P, P]), a.sb("behind", [P, P]), a.sb("own_block", [P, P])
        below, part, key, total = (a.sb("below", [P, EPAD // parts]), a.sb("part", [P, parts]), a.sb("key", [P, 1]),
                                   a.sb("total", [P, 1]))
        rank, src_rows, dst_rows, attr_rows = (a.sb("rank", [P, 1], I32), a.sb("src_rows", [P, 1], I32),
                                               a.sb("dst_rows", [P, 1], I32), a.sb("attr_rows", [P, P]))
        dst_loaded, made, v_step, rows_loaded, ranked, rank_free, scattered = (
            a.sem(n) for n in ("dst_loaded", "made", "v_step", "rows_loaded", "ranked", "rank_free", "scattered"))
        filled = a.sem("filled")
        block = ctx.enter_context(nc.Block())

        @block.sync
        def _(sp):
            unsorted = sp.value_load(t.unsorted[0:1, 0:1], min_val=0, max_val=E)
            with sp.If(unsorted != 0):
                sp.dma_start(key_of[:, 0:E].bitcast(I32), dst.partition_broadcast(P)).then_inc(dst_loaded, 16)

        @block.vector
        def _(dve):
            unsorted = dve.value_load(t.unsorted[0:1, 0:1], min_val=0, max_val=E)
            with dve.If(unsorted != 0):
                own = Own(dve, v_step)
                nc.vector.memset(key_of[:, E:EPAD], float(N))
                dve.wait_ge(dst_loaded, 16)
                own.step(nc.vector.tensor_copy(key_of[:, 0:E], key_of[:, 0:E].bitcast(I32)))
                dve.wait_ge(made, 2)
                with dve.Fori(0, EPAD // P) as tile:
                    own.start(tile * (5 + 2 * parts) + 1)
                    block_keys = key_of[:, bass.ds(tile * P, P)]
                    own.step(nc.vector.tensor_tensor(own_block[:, :], block_keys, t.ident[:, :], ALU.mult))
                    nc.vector.reduce_sum(key[:, :], own_block[:, :], axis=AX.X)
                    own.step(nc.vector.tensor_tensor(block_keys, block_keys, ahead[:, :], ALU.add))
                    for i in range(parts):
                        w = EPAD // parts
                        own.step(nc.vector.tensor_scalar(below[:, :], key_of[:, i * w:(i + 1) * w], key[:, 0:1], None,
                                                         ALU.is_lt))
                        own.step(nc.vector.reduce_sum(part[:, i:i + 1], below[:, :], axis=AX.X))
                    own.step(nc.vector.tensor_tensor(block_keys, block_keys, behind[:, :], ALU.add))
                    own.step(nc.vector.reduce_sum(total[:, :], part[:, :], axis=AX.X))
                    dve.wait_ge(rank_free, tile + 1)
                    own.step(nc.vector.tensor_copy(rank[:, :], total[:, :]))
                    nc.vector.sem_inc(ranked, 1)

        @block.gpsimd
        def _(pool):
            unsorted = pool.value_load(t.unsorted[0:1, 0:1], min_val=0, max_val=E)
            with pool.If(unsorted != 0):
                nc.gpsimd.memset(ahead[:, :], -0.5).then_inc(filled, 1)
                nc.gpsimd.memset(behind[:, :], -0.5).then_inc(filled, 1)
                pool.wait_ge(filled, 2)
                nc.gpsimd.affine_select(out=ahead[:, :], in_=ahead[:, :], compare_op=ALU.is_ge, fill=0.0, base=-1,
                                        pattern=[[-1, P]], channel_multiplier=1).then_inc(made, 1)
                nc.gpsimd.affine_select(out=behind[:, :], in_=behind[:, :], compare_op=ALU.is_ge, fill=0.0, base=0,
                                        pattern=[[1, P]], channel_multiplier=-1).then_inc(made, 1)
                pool.sem_inc(rank_free, 1)

                def scatter(tile, r=P):
                    pool.dma_start(src_rows[0:r, :], src[bass.ds(tile * P, r)].unsqueeze(1)).then_inc(rows_loaded, 16)
                    pool.dma_start(dst_rows[0:r, :], dst[bass.ds(tile * P, r)].unsqueeze(1)).then_inc(rows_loaded, 16)
                    pool.dma_start(attr_rows[0:r, :], edge_attr[bass.ds(tile * P, r), :]).then_inc(rows_loaded, 16)
                    wait(pool, rows_loaded, tile * 48 + 48)
                    wait(pool, ranked, tile + 1)
                    for o, rows_ in ((d.src, src_rows), (d.dst, dst_rows), (d.attr, attr_rows)):
                        pool.indirect_dma_start(
                            out=o[:, :], out_offset=bass.IndirectOffsetOnAxis(ap=rank[:, 0:1], axis=0),
                            in_=rows_[:, :], in_offset=None, bounds_check=E - 1, oob_is_err=False
                        ).then_inc(scattered, 16)
                    wait(pool, scattered, tile * 48 + 48)
                    pool.sem_inc(rank_free, 1)

                with pool.Fori(0, E // P) as tile:
                    scatter(tile)
                scatter(E // P, E % P)




def edge_tables(nc, d):
    w, r, full = TW, TR, TF
    src, dst = (v.rearrange("e o -> (e o)") for v in (d.src, d.dst))
    with ExitStack() as ctx:
        a = Allocator(nc, ctx, "tables")
        cur, nxt, prv, s, gd, si = (a.sb(n, [r, w], I32) for n in ("cur", "nxt", "prv", "src", "gdst", "sidx"))
        end, keep, start, last = a.sb("end", [r, w]), a.sb("keep", [r, w], BF16), a.sb("start", [r, w], BF16), \
            a.sb("last", [r, w], BF16)
        filled, loaded, step, done, stored = (a.sem(n) for n in ("filled", "loaded", "step", "done", "stored"))
        block = ctx.enter_context(nc.Block())

        @block.gpsimd
        def _(pool):
            nc.gpsimd.memset(cur[:, :], N).then_inc(filled, 1)
            nc.gpsimd.memset(nxt[:, :], N).then_inc(filled, 1)
            nc.gpsimd.memset(prv[:, :], -1).then_inc(filled, 1)
            nc.gpsimd.memset(s[:, :], 0).then_inc(filled, 1)

        @block.sync
        def _(sp):
            def load(tile, shift):
                values = src if tile is s else dst
                lead = 0
                if shift < 0:
                    sp.dma_start(tile[0:1, 1:w], values[0:w - 1].unsqueeze(0)).then_inc(loaded, 16)
                    lead = 1
                sp.dma_start(tile[lead:full, :],
                             values[lead * w + shift:full * w + shift].rearrange("(p e) -> p e", e=w)
                             ).then_inc(loaded, 16)
                rest = E - full * w - shift
                sp.dma_start(tile[full:full + 1, 0:rest], values[full * w + shift:E].unsqueeze(0)
                             ).then_inc(loaded, 16)

            sp.wait_ge(filled, 4)
            load(cur, 0)
            load(nxt, 1)
            load(prv, -1)
            load(s, 0)
            sp.wait_ge(done, 4)
            for tile, o in ((s, d.gather[0]), (gd, d.gather[1]), (si, d.scatter), (keep, d.keep), (start, d.start),
                            (last, d.last)):
                sp.dma_start(o.rearrange("(p e) -> p e", e=w), tile[:, :]).then_inc(stored, 16)
            sp.wait_ge(stored, 6 * 16)

        @block.vector
        def _(dve):
            dve.wait_ge(loaded, 9 * 16)
            nc.vector.tensor_tensor(end[:, :], cur[:, :], nxt[:, :], ALU.is_equal).then_inc(step, 1)
            nc.vector.tensor_tensor(keep[:, :], cur[:, :], prv[:, :], ALU.is_equal).then_inc(step, 1)
            nc.vector.tensor_scalar(gd[:, :], cur[:, :], float(N - 1), None, ALU.min).then_inc(done, 1)
            dve.wait_ge(step, 2)
            nc.vector.tensor_scalar(start[:, :], keep[:, :], -1.0, FAR, ALU.add, ALU.mult).then_inc(done, 1)
            nc.vector.tensor_scalar(last[:, :], end[:, :], -FAR, None, ALU.mult).then_inc(done, 1)
            nc.vector.tensor_scalar(end[:, :], end[:, :], float(NOWHERE), None, ALU.mult).then_inc(step, 1)
            dve.wait_ge(step, 3)
            nc.vector.tensor_tensor(si[:, :], end[:, :], cur[:, :], ALU.add).then_inc(done, 1)





class Tiny:

    def __init__(self, a, n, i=0):
        self.v, self.x, self.rstd, self.z, self.mean, self.shift = (
            a.sb(f"tiny_{k}{i}", [P, n]) for k in ("v", "x", "rstd", "z", "mean", "shift"))


NORM_STEPS = 14


def mean_var(nc, own, stats, lo, hi, tiny, meanwhile=iter(()), r=P):
    def c(tile):
        return tile[0:r, lo:hi]

    def s(i):
        return stats[0:r, lo:hi, i:i + 1].rearrange("p a b -> p (a b)")

    v, x, z = c(tiny.v), c(tiny.x), c(tiny.z)
    nc.vector.tensor_tensor(x, s(1), s(4), ALU.subtract)
    nc.vector.tensor_tensor(z, s(1), s(4), ALU.add)
    own.step(nc.vector.tensor_tensor(v, s(2), s(5), ALU.add), meanwhile)
    nc.vector.scalar_tensor_tensor(x, x, 0.25, x, ALU.mult, ALU.mult)
    nc.vector.tensor_scalar(c(tiny.mean), z, 0.5, None, ALU.mult)
    own.step(nc.vector.tensor_scalar(v, v, 1.0 / P, EPS, ALU.mult, ALU.add), meanwhile)
    return nc.vector.tensor_tensor(v, v, x, ALU.add)


def norm_scale(nc, own, stats, lo, hi, tiny, meanwhile=iter(()), r=P):
    v, x, y, z = (tile[0:r, lo:hi] for tile in (tiny.v, tiny.x, tiny.rstd, tiny.z))

    def step(instruction):
        own.step(instruction, meanwhile)

    step(mean_var(nc, own, stats, lo, hi, tiny, meanwhile, r))
    nc.vector.tensor_scalar(x, v, -0.5, None, ALU.mult)
    step(nc.vector.tensor_scalar(z.bitcast(I32), v.bitcast(I32), 1, None, ALU.logical_shift_right))
    step(nc.vector.tensor_scalar(y.bitcast(I32), z.bitcast(I32), -1.0, RSQRT_SEED, ALU.mult, ALU.add))
    for _ in range(3):
        step(nc.vector.tensor_tensor(z, y, y, ALU.mult))
        step(nc.vector.tensor_tensor(z, z, x, ALU.mult))
        step(nc.vector.scalar_tensor_tensor(y, z, 1.5, y, ALU.add, ALU.mult))




def attention(nc, t, d, x, edge_attr, out):
    with ExitStack() as ctx:
        a = Allocator(nc, ctx, "att")
        sb, ps, sem = a.sb, a.ps, a.sem

        def many(n, name, shape, dt=F32):
            return [sb(f"{name}{i}", shape, dt) for i in range(n)]

        def sems(name, n=2):
            return [sem(f"{name}{i}") for i in range(n)]

        idx, sidx = many(4, "idx", [P, 2, EQ], I32), many(2, "sidx", [P, EQ], I32)
        xs, xd, er = many(4, "xs", [P, EQ, P]), many(4, "xd", [P, EQ, P]), many(2, "er", [P, EQ, P])
        xn, xr, xrn = many(2, "xn", [P, 2 * EQ, P]), many(4, "xr", [P, DQ, P]), sb("xrn", [P, DQ, P])
        staged = many(2, "staged", [P, EG])
        stats, tiny = sb("stats", [P, 2 * EQ + DQ, 6]), [Tiny(a, 2 * EQ + DQ, i) for i in range(2)]
        eT, hsT, hdT, hrT = sb("eT", [P, EG]), sb("hsT", [P, EG]), sb("hdT", [P, EG]), sb("hrT", [P, DG])
        pos, neg = sb("pos", [P, EG]), sb("neg", [P, EG])
        start, last = many(2, "start", [P, EG], BF16), many(2, "last", [1, EG], BF16)
        before, gap, rise = (sb(n, [P, EG]) for n in ("before", "gap", "rise"))
        decay, weight, z, msg, h = (sb(n, [P, EG]) for n in ("decay", "weight", "z", "msg", "h"))
        carry, rz = sb("carry", [P, 1]), sb("rz", [P, EQ * HEADS])
        yd, y0 = sb("yd", [P, EG]), many(2, "y0", [P, DG])
        TP = [ps("TP0"), ps("TP1")]
        T, G, S, R, Y, ZT = (ps(n) for n in ("T", "G", "S", "R", "Y", "ZT"))

        s_idx, s_xs, s_xd, s_xr = sems("idx", 4), sems("xs", 4), sems("xd", 4), sems("xr", 4)
        s_er, s_start, s_last = sems("er"), sems("start"), sems("last")
        s_staged, s_sidx, s_scattered, s_y0_stored = sems("staged"), sems("sidx"), sems("scattered"), sems("y0_stored")
        copied, kept = sem("x_copied"), sem("kept")
        scaled, src_normed, dst_normed, node_normed = (sem(n) for n in ("scaled", "src_normed", "dst_normed",
                                                                        "node_normed"))
        tp_full, tp_free = sems("tp_full"), sems("tp_free")
        logits, signs, scores, before_done, gaps, exps = (sem(n) for n in ("logits", "signs", "scores", "before_done",
                                                                           "gaps", "exps"))
        g_full, msg_done, h_done, back, rz_done, new_done, x1_done = (
            sem(n) for n in ("g_full", "msg_done", "h_done", "back", "rz_done", "new_done", "x1_done"))
        y_full, y_free, y0_squared, yd_squared = sem("y_full"), sem("y_free"), sem("y0_squared"), sem("yd_squared")
        v_step = sem("v_step")

        gather_v = d.gather.rearrange("t (g p q) -> g p t q", p=P, q=EQ)
        scatter_v = d.scatter.rearrange("(g p q) -> g p q", p=P, q=EQ)
        x_full = x[0:(ND - 1) * DG, :].rearrange("(g p q) f -> g p (q f)", p=P, q=DQ)
        x_tail = x[(ND - 1) * DG:N, :].rearrange("(p q) f -> p (q f)", q=DQ)
        LAST = NEG - 1

        def height(g):
            return DTAIL if g.known and g.g == ND - 1 else P


        def edge_tp(g):
            if g.known and g.g == 0:
                return [(0, 0), (1, 0), (0, 1)]
            return [g.use(5, j - 2) for j in range(3)]

        def node_tp(g):
            return [g.use(5, 6 + j - 3 * (g.known and g.g == LAST)) for j in range(2)]

        block = ctx.enter_context(nc.Block())

        @block.sync
        def _(sp):
            def load_idx(g):
                k = g.k % 4
                sp.dma_start(idx[k][:, :, :], gather_v[bass.ds(g.g, 1)].rearrange("a p t q -> (a p) t q")
                             ).then_inc(s_idx[k], 16)

            def load_edges(g):
                k = g.k % 2
                for attr, chosen in ((edge_attr, unsorted == 0), (d.attr, unsorted != 0)):
                    with sp.If(chosen):
                        if g.known and g.g == LAST:
                            sp.dma_start(er[k][0:ETAIL // EQ].rearrange(FLAT),
                                         attr[LAST * EG:E, :].rearrange("(p q) f -> p (q f)", q=EQ)
                                         ).then_inc(s_er[k], 16)
                        else:
                            full = attr[0:LAST * EG, :].rearrange("(g p q) f -> g p (q f)", p=P, q=EQ)
                            sp.dma_start(er[k][:, :, :].rearrange(FLAT), rows(full, g.g)).then_inc(s_er[k], 16)
                sp.dma_start(start[k][:, :], d.start[bass.ds(g.times(EG), EG)].partition_broadcast(P)
                             ).then_inc(s_start[k], 16)
                sp.dma_start(last[k][:, :], d.last[bass.ds(g.times(EG), EG)].unsqueeze(0)).then_inc(s_last[k], 16)

            def load_nodes(g):
                k = g.k % 4
                if g.known and g.g == ND - 1:
                    sp.dma_start(xr[k][0:DTAIL].rearrange(FLAT), x_tail).then_inc(s_xr[k], 16)
                else:
                    sp.dma_start(xr[k][:, :, :].rearrange(FLAT), rows(x_full, g.g)).then_inc(s_xr[k], 16)

            def stage(g):
                k = g.k % 2
                wait(sp, s_scattered[k], g.half * 64)
                wait(sp, x1_done, g.g + 1)
                sp.dma_start(staged[k][:, :], t.x1[:, bass.ds(g.times(EG), EG)]).then_inc(s_staged[k], 16)
                sp.dma_start(sidx[k][:, :], rows(scatter_v, g.g)).then_inc(s_sidx[k], 16)

            def body(i):
                j = i + 3
                if is_group(i + 7):
                    wait(sp, s_xs[j.k % 4], j.quarter * 64 + 64)
                    wait(sp, s_xd[j.k % 4], j.quarter * 64 + 64)
                    load_idx(i + 7)
                if i.known and 0 <= i.g < COPIES:
                    n = N // COPIES
                    sp.dma_start(out[i.g * n:(i.g + 1) * n, :].rearrange("(a b) f -> a (b f)", b=COPY_ROWS),
                                 x[i.g * n:(i.g + 1) * n, :].rearrange("(a b) f -> a (b f)", b=COPY_ROWS)
                                 ).then_inc(copied, 16)
                if is_group(i + 2):
                    wait(sp, before_done, i.g + 1)
                    wait(sp, y_full, i.times(3, 1))
                    load_edges(group(i.g + 2) if i.known else i + 2)
                if is_group(i + 4):
                    wait(sp, node_normed, i.g + 1)
                    load_nodes(group(i.g + 4) if i.known else i + 4)
                k, w = i.k % 2, DQ * height(i)
                wait(sp, y_free, i.times(3, 3))
                sp.dma_start(d.y0[:, bass.ds(i.times(DG), w)], y0[k][:, 0:w]).then_inc(s_y0_stored[k], 16)
                if not i.known or STAGE_LAG <= i.g < CATCH_UP:
                    stage(i - STAGE_LAG)
                elif i.g >= CATCH_UP:
                    for n in range(2):
                        stage(group(2 * i.g - CATCH_UP - STAGE_LAG + n))

            unsorted = sp.value_load(t.unsorted[0:1, 0:1], min_val=0, max_val=E)
            for g in range(4):
                load_idx(group(g))
            for g in range(2):
                load_edges(group(g))
                load_nodes(group(g))
            for g in range(3):
                wait(sp, s_xs[g], 64)
                wait(sp, s_xd[g], 64)
                load_idx(group(g + 4))
                if g < 2:
                    load_nodes(group(g + 2))
            unrolled(sp, 0, 16, CATCH_UP, NEG, body)
            for g in range(2 * NEG - CATCH_UP - STAGE_LAG, NEG):
                stage(group(g))
            for i in range(2):
                wait(sp, s_y0_stored[i], 16 + 16 * len(range(i, ND, 2)))

        @block.gpsimd
        def _(pool):
            def gather(j):
                k = j.k % 4
                wait(pool, s_idx[k], j.quarter * 16 + 16)
                wait(pool, src_normed, j.g - 3)
                for q in range(EQ):
                    pool.indirect_dma_start(
                        out=xs[k][:, q, :], out_offset=None, in_=x[:, :],
                        in_offset=bass.IndirectOffsetOnAxis(ap=idx[k][:, 0, q:q + 1], axis=0)
                    ).then_inc(s_xs[k], 16)
                wait(pool, dst_normed, j.g - 3)
                wait(pool, kept, j.g - 3)
                for q in range(EQ):
                    pool.indirect_dma_start(
                        out=xd[k][:, q, :], out_offset=None, in_=x[:, :],
                        in_offset=bass.IndirectOffsetOnAxis(ap=idx[k][:, 1, q:q + 1], axis=0)
                    ).then_inc(s_xd[k], 16)

            def scatter(g):
                k = g.k % 2
                wait(pool, s_staged[k], g.half * 16 + 16)
                wait(pool, s_sidx[k], g.half * 16 + 16)
                for q in range(EQ):
                    pool.indirect_dma_start(
                        out=out[:, :], out_offset=bass.IndirectOffsetOnAxis(ap=sidx[k][:, q:q + 1], axis=0),
                        in_=staged[k][:, q * P:(q + 1) * P], in_offset=None, bounds_check=N - 1, oob_is_err=False
                    ).then_inc(s_scattered[k], 16)

            def both(j):
                gather(j)
                scatter(j - SCATTER_LAG)

            loop(pool, 0, SCATTER_LAG, gather, by_hand=4)
            wait(pool, copied, 16 * COPIES)
            loop(pool, SCATTER_LAG, NEG, both)
            for g in range(NEG - SCATTER_LAG, NEG):
                scatter(group(g))
            for i in range(2):
                wait(pool, s_scattered[i], 64 * len(range(i, NEG, 2)))

        @block.vector
        def _(dve):
            own = Own(dve, v_step)
            nc.vector.memset(before[:, :], 0.0)
            nc.vector.memset(z[:, :], 0.0)
            nc.vector.memset(h[:, :], 0.0)
            own.step(nc.vector.memset(carry[:, :], 0.0))

            def statistics(e, n):
                if is_group(e):
                    k = e.k % 4
                    for m, tile, s in ((0, xs[k], s_xs[k]), (EQ, xd[k], s_xd[k])):
                        dve.wait_ge(s, e.quarter * 64 + 64)
                        for q in range(EQ):
                            yield nc.vector.bn_stats(stats[:, m + q, :], tile[:, q, :])
                if is_group(n):
                    k, r = n.k % 4, height(n)
                    dve.wait_ge(s_xr[k], n.quarter * 16 + 16)
                    for q in range(DQ):
                        yield nc.vector.bn_stats(stats[0:r, 2 * EQ + q, :], xr[k][0:r, q, :])

            def edge_norm(g, tile, m, done):
                s = tiny[g.k % 2]
                for q in range(EQ):
                    ins = nc.vector.tensor_scalar(xn[g.k % 2][:, m + q, :], tile[:, q, :], s.mean[:, m + q:m + q + 1],
                                                  s.rstd[:, m + q:m + q + 1], ALU.subtract, ALU.mult)
                    if q == EQ - 1:
                        ins.then_inc(done, 1)
                    yield

            def score_scan(g, tiles):
                k = g.k % 2
                dve.wait_ge(s_start[k], g.half * 16 + 16)
                own.step(nc.vector.tensor_tensor(before[:, 0:1], carry[:, :], start[k][:, 0:1], ALU.add), tiles)
                dve.wait_ge(scores, g.g + 1)
                nc.vector.tensor_tensor_scan(before[:, 1:EG], S[:, 0:EG - 1], start[k][:, 1:EG],
                                             before[:, 0:1], ALU.max, ALU.add).then_inc(before_done, 1)
                next(tiles, None)
                dve.wait_ge(before_done, g.g + 1)
                nc.vector.tensor_tensor(gap[:, :], S[:, :], before[:, :], ALU.subtract)
                own.step(nc.vector.tensor_tensor(carry[:, :], S[:, EG - 1:EG], before[:, EG - 1:EG], ALU.max), tiles)
                nc.vector.tensor_scalar(rise[:, :], gap[:, :], 0.0, None, ALU.max)
                nc.vector.tensor_scalar(gap[:, :], gap[:, :], 0.0, None, ALU.min).then_inc(gaps, 1)

            def new_rows(g):
                dve.wait_ge(back, g.g + 1)
                nc.vector.reciprocal(rz[:, :], ZT[:, 0:EQ * HEADS]).then_inc(rz_done, 1)
                yield
                dve.wait_ge(rz_done, g.g + 1)
                nc.vector.scalar_tensor_tensor(
                    msg[:, :].rearrange("p (a c) -> p a c", c=HEAD_DIM),
                    R[:, :].rearrange("p (a c) -> p a c", c=HEAD_DIM), 0.0,
                    rz[:, :].unsqueeze(2).to_broadcast([P, EQ * HEADS, HEAD_DIM]),
                    ALU.max, ALU.mult).then_inc(new_done, 1)
                yield
                dve.wait_ge(new_done, g.g + 1)
                dve.wait_ge(kept, g.g + 1)
                o = t.x1[:, bass.ds(g.times(EG), EG)]
                nc.vector.tensor_tensor(o, msg[:, :], o, ALU.add).then_inc(x1_done, 1)
                yield

            def sum_scan(g):
                dve.wait_ge(exps, g.g + 1)
                nc.vector.tensor_tensor_scan(z[:, :], decay[:, :], weight[:, :], z[:, EG - 1:EG], ALU.mult, ALU.add)
                yield
                dve.wait_ge(g_full, g.g + 1)
                wait(dve, x1_done, g.g)
                nc.vector.scalar_tensor_tensor(msg[:, :], G[:, :], t.b_src[:, 0:1], weight[:, :],
                                               ALU.add, ALU.mult).then_inc(msg_done, 1)
                yield
                dve.wait_ge(msg_done, g.g + 1)
                nc.vector.tensor_tensor_scan(h[:, :], decay[:, :], msg[:, :], h[:, EG - 1:EG],
                                             ALU.mult, ALU.add).then_inc(h_done, 1)
                yield

            def wide(i):
                e = i + 2
                if is_group(e):
                    yield from edge_norm(e, xs[e.k % 4], 0, src_normed)
                if is_group(i - 1):
                    yield from new_rows(i - 1)
                if is_group(i):
                    yield from sum_scan(i)
                if is_group(e):
                    yield from edge_norm(e, xd[e.k % 4], EQ, dst_normed)

            def body(i):
                tiles = statistics(i + 3, i + 2)
                if is_group(i):
                    score_scan(i, tiles)
                ins = None
                for ins in tiles:
                    pass
                rest = wide(i)
                if ins is not None:
                    own.step(ins)
                    lo, hi = 0 if is_group(i + 3) else 2 * EQ, 2 * EQ + DQ if is_group(i + 2) else 2 * EQ
                    r = P if is_group(i + 3) else height(i + 2)
                    s = tiny[(i.k + 1) % 2]
                    wait(dve, node_normed, i.g + 1)
                    norm_scale(nc, own, stats, lo, hi, s, rest, r)
                    c = (slice(0, r), slice(2 * EQ, hi))
                    if hi > 2 * EQ:
                        nc.vector.scalar_tensor_tensor(s.shift[c], s.mean[c], -1.0, s.rstd[c], ALU.mult,
                                                       ALU.mult).then_inc(scaled, 1)
                for _ in rest:
                    pass

            lo, hi, per = 4, 44, NORM_STEPS + 3
            for g in range(-3, lo):
                body(group(g))
            first = own.base + own.k - lo * per
            with dve.Fori(lo // 4, hi // 4) as turn:
                for k in range(4):
                    i = Group(turn, k)
                    own.start(i.times(per, first))
                    body(i)
                    assert own.k == per
            own.start(hi * per + first)
            for g in range(hi, NEG + 1):
                body(group(g))

        @block.tensor
        def _(pe):
            def turn(tile, first, use, r=P, strided=True):
                b, n = use
                wait(pe, tp_free[b], n)
                for q in range(EQ):
                    o = TP[b][:, q:EG:EQ] if strided else TP[b][:, q * r:(q + 1) * r]
                    ins = nc.tensor.transpose(o, tile[0:r, first + q, :], t.ident[0:r, 0:r])
                ins.then_inc(tp_full[b], 1)

            def edge_logits(g):
                uses, k = edge_tp(g), g.k % 2
                pe.wait_ge(s_er[k], g.half * 16 + 16)
                turn(er[k], 0, uses[0])
                pe.wait_ge(src_normed, g.g + 1)
                turn(xn[k], 0, uses[1])
                pe.wait_ge(dst_normed, g.g + 1)
                turn(xn[k], EQ, uses[2])
                wait(pe, y_free, g.times(3, -3))
                for j, W, hT in ((0, t.W_edgeT, eT), (1, t.W_srcT, hsT), (2, t.W_dstT, hdT)):
                    b, n = uses[j]
                    pe.wait_ge(tp_free[b], n + 1)
                    ins = nc.tensor.matmul(T[:, :], W[:, :], hT[:, :], start=j == 0, stop=j == 2)
                ins.then_inc(logits, 1)

            def edge_scores(g):
                pe.wait_ge(signs, g.g + 1)
                wait(pe, gaps, g.g)
                nc.tensor.matmul(S[:, :], t.A_pos[:, :], pos[:, :], start=True, stop=False)
                nc.tensor.matmul(S[:, :], t.A_neg[:, :], neg[:, :], start=False, stop=True).then_inc(scores, 1)

            def edge_summands(g):
                wait(pe, msg_done, g.g)
                nc.tensor.matmul(G[:, :], t.W_srcT[:, :], hsT[:, :], start=True, stop=False)
                nc.tensor.matmul(G[:, :], t.W_edgeT[:, :], eT[:, :], start=False, stop=True).then_inc(g_full, 1)

            def own_part(g):
                wait(pe, y_free, g.times(3, -1))
                pe.wait_ge(s_last[g.k % 2], g.half * 16 + 16)
                nc.tensor.matmul(Y[:, :], t.W1T[:, :], hdT[:, :], start=True, stop=False)
                nc.tensor.matmul(Y[:, :], t.ones_row_bf[:, :], last[g.k % 2][:, :], start=False,
                                 stop=True).then_inc(y_full, 1)

            def back_rows(g):
                pe.wait_ge(h_done, g.g + 1)
                wait(pe, new_done, g.g)
                for q in range(EQ):
                    nc.tensor.transpose(R[:, q * P:(q + 1) * P], h[:, q:EG:EQ], t.ident[:, :])
                for q in range(EQ):
                    ins = nc.tensor.matmul(ZT[:, q * HEADS:(q + 1) * HEADS], z[:, q:EG:EQ], t.pick[:, :],
                                           start=True, stop=True)
                ins.then_inc(back, 1)

            def node_turn(i):
                pe.wait_ge(node_normed, i.g + 1)
                for m, use in enumerate(node_tp(i)):
                    turn(xrn, m * EQ, use, r=height(i), strided=False)

            def node_product(i):
                w = EQ * height(i)
                for m, (b, n) in enumerate(node_tp(i)):
                    pe.wait_ge(tp_free[b], n + 1)
                    if m == 0:
                        pe.wait_ge(y_free, i.times(3, 1))
                    nc.tensor.matmul((Y, T)[m][:, 0:w], t.W1T[:, :], hrT[:, m * w:(m + 1) * w],
                                     start=True, stop=True).then_inc(y_full, 1)

            def body(i):
                e = i + 1
                if is_group(e):
                    edge_logits(group(e.g) if e.known else e)
                if is_group(i):
                    node_turn(i)
                if is_group(e):
                    edge_scores(e)
                if is_group(i):
                    node_product(i)
                if is_group(e):
                    edge_summands(e)
                if is_group(e):
                    own_part(e)
                if is_group(i):
                    back_rows(i)

            unrolled(pe, -1, 4, 44, NEG, body)

        @block.scalar
        def _(act):
            for i in range(2):
                act.sem_inc(s_y0_stored[i], 16)

            def evacuate(o, func, use, w=EG):
                b, n = use
                act.wait_ge(tp_full[b], n + 1)
                nc.scalar.activation(o, TP[b][:, 0:w], func).then_inc(tp_free[b], 1)

            def edge_rows(g):
                for o, func, use in zip((eT, hsT, hdT), (ACT.Copy, ACT.Relu, ACT.Relu), edge_tp(g)):
                    evacuate(o[:, :], func, use)

            def softmax(g):
                act.wait_ge(gaps, g.g + 1)
                nc.scalar.activation(decay[:, :], rise[:, :], ACT.Exp, scale=-1.0)
                nc.scalar.activation(weight[:, :], gap[:, :], ACT.Exp).then_inc(exps, 1)

            def both_signs(g):
                act.wait_ge(logits, g.g + 1)
                nc.scalar.activation(pos[:, :], T[:, :], ACT.Relu, bias=t.b_sum[:, 0:1])
                nc.scalar.activation(neg[:, :], T[:, :], ACT.Relu, bias=t.b_sum_neg[:, 0:1],
                                     scale=-1.0).then_inc(signs, 1)

            def node_rows(i):
                w = EQ * height(i)
                for m, use in enumerate(node_tp(i)):
                    evacuate(hrT[:, m * w:(m + 1) * w], ACT.Relu, use, w)

            def node_hidden(i):
                k, w = i.k % 2, EQ * height(i)
                act.wait_ge(s_y0_stored[k], i.half * 16 + 16)
                for m in range(2):
                    act.wait_ge(y_full, i.times(3, 2 + m))
                    nc.scalar.activation(y0[k][:, m * w:(m + 1) * w], (Y, T)[m][:, 0:w], ACT.Relu, bias=t.b1[:, 0:1],
                                         accum_out=t.col("node", i.times(2, m))).then_inc(y_free, 1)

            def own_hidden(g):
                act.wait_ge(y_full, g.times(3, 1))
                nc.scalar.activation(yd[:, :], Y[:, :], ACT.Relu, bias=t.b1[:, 0:1],
                                     accum_out=t.col("edge_old", g.g)).then_inc(y_free, 1)

            def node_norm(i):
                k, r = i.k % 4, height(i)
                s = tiny[(i.k + 1) % 2]
                act.wait_ge(scaled, i.g + 1)
                act.wait_ge(s_xr[k], i.quarter * 16 + 16)
                for q in range(DQ):
                    m = 2 * EQ + q
                    ins = nc.scalar.activation(xrn[0:r, q, :], xr[k][0:r, q, :], ACT.Identity,
                                               bias=s.shift[0:r, m:m + 1], scale=s.rstd[0:r, m:m + 1])
                ins.then_inc(node_normed, 1)

            def keep_rows(g):
                act.wait_ge(s_xd[g.k % 4], g.quarter * 64 + 64)
                nc.scalar.copy(t.x1[:, bass.ds(g.times(EG), EG)], xd[g.k % 4][:, :, :].rearrange(FLAT)
                               ).then_inc(kept, 1)

            def squares(i):
                e, w = i + 1, DQ * height(i)
                if is_group(e):
                    act.wait_ge(y_free, e.times(3, 1))
                    nc.scalar.activation(yd[:, :], yd[:, :], ACT.Square,
                                         accum_out=t.col("edge_old_sq", e.g)).then_inc(yd_squared, 1)
                if is_group(i):
                    act.wait_ge(y_free, i.times(3, 3))
                    nc.scalar.activation(hrT[:, 0:w], y0[i.k % 2][:, 0:w], ACT.Square,
                                         accum_out=t.col("node_sq", i.g)).then_inc(y0_squared, 1)

            def body(i):
                e = group(i.g + 1) if i.known else i + 1
                if is_group(i):
                    softmax(i)
                if is_group(e):
                    edge_rows(e)
                squares(i - 1)
                if is_group(e):
                    both_signs(e)
                if is_group(i + 2):
                    keep_rows(i + 2)
                if is_group(i):
                    wait(act, y0_squared, i.g)
                    node_rows(i)
                if is_group(e):
                    node_norm(e)
                if is_group(i):
                    node_hidden(i)
                if is_group(e):
                    wait(act, yd_squared, e.g)
                    own_hidden(e)

            unrolled(act, -2, 4, 44, NEG, body)
            squares(group(LAST))




def aggregation(nc, t, d, out):
    with ExitStack() as ctx:
        a = Allocator(nc, ctx, "agg")
        sb, ps, sem = a.sb, a.ps, a.sem

        def sems(name, n=2):
            return [sem(f"{name}{i}") for i in range(n)]

        def two(name, shape, dt=F32):
            return [sb(f"{name}{i}", shape, dt) for i in range(2)]

        idx = [sb(f"idx{i}", [P, EQ], I32) for i in range(4)]
        xs = [sb(f"xs{i}", [P, EQ, P]) for i in range(4)]
        xsn, xdn, hsT, hdT, agg, y = (two("xsn", [P, EQ, P]), two("xdn", [P, EQ, P]), two("hsT", [P, EG]),
                                      two("hdT", [P, EG]), two("agg", [P, EG]), two("y", [P, EG]))
        keep, last, junk = two("keep", [P, EG], BF16), two("last", [1, EG], BF16), sb("junk", [P, EG])
        stats, tiny = sb("stats", [P, 2 * EQ, 6]), [Tiny(a, 2 * EQ, i) for i in range(2)]
        TS, TD, Y = [ps("TS0"), ps("TS1")], [ps("TD0"), ps("TD1")], [ps("Y0"), ps("Y1")]
        s_idx, s_xs, s_keep, s_last, s_stored = sems("idx", 4), sems("xs", 4), sems("keep"), sems("last"), sems("stored")
        var_done, root, scaled, src_normed, dst_normed, turned, hs_done, hd_done, agg_done = (
            sem(n) for n in ("var_done", "root", "scaled", "src_normed", "dst_normed", "turned", "hs_done", "hd_done",
                             "agg_done"))
        y_full, y_done, squared, v_step = (sem(n) for n in ("y_full", "y_done", "squared", "v_step"))
        gather_v = d.gather[0].rearrange("(g p q) -> g p q", p=P, q=EQ)
        block = ctx.enter_context(nc.Block())

        @block.sync
        def _(sp):
            def load_idx(g):
                sp.dma_start(idx[g.k % 4][:, :], rows(gather_v, g.g)).then_inc(s_idx[g.k % 4], 16)

            def load_masks(g):
                k = g.k % 2
                sp.dma_start(keep[k][:, :], d.keep[bass.ds(g.times(EG), EG)].partition_broadcast(P)
                             ).then_inc(s_keep[k], 16)
                sp.dma_start(last[k][:, :], d.last[bass.ds(g.times(EG), EG)].unsqueeze(0)).then_inc(s_last[k], 16)

            def body(i):
                known = i.known
                if not known or i.g + 6 < NEG:
                    j = i + 2
                    wait(sp, s_xs[j.k % 4], j.quarter * 64 + 64)
                    load_idx(i + 6)
                wait(sp, y_done, i.g + 1)
                if not known or i.g + 2 < NEG:
                    load_masks(i + 2)
                sp.dma_start(d.y1[:, bass.ds(i.times(EG), EG)], y[i.k % 2][:, :]).then_inc(s_stored[i.k % 2], 16)

            for g in range(4):
                load_idx(group(g))
            for g in range(2):
                load_masks(group(g))
            for g in range(2):
                wait(sp, s_xs[g], 64)
                load_idx(group(g + 4))
            loop(sp, 0, NEG - 7, body)
            for g in range(NEG - 7, NEG):
                body(group(g))
            for i in range(2):
                wait(sp, s_stored[i], 16 + 16 * len(range(i, NEG, 2)))

        @block.gpsimd
        def _(pool):
            def gather(j):
                k = j.k % 4
                wait(pool, s_idx[k], j.quarter * 16 + 16)
                wait(pool, src_normed, j.g - 3)
                for q in range(EQ):
                    pool.indirect_dma_start(
                        out=xs[k][:, q, :], out_offset=None, in_=out[:, :],
                        in_offset=bass.IndirectOffsetOnAxis(ap=idx[k][:, q:q + 1], axis=0)).then_inc(s_xs[k], 16)

            loop(pool, 0, NEG, gather, by_hand=4)

        @block.vector
        def _(dve):
            own = Own(dve, v_step)

            def scan(g):
                k = g.k % 2
                dve.wait_ge(s_keep[k], g.half * 16 + 16)
                dve.wait_ge(hs_done, g.g + 1)
                wait(dve, agg_done, g.g)
                nc.vector.tensor_tensor_scan(agg[k][:, :], keep[k][:, :], hsT[k][:, :], agg[1 - k][:, EG - 1:EG],
                                             ALU.mult, ALU.add).then_inc(agg_done, 1)

            def scales(g):
                s = tiny[g.k % 2]
                c = (slice(0, P), slice(EQ, 2 * EQ))
                dve.wait_ge(root, g.g + 1)
                own.step(nc.vector.reciprocal(s.rstd[:, :], s.x[:, :]))
                nc.vector.scalar_tensor_tensor(s.shift[c], s.mean[c], -1.0, s.rstd[c], ALU.mult,
                                               ALU.mult).then_inc(scaled, 1)

            def wide(i):
                if is_group(i):
                    scan(i)
                    yield
                if is_group(i + 1):
                    k = (i + 1).k % 2
                    for q in range(EQ):
                        ins = nc.vector.tensor_scalar(xsn[k][:, q, :], xs[(i + 1).k % 4][:, q, :],
                                                      tiny[k].mean[:, q:q + 1], tiny[k].rstd[:, q:q + 1],
                                                      ALU.subtract, ALU.mult)
                        if q == EQ - 1:
                            ins.then_inc(src_normed, 1)
                        yield

            def body(i):
                e = i + 2
                if is_group(i + 1):
                    scales(i + 1)
                rest = wide(i)
                if is_group(e):
                    for q in range(EQ):
                        nc.vector.bn_stats(stats[:, EQ + q, :], t.x1[:, bass.ds(e.times(EG, q * P), P)])
                    dve.wait_ge(s_xs[e.k % 4], e.quarter * 64 + 64)
                    for q in range(EQ):
                        ins = nc.vector.bn_stats(stats[:, q, :], xs[e.k % 4][:, q, :])
                    own.step(ins, rest)
                    wait(dve, dst_normed, i.g + 1)
                    mean_var(nc, own, stats, 0, 2 * EQ, tiny[i.k % 2], rest).then_inc(var_done, 1)
                for _ in rest:
                    pass

            nc.vector.memset(agg[1][:, :], 0.0)
            lo, hi, per = 4, 44, 4
            for g in range(-2, lo):
                body(group(g))
            first = own.base + own.k - lo * per
            with dve.Fori(lo // 4, hi // 4) as turn:
                for k in range(4):
                    i = Group(turn, k)
                    own.start(i.times(per, first))
                    body(i)
                    assert own.k == per
            own.start(hi * per + first)
            for g in range(hi, NEG):
                body(group(g))

        @block.tensor
        def _(pe):
            def turn(g):
                for rows_, normed, bank in ((xsn, src_normed, TS), (xdn, dst_normed, TD)):
                    pe.wait_ge(normed, g.g + 1)
                    for q in range(EQ):
                        ins = nc.tensor.transpose(bank[g.k % 2][:, q:EG:EQ], rows_[g.k % 2][:, q, :], t.ident[:, :])
                    ins.then_inc(turned, 1)

            def product(g):
                k = g.k % 2
                pe.wait_ge(s_last[k], g.half * 16 + 16)
                pe.wait_ge(hd_done, g.g + 1)
                nc.tensor.matmul(Y[k][:, :], t.W1T[:, :], hdT[k][:, :], start=True, stop=False)
                nc.tensor.matmul(Y[k][:, :], t.ones_row_bf[:, :], last[k][:, :], start=False, stop=False)
                pe.wait_ge(agg_done, g.g + 1)
                nc.tensor.matmul(Y[k][:, :], t.W1T[:, :], agg[k][:, :], start=False, stop=True).then_inc(y_full, 1)

            def body(i):
                if is_group(i):
                    product(i)
                if is_group(i + 1):
                    turn(i + 1)

            unrolled(pe, -1, 4, 44, NEG, body)

        @block.scalar
        def _(act):
            for i in range(2):
                act.sem_inc(s_stored[i], 16)

            def evacuate(g):
                k = g.k % 2
                act.wait_ge(turned, g.times(2, 1))
                nc.scalar.activation(hsT[k][:, :], TS[k][:, :], ACT.Relu).then_inc(hs_done, 1)
                act.wait_ge(turned, g.times(2, 2))
                nc.scalar.activation(hdT[k][:, :], TD[k][:, :], ACT.Relu).then_inc(hd_done, 1)

            def hidden(g):
                k = g.k % 2
                act.wait_ge(s_stored[k], g.half * 16 + 16)
                act.wait_ge(y_full, g.g + 1)
                nc.scalar.activation(y[k][:, :], Y[k][:, :], ACT.Relu, bias=t.b1[:, 0:1],
                                     accum_out=t.col("edge_new", g.g)).then_inc(y_done, 1)

            def dst_norm(g):
                s = tiny[g.k % 2]
                act.wait_ge(scaled, g.g + 1)
                for q in range(EQ):
                    m = EQ + q
                    ins = nc.scalar.activation(xdn[g.k % 2][:, q, :], t.x1[:, bass.ds(g.times(EG, q * P), P)],
                                               ACT.Identity, bias=s.shift[:, m:m + 1], scale=s.rstd[:, m:m + 1])
                ins.then_inc(dst_normed, 1)

            def square(g):
                act.wait_ge(y_done, g.g + 1)
                wait(act, squared, g.g)
                nc.scalar.activation(junk[:, :], y[g.k % 2][:, :], ACT.Square,
                                     accum_out=t.col("edge_new_sq", g.g)).then_inc(squared, 1)

            def body(i):
                if is_group(i + 1):
                    dst_norm(i + 1)
                if is_group(i + 2):
                    act.wait_ge(var_done, i.g + 3)
                    s = tiny[i.k % 2]
                    nc.scalar.activation(s.x[:, :], s.v[:, :], ACT.Sqrt).then_inc(root, 1)
                if is_group(i + 1):
                    evacuate(i + 1)
                if is_group(i):
                    hidden(i)
                    square(i)

            unrolled(act, -2, 4, 44, NEG, body)




class BatchNorm:

    def __init__(self, nc, a, t):
        self.nc, self.t = nc, t
        self.part, self.tot, self.c = a.sb("bn_part", [P, 6]), a.sb("bn_tot", [P, 2]), a.sb("bn_c", [P, 8])
        self.ones, self.shift, self.bank = a.sb("bn_ones", [P, P]), a.sb("bn_shift", [P, P]), a.ps("bn_bank", (P, P))
        self.v_step, self.var_done, self.root, self.folded, self.product, self.row_done = (
            a.sem(n) for n in ("v_step", "var_done", "root", "folded", "product", "row_done"))

    def vector(self, dve):
        nc, t, part, tot, c, ones, shift = self.nc, self.t, self.part, self.tot, self.c, self.ones, self.shift
        own = Own(dve, self.v_step)
        for i, n in enumerate(("node", "edge_old", "edge_new", "node_sq", "edge_old_sq", "edge_new_sq")):
            o, w = t.cols[n]
            nc.vector.reduce_sum(part[:, i:i + 1], t.sums[:, o:o + w], axis=AX.X)
        own.step(nc.vector.memset(ones[:, :], 1.0))
        for i in range(2):
            ins = nc.vector.tensor_tensor(tot[:, i:i + 1], part[:, 3 * i + 2:3 * i + 3], part[:, 3 * i + 1:3 * i + 2],
                                          ALU.subtract)
        own.step(ins)
        for i in range(2):
            ins = nc.vector.tensor_tensor(tot[:, i:i + 1], tot[:, i:i + 1], part[:, 3 * i:3 * i + 1], ALU.add)
        own.step(ins)
        mean, sq, var, rstd, s, sh = (c[:, i:i + 1] for i in range(6))
        own.step(nc.vector.tensor_scalar(c[:, 0:2], tot[:, 0:2], 1.0 / N, None, ALU.mult))
        own.step(nc.vector.tensor_tensor(var, mean, mean, ALU.mult))
        own.step(nc.vector.tensor_tensor(var, sq, var, ALU.subtract))
        nc.vector.tensor_scalar(var, var, 0.0, EPS, ALU.max, ALU.add).then_inc(self.var_done, 1)
        dve.wait_ge(self.root, 1)
        own.step(nc.vector.reciprocal(rstd, rstd))
        own.step(nc.vector.tensor_tensor(s, rstd, t.gamma[:, :], ALU.mult))
        nc.vector.tensor_scalar(t.W2s[:, :], t.W2T[:, :], s, None, ALU.mult)
        own.step(nc.vector.tensor_tensor(sh, mean, s, ALU.mult))
        own.step(nc.vector.tensor_tensor(sh, t.beta[:, :], sh, ALU.subtract))
        nc.vector.tensor_scalar(shift[:, :], ones[:, :], sh, None, ALU.mult).then_inc(self.folded, 1)
        dve.wait_ge(self.product, 1)
        nc.vector.tensor_copy(t.b_row[:, :], self.bank[:, :]).then_inc(self.row_done, 1)
        dve.wait_ge(self.row_done, 1)

    def scalar(self, act):
        act.wait_ge(self.var_done, 1)
        self.nc.scalar.activation(self.c[:, 3:4], self.c[:, 2:3], ACT.Sqrt).then_inc(self.root, 1)

    def tensor(self, pe):
        nc, t = self.nc, self.t
        pe.wait_ge(self.folded, 1)
        nc.tensor.matmul(self.bank[:, :], self.shift[:, :], t.W2T[:, :], start=True, stop=False)
        nc.tensor.matmul(self.bank[:, :], t.ones_row[:, :], t.b2_row[:, :], start=False,
                         stop=True).then_inc(self.product, 1)




def result(nc, t, d, x, out):
    with ExitStack() as ctx:
        a = Allocator(nc, ctx, "out")
        sb, ps, sem = a.sb, a.ps, a.sem

        def sems(name, n=2):
            return [sem(f"{name}{i}") for i in range(n)]

        xr = [sb(f"xr{i}", [P, DQ * P]) for i in range(4)]
        y0 = [sb(f"y0{i}", [P, DG]) for i in range(4)]
        y1 = [sb(f"y1{i}", [P, EG]) for i in range(4)]
        staged = [sb(f"staged{i}", [P, EG]) for i in range(4)]
        sidx = [sb(f"sidx{i}", [P, EQ], I32) for i in range(4)]
        D, Z = [ps(f"D{i}") for i in range(4)], [ps(f"Z{i}") for i in range(2)]
        s_xr, s_y0, s_y1, s_out = sems("xr", 4), sems("y0", 4), sems("y1", 4), sems("stored", 4)
        need, where = sb("need", [1, NEG], I32), sb("where", [P, NEG, EQ], I32)
        need_loaded, need_step, need_done = sem("need_loaded"), sem("need_step"), sem("need_done")
        s_where, s_scattered, s_staged = sem("where"), sems("scattered", 4), sem("staged")
        node_full, edge_full, node_done, edge_done, biased, nodes_written = (
            sem(n) for n in ("node_full", "edge_full", "node_done", "edge_done", "biased", "nodes_written"))
        scatter_v = d.scatter.rearrange("(g p q) -> g p q", p=P, q=EQ)
        x_full = x[0:(ND - 1) * DG, :].rearrange("(g p q) f -> g p (q f)", p=P, q=DQ)
        x_tail = x[(ND - 1) * DG:N, :].rearrange("(p q) f -> p (q f)", q=DQ)
        o_full = out[0:(ND - 1) * DG, :].rearrange("(g p q) f -> g p (q f)", p=P, q=DQ)
        o_tail = out[(ND - 1) * DG:N, :].rearrange("(p q) f -> p (q f)", q=DQ)
        TAIL = group(ND - 1)
        batch_norm = BatchNorm(nc, a, t)
        block = ctx.enter_context(nc.Block())

        @block.sync
        def _(sp):
            def load(g):
                k = g.k % 4
                if g.known and g.g == ND - 1:
                    w = DTAIL * DQ
                    sp.dma_start(xr[k][0:DTAIL, :], x_tail).then_inc(s_xr[k], 16)
                    sp.dma_start(y0[k][:, 0:w], d.y0[:, (ND - 1) * DG:N]).then_inc(s_y0[k], 16)
                else:
                    sp.dma_start(xr[k][:, :], rows(x_full, g.g)).then_inc(s_xr[k], 16)
                    sp.dma_start(y0[k][:, :], d.y0[:, bass.ds(g.times(DG), DG)]).then_inc(s_y0[k], 16)
                sp.dma_start(y1[k][:, :], d.y1[:, bass.ds(g.times(EG), EG)]).then_inc(s_y1[k], 16)

            def body(i):
                k = i.k % 4
                known = i.known
                wait(sp, node_done, i.g + 1)
                if known and i.g == ND - 1:
                    sp.dma_start(o_tail, xr[k][0:DTAIL, :]).then_inc(s_out[k], 16)
                else:
                    sp.dma_start(rows(o_full, i.g), xr[k][:, :]).then_inc(s_out[k], 16)
                if not known or i.g >= 1:
                    wait(sp, s_out[(i.k - 1) % 4], (i - 1).quarter * 16 + 16)
                    sp.sem_inc(nodes_written, 1)
                    if not known or i.g + 3 < ND:
                        wait(sp, edge_done, i.g)
                        load(group(i.g + 3) if known else i + 3)

            sp.dma_start(need[:, :], d.gather[1].rearrange("(g e) -> e g", e=EG)[EG - 1:EG, :],
                         allow_slow_non_contiguous=True).then_inc(need_loaded, 16)
            sp.dma_start(where[:, :, :], d.scatter.rearrange("(g p q) -> p g q", p=P, q=EQ)).then_inc(s_where, 16)
            for g in range(4):
                load(group(g))
            loop(sp, 0, ND - 5, body, by_hand=4)
            for g in range(ND - 5, ND):
                body(group(g))
            wait(sp, s_out[(ND - 1) % 4], TAIL.quarter * 16 + 16)
            sp.sem_inc(nodes_written, 1)

        @block.vector
        def _(dve):
            batch_norm.vector(dve)
            dve.wait_ge(need_loaded, 16)
            nc.vector.tensor_scalar(need[:, :], need[:, :], DG.bit_length() - 1, None,
                                    ALU.logical_shift_right).then_inc(need_step, 1)
            dve.wait_ge(need_step, 1)
            nc.vector.tensor_scalar(need[:, :], need[:, :], 1.0, None, ALU.add).then_inc(need_done, 1)

            def nodes(i, r=P):
                k, w = i.k % 4, DQ * P // 2
                dve.wait_ge(s_xr[k], i.quarter * 16 + 16)
                v = xr[k][0:r, :].rearrange("p (q f) -> p q f", f=P)
                nc.vector.tensor_tensor(v, v, t.b_row[0:r, :].unsqueeze(1).to_broadcast([r, DQ, P]),
                                        ALU.add).then_inc(biased, 1)
                dve.wait_ge(biased, i.times(2, 1))
                for m in range(2):
                    dve.wait_ge(node_full, i.times(2, m + 1))
                    o = xr[k][0:r, m * w:(m + 1) * w]
                    ins = nc.vector.tensor_tensor(o, D[(2 * i.k + m) % 4][0:r, :], o, ALU.add)
                ins.then_inc(node_done, 1)

            def edges(i):
                o = t.x1[:, bass.ds(i.times(EG), EG)]
                v = o.rearrange("p (q f) -> p q f", f=P)
                nc.vector.tensor_tensor(v, v, t.b_row[:, :].unsqueeze(1).to_broadcast([P, EQ, P]),
                                        ALU.add).then_inc(biased, 1)
                dve.wait_ge(biased, i.times(2, 2))
                dve.wait_ge(edge_full, i.g + 1)
                nc.vector.tensor_tensor(o, Z[i.k % 2][:, :], o, ALU.add).then_inc(edge_done, 1)

            def body(i):
                nodes(i)
                edges(i)

            loop(dve, 0, ND - 1, body)
            nodes(TAIL, DTAIL)
            edges(TAIL)

        @block.tensor
        def _(pe):
            batch_norm.tensor(pe)
            def body(i, r=P):
                k = i.k % 4
                pe.wait_ge(s_y0[k], i.quarter * 16 + 16)
                for m in range(2):
                    wait(pe, node_done, i.g - 1)
                    for q in range(EQ):
                        c = (m * EQ + q) * r
                        ins = nc.tensor.matmul(D[(2 * i.k + m) % 4][0:r, q * P:(q + 1) * P], y0[k][:, c:c + r],
                                               t.W2s[:, :], start=True, stop=True)
                    ins.then_inc(node_full, 1)
                pe.wait_ge(s_y1[k], i.quarter * 16 + 16)
                wait(pe, edge_done, i.g - 1)
                for q in range(EQ):
                    ins = nc.tensor.matmul(Z[i.k % 2][:, q * P:(q + 1) * P], y1[k][:, q:EG:EQ], t.W2s[:, :],
                                           start=True, stop=True)
                ins.then_inc(edge_full, 1)

            loop(pe, 0, ND - 1, body, by_hand=2)
            body(TAIL, DTAIL)

        @block.scalar
        def _(act):
            batch_norm.scalar(act)
            def stage(g):
                k = g.k % 4
                wait(act, s_scattered[k], g.quarter * 64)
                act.wait_ge(edge_done, g.g + 1)
                nc.scalar.copy(sidx[k][:, :], where[:, bass.ds(g.g, 1), :].rearrange("p a q -> p (a q)"))
                nc.scalar.copy(staged[k][:, :], t.x1[:, bass.ds(g.times(EG), EG)]).then_inc(s_staged, 1)

            act.wait_ge(s_where, 16)
            loop(act, 0, NEG, stage, by_hand=4)

        @block.gpsimd
        def _(pool):
            wait(pool, need_done, 1)

            def scatter(g):
                k = g.k % 4
                wait(pool, s_staged, g.g + 1)
                rank = pool.value_load(need[0:1, bass.ds(g.g, 1)], min_val=1, max_val=ND)
                wait(pool, nodes_written, rank)
                for q in range(EQ):
                    pool.indirect_dma_start(
                        out=out[:, :], out_offset=bass.IndirectOffsetOnAxis(ap=sidx[k][:, q:q + 1], axis=0),
                        in_=staged[k][:, q * P:(q + 1) * P], in_offset=None, bounds_check=N - 1, oob_is_err=False
                    ).then_inc(s_scattered[k], 16)

            loop(pool, 0, NEG, scatter)
            for i in range(4):
                wait(pool, s_scattered[i], 64 * len(range(i, NEG, 4)))




class Tiles:

    def __init__(self, a):
        self.x1 = a.sb("x1", [P, EPAD])
        (self.W_srcT, self.W_dstT, self.W_edgeT, self.W1T, self.W2T, self.W2s, self.A_pos, self.A_neg, self.ident,
         self.b_row) = (a.sb(n, [P, P]) for n in ("W_srcT", "W_dstT", "W_edgeT", "W1T", "W2T", "W2s", "A_pos", "A_neg",
                                                  "ident", "b_row"))
        self.pick = a.sb("pick", [P, HEADS])
        self.unsorted = a.sb("unsorted", [1, 1], I32)
        self.ones_row, self.ones_row_bf, self.b2_row = a.sb("ones_row", [1, P]), a.sb("ones_row_bf", [1, P], BF16), \
            a.sb("b2_row", [1, P])
        (self.b_src, self.b_dst, self.attn, self.b1, self.gamma, self.beta, self.b_sum, self.b_sum_neg) = (
            a.sb(n, [P, 1]) for n in ("b_src", "b_dst", "attn", "b1", "gamma", "beta", "b_sum", "b_sum_neg"))
        self.cols, o = {}, 0
        for n, w in (("node", 2 * ND), ("node_sq", ND), ("edge_old", NEG), ("edge_old_sq", NEG),
                     ("edge_new", NEG), ("edge_new_sq", NEG)):
            self.cols[n] = (o, w)
            o += w
        self.sums = a.sb("sums", [P, o])

    def col(self, name, i):
        return self.sums[:, bass.ds(self.cols[name][0] + i, 1)]


class Scratch:

    def __init__(self, nc):
        def dram(name, shape, dt=F32):
            return nc.dram_tensor(name, list(shape), dt, kind="Internal").ap()

        self.src, self.dst = dram("src_sorted", (E, 1), I32), dram("dst_sorted", (E, 1), I32)
        self.attr = dram("edge_attr_sorted", (E, P))
        self.gather = dram("gather_rows", (2, EPAD), I32)
        self.scatter = dram("scatter_rows", (EPAD,), I32)
        self.keep, self.start, self.last = (dram(n, (EPAD,), BF16) for n in ("keep", "start", "last"))
        self.y0 = dram("y_nodes", (P, N))
        self.y1 = dram("y_edges", (P, EPAD))


def program(nc, x, src, dst, edge_attr, W_src, b_src, W_dst, b_dst, W_edge, attn, W1, b1, gamma, beta, W2, b2, out):
    d = Scratch(nc)

    def column(v):
        return v.rearrange("(f o) -> f o", o=1)

    w = {"W_src": W_src, "W_dst": W_dst, "W_edge": W_edge, "W1": W1, "W2": W2, "b_src": column(b_src),
         "b_dst": column(b_dst), "attn": attn.rearrange("h (f o) -> (h f) o", o=1), "b1": column(b1),
         "gamma": column(gamma), "beta": column(beta), "b2": b2.unsqueeze(0)}
    with ExitStack() as ctx:
        t = Tiles(Allocator(nc, ctx, "t"))
        constants(nc, t, w, d, src, dst)
        sort_edges(nc, t, d, src, dst, edge_attr)
        edge_tables(nc, d)
        attention(nc, t, d, x, edge_attr, out)
        aggregation(nc, t, d, out)
        result(nc, t, d, x, out)


_INS = ['x', 'src', 'dst', 'edge_attr_128', 'L0_gnn_W_src', 'L0_gnn_b_src', 'L0_gnn_W_dst', 'L0_gnn_b_dst',
        'L0_gnn_W_edge', 'L0_gnn_attn', 'L1_gnn_W1', 'L1_gnn_b1', 'L1_gnn_gamma', 'L1_gnn_beta', 'L1_gnn_W2',
        'L1_gnn_b2']


def kernel(**inputs):
    import concourse.bacc as _bacc
    from concourse.bass_utils import run_bass_kernel_spmd as _run

    nc = _bacc.Bacc("TRN2", target_bir_lowering=False, num_devices=1)
    arrays, args = {}, []
    for name in _INS:
        v = np.ascontiguousarray(inputs[name])
        arrays[f"in_{name}"] = v
        args.append(nc.dram_tensor(f"in_{name}", v.shape, mybir.dt.from_np(v.dtype), kind="ExternalInput").ap())
    args.append(nc.dram_tensor("out_0", (N, P), F32, kind="ExternalOutput").ap())
    program(nc, *args)
    return _run(nc, [arrays], core_ids=[0]).results[0]["out_0"]
```

```python
from contextlib import ExitStack

import numpy as np

import concourse.bass as bass
from concourse import mybir

F32 = mybir.dt.float32
BF16 = mybir.dt.bfloat16
I32 = mybir.dt.int32
ALU = mybir.AluOpType
ACT = mybir.ActivationFunctionType
AX = mybir.AxisListType

P = 128
N, E = 50000, 25000
HEADS, HEAD_DIM = 8, 16
SLOPE = 0.2
EPS = 1e-5
EQ, EG = 4, 512
NEG = -(-E // EG)
EPAD = NEG * EG
DQ, DG = 8, 1024
ND = -(-N // DG)
DTAIL = (N - (ND - 1) * DG) // DQ
ETAIL = E - (NEG - 1) * EG
COPIES, COPY_ROWS = 10, 25
STAGE_LAG = COPIES + 2
SCATTER_LAG = STAGE_LAG + 6
DIRECT = NEG - SCATTER_LAG
RESIDENT = 36
FAR = float(2 ** 127)
NOWHERE = 65536
RSQRT_SEED = float(0x5F3759DF)
assert DIRECT + STAGE_LAG < NEG and (ND - 1) * DG + DTAIL * DQ == N and ETAIL % EQ == 0 and NEG == ND


class Allocator:

    def __init__(self, nc, ctx, tag):
        self.nc, self.ctx, self.tag = nc, ctx, tag

    def sb(self, name, shape, dt=F32):
        return self.ctx.enter_context(self.nc.sbuf_tensor(f"{self.tag}_{name}", shape, dt))

    def ps(self, name, shape=(P, 512), dt=F32):
        return self.ctx.enter_context(self.nc.psum_tensor(f"{self.tag}_{name}", list(shape), dt))

    def sem(self, name):
        return self.ctx.enter_context(self.nc.semaphore(f"{self.tag}_{name}"))


class Group:

    def __init__(self, t, k, low=0):
        self.t, self.k, self.low = t, k, low

    def __add__(self, n):
        return Group(self.t, self.k + n)

    def __sub__(self, n):
        return self + -n

    def times(self, a, b=0):
        return self.t * (4 * a) + (a * self.k + b)

    def use(self, a, b):
        m = a * self.k + b
        return m % 2, self.t * (2 * a) + m // 2

    @property
    def known(self):
        return isinstance(self.t, int)

    @property
    def g(self):
        return self.times(1)

    @property
    def half(self):
        return self.t * 2 + self.k // 2

    @property
    def quarter(self):
        return self.t + self.k // 4


def group(g):
    return Group(g // 4, g % 4)


def is_group(g):
    return not g.known or 0 <= g.g < NEG


def loop(eng, start, stop, body, by_hand=0):
    lo = -(-(start + by_hand) // 4) * 4
    hi = max(stop // 4 * 4, lo)
    for g in range(start, min(lo, stop)):
        body(group(g))
    if hi > lo:
        with eng.Fori(lo // 4, hi // 4) as t:
            for k in range(4):
                body(Group(t, k))
    for g in range(hi, stop):
        body(group(g))


def unrolled(eng, start, lo, hi, stop, body):
    for g in range(start, lo):
        body(group(g))
    with eng.Fori(lo // 4, hi // 4) as t:
        for k in range(4):
            body(Group(t, k, lo))
    for g in range(hi, stop):
        body(group(g))


def resident(g):
    return (g.g if g.known else g.low) >= RESIDENT


def wait(eng, sem, value):
    if not isinstance(value, int):
        eng.wait_ge(sem, value)
        if eng.engine in (mybir.EngineType.SP, mybir.EngineType.Pool):
            eng.nop(nofuse=True)
    elif value > 0:
        eng.wait_ge(sem, value)


class Own:

    def __init__(self, engine, sem):
        self.engine, self.sem, self.base, self.k = engine, sem, 0, 0

    def start(self, base):
        self.base, self.k = base, 0

    def step(self, instruction, meanwhile=iter(())):
        self.k += 1
        instruction.then_inc(self.sem, 1)
        next(meanwhile, None)
        self.engine.wait_ge(self.sem, self.base + self.k)


def rows(view, g):
    return view[bass.ds(g, 1)].rearrange("a p n -> (a p) n")


FLAT = "p q f -> p (q f)"




TW = 256
TR = EPAD // TW
TF = E // TW
assert TR <= P and EPAD % TW == 0 and TR == TF + 1


def edge_order(nc, t, w, d, src, dst):
    with ExitStack() as ctx:
        a = Allocator(nc, ctx, "order")
        cur, nxt = a.sb("cur", [TR, TW], I32), a.sb("nxt", [TR, TW], I32)
        falls, count, ones = a.sb("falls", [TR, TW]), a.sb("count", [TR, 1]), a.sb("ones", [TR, 1])
        total = a.ps("total", (P, P))
        filled, ones_made, zeroed, ends, copies, compared, counted, summed = (
            a.sem(n) for n in ("filled", "ones_made", "zeroed", "ends", "copies", "compared", "counted", "summed"))
        block = ctx.enter_context(nc.Block())

        @block.sync
        def _(sp):
            sp.wait_ge(filled, 2)
            for shift, tile in enumerate((cur, nxt)):
                n = E - TF * TW - shift
                sp.dma_start(tile[0:TF, :], dst[shift:TF * TW + shift].rearrange("(p e) -> p e", e=TW)
                             ).then_inc(ends, 16)
                sp.dma_start(tile[TF:TR, 0:n], dst[TF * TW + shift:E].unsqueeze(0)).then_inc(ends, 16)
            sp.dma_start(d.src.rearrange("(a e) o -> a (e o)", a=1), src.unsqueeze(0)).then_inc(copies, 16)
            sp.dma_start(d.dst.rearrange("(a e) o -> a (e o)", a=1), dst.unsqueeze(0)).then_inc(copies, 16)
            for n, tile in t.columns:
                sp.dma_start(tile[:, :], w[n]).then_inc(t.columns_loaded, 16)
            sp.wait_ge(copies, 2 * 16)

        @block.gpsimd
        def _(pool):
            nc.gpsimd.memset(cur[:, :], N).then_inc(filled, 1)
            nc.gpsimd.memset(nxt[:, :], N).then_inc(filled, 1)
            nc.gpsimd.memset(ones[:, :], 1.0).then_inc(ones_made, 1)
            nc.gpsimd.memset(t.ident[:, :], 0.0).then_inc(zeroed, 1)
            pool.wait_ge(zeroed, 1)
            nc.gpsimd.affine_select(out=t.ident[:, :], in_=t.ident[:, :], compare_op=ALU.not_equal, fill=1.0,
                                    base=0, pattern=[[-1, P]], channel_multiplier=1)

        @block.vector
        def _(dve):
            nc.vector.memset(t.sums[:, :], 0.0)
            dve.wait_ge(ends, 4 * 16)
            nc.vector.tensor_tensor(falls[:, :], cur[:, :], nxt[:, :], ALU.is_gt).then_inc(compared, 1)
            dve.wait_ge(compared, 1)
            nc.vector.reduce_sum(count[:, :], falls[:, :], axis=AX.X).then_inc(counted, 1)
            dve.wait_ge(summed, 1)
            nc.vector.tensor_copy(t.unsorted[:, :], total[0:1, 0:1])

        @block.tensor
        def _(pe):
            pe.wait_ge(ones_made, 1)
            pe.wait_ge(counted, 1)
            nc.tensor.matmul(total[0:1, 0:1], count[:, :], ones[:, :], start=True, stop=True).then_inc(summed, 1)


def sort_edges(nc, t, d, src, dst, edge_attr):
    parts = 4
    with ExitStack() as ctx:
        a = Allocator(nc, ctx, "sort")
        key_of = t.x1
        ahead, behind, own_block = a.sb("ahead", [P, P]), a.sb("behind", [P, P]), a.sb("own_block", [P, P])
        below, part, key, total = (a.sb("below", [P, EPAD // parts]), a.sb("part", [P, parts]), a.sb("key", [P, 1]),
                                   a.sb("total", [P, 1]))
        rank, src_rows, dst_rows, attr_rows = (a.sb("rank", [P, 1], I32), a.sb("src_rows", [P, 1], I32),
                                               a.sb("dst_rows", [P, 1], I32), a.sb("attr_rows", [P, P]))
        dst_loaded, made, v_step, rows_loaded, ranked, rank_free, scattered = (
            a.sem(n) for n in ("dst_loaded", "made", "v_step", "rows_loaded", "ranked", "rank_free", "scattered"))
        filled = a.sem("filled")
        block = ctx.enter_context(nc.Block())

        @block.sync
        def _(sp):
            unsorted = sp.value_load(t.unsorted[0:1, 0:1], min_val=0, max_val=E)
            with sp.If(unsorted != 0):
                sp.dma_start(key_of[:, 0:E].bitcast(I32), dst.partition_broadcast(P)).then_inc(dst_loaded, 16)

        @block.vector
        def _(dve):
            unsorted = dve.value_load(t.unsorted[0:1, 0:1], min_val=0, max_val=E)
            with dve.If(unsorted != 0):
                own = Own(dve, v_step)
                nc.vector.memset(key_of[:, E:EPAD], float(N))
                dve.wait_ge(dst_loaded, 16)
                own.step(nc.vector.tensor_copy(key_of[:, 0:E], key_of[:, 0:E].bitcast(I32)))
                dve.wait_ge(made, 2)
                with dve.Fori(0, EPAD // P) as tile:
                    own.start(tile * (5 + 2 * parts) + 1)
                    block_keys = key_of[:, bass.ds(tile * P, P)]
                    own.step(nc.vector.tensor_tensor(own_block[:, :], block_keys, t.ident[:, :], ALU.mult))
                    nc.vector.reduce_sum(key[:, :], own_block[:, :], axis=AX.X)
                    own.step(nc.vector.tensor_tensor(block_keys, block_keys, ahead[:, :], ALU.add))
                    for i in range(parts):
                        w = EPAD // parts
                        own.step(nc.vector.tensor_scalar(below[:, :], key_of[:, i * w:(i + 1) * w], key[:, 0:1], None,
                                                         ALU.is_lt))
                        own.step(nc.vector.reduce_sum(part[:, i:i + 1], below[:, :], axis=AX.X))
                    own.step(nc.vector.tensor_tensor(block_keys, block_keys, behind[:, :], ALU.add))
                    own.step(nc.vector.reduce_sum(total[:, :], part[:, :], axis=AX.X))
                    dve.wait_ge(rank_free, tile + 1)
                    own.step(nc.vector.tensor_copy(rank[:, :], total[:, :]))
                    nc.vector.sem_inc(ranked, 1)

        @block.gpsimd
        def _(pool):
            unsorted = pool.value_load(t.unsorted[0:1, 0:1], min_val=0, max_val=E)
            with pool.If(unsorted != 0):
                nc.gpsimd.memset(ahead[:, :], -0.5).then_inc(filled, 1)
                nc.gpsimd.memset(behind[:, :], -0.5).then_inc(filled, 1)
                pool.wait_ge(filled, 2)
                nc.gpsimd.affine_select(out=ahead[:, :], in_=ahead[:, :], compare_op=ALU.is_ge, fill=0.0, base=-1,
                                        pattern=[[-1, P]], channel_multiplier=1).then_inc(made, 1)
                nc.gpsimd.affine_select(out=behind[:, :], in_=behind[:, :], compare_op=ALU.is_ge, fill=0.0, base=0,
                                        pattern=[[1, P]], channel_multiplier=-1).then_inc(made, 1)
                pool.sem_inc(rank_free, 1)

                def scatter(tile, r=P):
                    pool.dma_start(src_rows[0:r, :], src[bass.ds(tile * P, r)].unsqueeze(1)).then_inc(rows_loaded, 16)
                    pool.dma_start(dst_rows[0:r, :], dst[bass.ds(tile * P, r)].unsqueeze(1)).then_inc(rows_loaded, 16)
                    pool.dma_start(attr_rows[0:r, :], edge_attr[bass.ds(tile * P, r), :]).then_inc(rows_loaded, 16)
                    wait(pool, rows_loaded, tile * 48 + 48)
                    wait(pool, ranked, tile + 1)
                    for o, rows_ in ((d.src, src_rows), (d.dst, dst_rows), (d.attr, attr_rows)):
                        pool.indirect_dma_start(
                            out=o[:, :], out_offset=bass.IndirectOffsetOnAxis(ap=rank[:, 0:1], axis=0),
                            in_=rows_[:, :], in_offset=None, bounds_check=E - 1, oob_is_err=False
                        ).then_inc(scattered, 16)
                    wait(pool, scattered, tile * 48 + 48)
                    pool.sem_inc(rank_free, 1)

                with pool.Fori(0, E // P) as tile:
                    scatter(tile)
                scatter(E // P, E % P)




def tables(nc, t, w, d):
    r, full = TR, TF
    src, dst = (v.rearrange("e o -> (e o)") for v in (d.src, d.dst))
    with ExitStack() as ctx:
        a = Allocator(nc, ctx, "tables")
        cur, nxt, prv, s, gd, si = (a.sb(n, [r, TW], I32) for n in ("cur", "nxt", "prv", "src", "gdst", "sidx"))
        end, keep, start, last = a.sb("end", [r, TW]), a.sb("keep", [r, TW], BF16), a.sb("start", [r, TW], BF16), \
            a.sb("last", [r, TW], BF16)
        filled, loaded, step, done, stored = (a.sem(n) for n in ("filled", "loaded", "step", "done", "stored"))
        names = ("W_src", "W_dst", "W_edge", "W1", "W2")
        raw = [a.sb(f"raw_{n}", [P, P]) for n in names]
        heads = a.sb("heads", [P, P])
        bank = [a.ps(f"bank{i}", (P, P)) for i in range(len(names))]
        weights = a.sem("weights")
        pool_step, made, turned, copied, v_step = (a.sem(n) for n in ("pool_step", "made", "turned", "copied", "v_step"))
        block = ctx.enter_context(nc.Block())

        @block.gpsimd
        def _(pool):
            nc.gpsimd.memset(cur[:, :], N).then_inc(filled, 1)
            nc.gpsimd.memset(nxt[:, :], N).then_inc(filled, 1)
            nc.gpsimd.memset(prv[:, :], -1).then_inc(filled, 1)
            nc.gpsimd.memset(s[:, :], 0).then_inc(filled, 1)
            nc.gpsimd.memset(heads[:, :], 1.0).then_inc(pool_step, 1)
            nc.gpsimd.memset(t.ones_row[:, :], 1.0).then_inc(pool_step, 1)
            nc.gpsimd.memset(t.ones_row_bf[:, :], 1.0).then_inc(pool_step, 1)
            pool.wait_ge(pool_step, 3)
            nc.gpsimd.affine_select(out=heads[:, :], in_=heads[:, :], compare_op=ALU.is_ge, fill=0.0, base=0,
                                    pattern=[[-HEAD_DIM, HEADS], [0, HEAD_DIM]],
                                    channel_multiplier=1).then_inc(made, 1)
            pool.wait_ge(made, 1)
            nc.gpsimd.affine_select(out=heads[:, :], in_=heads[:, :], compare_op=ALU.is_ge, fill=0.0,
                                    base=HEAD_DIM - 1, pattern=[[HEAD_DIM, HEADS], [0, HEAD_DIM]],
                                    channel_multiplier=-1).then_inc(made, 1)

        @block.sync
        def _(sp):
            def load(tile, shift):
                values = src if tile is s else dst
                lead = 0
                if shift < 0:
                    sp.dma_start(tile[0:1, 1:TW], values[0:TW - 1].unsqueeze(0)).then_inc(loaded, 16)
                    lead = 1
                sp.dma_start(tile[lead:full, :],
                             values[lead * TW + shift:full * TW + shift].rearrange("(p e) -> p e", e=TW)
                             ).then_inc(loaded, 16)
                rest = E - full * TW - shift
                sp.dma_start(tile[full:full + 1, 0:rest], values[full * TW + shift:E].unsqueeze(0)
                             ).then_inc(loaded, 16)

            sp.wait_ge(filled, 4)
            load(cur, 0)
            load(nxt, 1)
            load(prv, -1)
            load(s, 0)
            for n, tile in zip(names, raw):
                sp.dma_start(tile[:, :], w[n]).then_inc(weights, 16)
            sp.wait_ge(done, 4)
            for tile, o in ((s, d.gather[0]), (gd, d.gather[1]), (si, d.scatter), (keep, d.keep), (start, d.start),
                            (last, d.last)):
                sp.dma_start(o.rearrange("(p e) -> p e", e=TW), tile[:, :]).then_inc(stored, 16)
            sp.wait_ge(stored, 6 * 16)

        @block.vector
        def _(dve):
            dve.wait_ge(loaded, 9 * 16)
            nc.vector.tensor_tensor(end[:, :], cur[:, :], nxt[:, :], ALU.is_equal).then_inc(step, 1)
            nc.vector.tensor_tensor(keep[:, :], cur[:, :], prv[:, :], ALU.is_equal).then_inc(step, 1)
            nc.vector.tensor_scalar(gd[:, :], cur[:, :], float(N - 1), None, ALU.min).then_inc(done, 1)
            dve.wait_ge(step, 2)
            nc.vector.tensor_scalar(start[:, :], keep[:, :], -1.0, FAR, ALU.add, ALU.mult).then_inc(done, 1)
            nc.vector.tensor_scalar(last[:, :], end[:, :], -FAR, None, ALU.mult).then_inc(done, 1)
            nc.vector.tensor_scalar(end[:, :], end[:, :], float(NOWHERE), None, ALU.mult).then_inc(step, 1)
            dve.wait_ge(step, 3)
            nc.vector.tensor_tensor(si[:, :], end[:, :], cur[:, :], ALU.add).then_inc(done, 1)
            dve.wait_ge(t.columns_loaded, 16 * len(t.columns))
            dve.wait_ge(made, 2)
            nc.vector.tensor_scalar(t.A_pos[:, :], heads[:, :], t.attn[:, 0:1], None, ALU.mult).then_inc(v_step, 1)
            dve.wait_ge(v_step, 1)
            nc.vector.tensor_scalar(t.A_neg[:, :], t.A_pos[:, :], -SLOPE, None, ALU.mult)
            nc.vector.tensor_tensor(t.b_sum[:, :], t.b_src[:, :], t.b_dst[:, :], ALU.add).then_inc(v_step, 1)
            dve.wait_ge(v_step, 2)
            nc.vector.tensor_scalar(t.b_sum_neg[:, :], t.b_sum[:, :], -1.0, None, ALU.mult)

        @block.tensor
        def _(pe):
            pe.wait_ge(weights, 16 * len(names))
            for tile, o in zip(raw, bank):
                nc.tensor.transpose(o[:, :], tile[:, :], t.ident[:, :]).then_inc(turned, 1)

        @block.scalar
        def _(act):
            for i, o in enumerate((t.W_srcT, t.W_dstT, t.W_edgeT, t.W1T, t.W2T)):
                act.wait_ge(turned, i + 1)
                nc.scalar.copy(o[:, :], bank[i][:, :]).then_inc(copied, 1)




class Tiny:

    def __init__(self, a, n, i=0):
        self.v, self.x, self.rstd, self.z, self.mean, self.shift = (
            a.sb(f"tiny_{k}{i}", [P, n]) for k in ("v", "x", "rstd", "z", "mean", "shift"))


NORM_STEPS = 14


def mean_var(nc, own, stats, lo, hi, tiny, meanwhile=iter(()), r=P):
    def c(tile):
        return tile[0:r, lo:hi]

    def s(i):
        return stats[0:r, lo:hi, i:i + 1].rearrange("p a b -> p (a b)")

    v, x, z = c(tiny.v), c(tiny.x), c(tiny.z)
    nc.vector.tensor_tensor(x, s(1), s(4), ALU.subtract)
    nc.vector.tensor_tensor(z, s(1), s(4), ALU.add)
    own.step(nc.vector.tensor_tensor(v, s(2), s(5), ALU.add), meanwhile)
    nc.vector.scalar_tensor_tensor(x, x, 0.25, x, ALU.mult, ALU.mult)
    nc.vector.tensor_scalar(c(tiny.mean), z, 0.5, None, ALU.mult)
    own.step(nc.vector.tensor_scalar(v, v, 1.0 / P, EPS, ALU.mult, ALU.add), meanwhile)
    return nc.vector.tensor_tensor(v, v, x, ALU.add)


def norm_scale(nc, own, stats, lo, hi, tiny, meanwhile=iter(()), r=P):
    v, x, y, z = (tile[0:r, lo:hi] for tile in (tiny.v, tiny.x, tiny.rstd, tiny.z))

    def step(instruction):
        own.step(instruction, meanwhile)

    step(mean_var(nc, own, stats, lo, hi, tiny, meanwhile, r))
    nc.vector.tensor_scalar(x, v, -0.5, None, ALU.mult)
    step(nc.vector.tensor_scalar(z.bitcast(I32), v.bitcast(I32), 1, None, ALU.logical_shift_right))
    step(nc.vector.tensor_scalar(y.bitcast(I32), z.bitcast(I32), -1.0, RSQRT_SEED, ALU.mult, ALU.add))
    for _ in range(3):
        step(nc.vector.tensor_tensor(z, y, y, ALU.mult))
        step(nc.vector.tensor_tensor(z, z, x, ALU.mult))
        step(nc.vector.scalar_tensor_tensor(y, z, 1.5, y, ALU.add, ALU.mult))




def attention(nc, t, d, x, edge_attr, out):
    with ExitStack() as ctx:
        a = Allocator(nc, ctx, "att")
        sb, ps, sem = a.sb, a.ps, a.sem

        def many(n, name, shape, dt=F32):
            return [sb(f"{name}{i}", shape, dt) for i in range(n)]

        def sems(name, n=2):
            return [sem(f"{name}{i}") for i in range(n)]

        idx, sidx = many(4, "idx", [P, 2, EQ], I32), many(2, "sidx", [P, EQ], I32)
        xs, xd, er = many(4, "xs", [P, EQ, P]), many(4, "xd", [P, EQ, P]), many(2, "er", [P, EQ, P])
        xn, xr, xrn = many(2, "xn", [P, 2 * EQ, P]), many(4, "xr", [P, DQ, P]), sb("xrn", [P, DQ, P])
        staged, direct_sidx = many(2, "staged", [P, EG]), sb("direct_sidx", [P, NEG - DIRECT, EQ], I32)
        stats, tiny = sb("stats", [P, 2 * EQ + DQ, 6]), [Tiny(a, 2 * EQ + DQ, i) for i in range(2)]
        eT, hsT, hdT, hrT = sb("eT", [P, EG]), sb("hsT", [P, EG]), sb("hdT", [P, EG]), sb("hrT", [P, DG])
        pos, neg = sb("pos", [P, EG]), sb("neg", [P, EG])
        start, last = many(2, "start", [P, EG], BF16), many(2, "last", [1, EG], BF16)
        before, gap, rise = (sb(n, [P, EG]) for n in ("before", "gap", "rise"))
        decay, weight, z, msg, h = (sb(n, [P, EG]) for n in ("decay", "weight", "z", "msg", "h"))
        carry, rz = sb("carry", [P, 1]), sb("rz", [P, EQ * HEADS])
        yd, y0 = sb("yd", [P, EG]), many(2, "y0", [P, DG])
        TP = [ps("TP0"), ps("TP1")]
        T, G, S, R, Y, ZT = (ps(n) for n in ("T", "G", "S", "R", "Y", "ZT"))

        s_idx, s_xs, s_xd, s_xr = sems("idx", 4), sems("xs", 4), sems("xd", 4), sems("xr", 4)
        s_er, s_start, s_last = sems("er"), sems("start"), sems("last")
        s_staged, s_sidx, s_scattered, s_y0_stored = sems("staged"), sems("sidx"), sems("scattered"), sems("y0_stored")
        copied, kept, s_direct, s_direct_scattered = (sem(n) for n in ("x_copied", "kept", "direct", "direct_scattered"))
        scaled, src_normed, dst_normed, node_normed = (sem(n) for n in ("scaled", "src_normed", "dst_normed",
                                                                        "node_normed"))
        tp_full, tp_free = sems("tp_full"), sems("tp_free")
        logits, signs, scores, before_done, gaps, exps = (sem(n) for n in ("logits", "signs", "scores", "before_done",
                                                                           "gaps", "exps"))
        g_full, msg_done, h_done, back, rz_done, new_done, x1_done = (
            sem(n) for n in ("g_full", "msg_done", "h_done", "back", "rz_done", "new_done", "x1_done"))
        y_full, y_free, y0_squared, yd_squared = sem("y_full"), sem("y_free"), sem("y0_squared"), sem("yd_squared")
        v_step = sem("v_step")

        gather_v = d.gather.rearrange("t (g p q) -> g p t q", p=P, q=EQ)
        scatter_v = d.scatter.rearrange("(g p q) -> g p q", p=P, q=EQ)
        x_full = x[0:(ND - 1) * DG, :].rearrange("(g p q) f -> g p (q f)", p=P, q=DQ)
        x_tail = x[(ND - 1) * DG:N, :].rearrange("(p q) f -> p (q f)", q=DQ)
        LAST = NEG - 1

        def height(g):
            return DTAIL if g.known and g.g == ND - 1 else P


        def edge_tp(g):
            if g.known and g.g == 0:
                return [(0, 0), (1, 0), (0, 1)]
            return [g.use(5, j - 2) for j in range(3)]

        def node_tp(g):
            return [g.use(5, 6 + j - 3 * (g.known and g.g == LAST)) for j in range(2)]

        block = ctx.enter_context(nc.Block())

        @block.sync
        def _(sp):
            def load_idx(g):
                k = g.k % 4
                sp.dma_start(idx[k][:, :, :], gather_v[bass.ds(g.g, 1)].rearrange("a p t q -> (a p) t q")
                             ).then_inc(s_idx[k], 16)

            def load_edges(g):
                k = g.k % 2
                for attr, chosen in ((edge_attr, unsorted == 0), (d.attr, unsorted != 0)):
                    with sp.If(chosen):
                        if g.known and g.g == LAST:
                            sp.dma_start(er[k][0:ETAIL // EQ].rearrange(FLAT),
                                         attr[LAST * EG:E, :].rearrange("(p q) f -> p (q f)", q=EQ)
                                         ).then_inc(s_er[k], 16)
                        else:
                            full = attr[0:LAST * EG, :].rearrange("(g p q) f -> g p (q f)", p=P, q=EQ)
                            sp.dma_start(er[k][:, :, :].rearrange(FLAT), rows(full, g.g)).then_inc(s_er[k], 16)
                sp.dma_start(start[k][:, :], d.start[bass.ds(g.times(EG), EG)].partition_broadcast(P)
                             ).then_inc(s_start[k], 16)
                sp.dma_start(last[k][:, :], d.last[bass.ds(g.times(EG), EG)].unsqueeze(0)).then_inc(s_last[k], 16)

            def load_nodes(g):
                k = g.k % 4
                if g.known and g.g == ND - 1:
                    sp.dma_start(xr[k][0:DTAIL].rearrange(FLAT), x_tail).then_inc(s_xr[k], 16)
                else:
                    sp.dma_start(xr[k][:, :, :].rearrange(FLAT), rows(x_full, g.g)).then_inc(s_xr[k], 16)

            def stage(g):
                k = g.k % 2
                wait(sp, s_scattered[k], g.half * 64)
                wait(sp, x1_done, g.g + 1)
                sp.dma_start(staged[k][:, :], t.x1[:, bass.ds(g.times(EG), EG)]).then_inc(s_staged[k], 16)
                sp.dma_start(sidx[k][:, :], rows(scatter_v, g.g)).then_inc(s_sidx[k], 16)

            def body(i):
                j = i + 3
                if is_group(i + 7):
                    wait(sp, s_xs[j.k % 4], j.quarter * 64 + 64)
                    wait(sp, s_xd[j.k % 4], j.quarter * 64 + 64)
                    load_idx(i + 7)
                if i.known and 0 <= i.g < COPIES:
                    n = N // COPIES
                    sp.dma_start(out[i.g * n:(i.g + 1) * n, :].rearrange("(a b) f -> a (b f)", b=COPY_ROWS),
                                 x[i.g * n:(i.g + 1) * n, :].rearrange("(a b) f -> a (b f)", b=COPY_ROWS)
                                 ).then_inc(copied, 16)
                if is_group(i + 2):
                    wait(sp, before_done, i.g + 1)
                    wait(sp, y_full, i.times(3, 1))
                    load_edges(group(i.g + 2) if i.known else i + 2)
                if is_group(i + 4):
                    wait(sp, node_normed, i.g + 1)
                    load_nodes(group(i.g + 4) if i.known else i + 4)
                k, w = i.k % 2, DQ * height(i)
                wait(sp, y_free, i.times(3, 3))
                sp.dma_start(d.y0[:, bass.ds(i.times(DG), w)], y0[k][:, 0:w]).then_inc(s_y0_stored[k], 16)
                if not i.known or STAGE_LAG <= i.g < DIRECT + STAGE_LAG:
                    stage(i - STAGE_LAG)

            unsorted = sp.value_load(t.unsorted[0:1, 0:1], min_val=0, max_val=E)
            for g in range(4):
                load_idx(group(g))
            for g in range(2):
                load_edges(group(g))
                load_nodes(group(g))
            sp.dma_start(direct_sidx[:, :, :], d.scatter[DIRECT * EG:].rearrange("(g p q) -> p g q", p=P, q=EQ)
                         ).then_inc(s_direct, 16)
            for g in range(3):
                wait(sp, s_xs[g], 64)
                wait(sp, s_xd[g], 64)
                load_idx(group(g + 4))
                if g < 2:
                    load_nodes(group(g + 2))
            unrolled(sp, 0, 16, 40, NEG, body)
            for i in range(2):
                wait(sp, s_y0_stored[i], 16 + 16 * len(range(i, ND, 2)))

        @block.gpsimd
        def _(pool):
            def gather(j):
                k = j.k % 4
                wait(pool, s_idx[k], j.quarter * 16 + 16)
                wait(pool, src_normed, j.g - 3)
                for q in range(EQ):
                    pool.indirect_dma_start(
                        out=xs[k][:, q, :], out_offset=None, in_=x[:, :],
                        in_offset=bass.IndirectOffsetOnAxis(ap=idx[k][:, 0, q:q + 1], axis=0)
                    ).then_inc(s_xs[k], 16)
                wait(pool, dst_normed, j.g - 3)
                wait(pool, kept, j.g - 3)
                for q in range(EQ):
                    pool.indirect_dma_start(
                        out=xd[k][:, q, :], out_offset=None, in_=x[:, :],
                        in_offset=bass.IndirectOffsetOnAxis(ap=idx[k][:, 1, q:q + 1], axis=0)
                    ).then_inc(s_xd[k], 16)

            def scatter(g):
                k = g.k % 2
                wait(pool, s_staged[k], g.half * 16 + 16)
                wait(pool, s_sidx[k], g.half * 16 + 16)
                for q in range(EQ):
                    pool.indirect_dma_start(
                        out=out[:, :], out_offset=bass.IndirectOffsetOnAxis(ap=sidx[k][:, q:q + 1], axis=0),
                        in_=staged[k][:, q * P:(q + 1) * P], in_offset=None, bounds_check=N - 1, oob_is_err=False
                    ).then_inc(s_scattered[k], 16)

            def both(j):
                gather(j)
                scatter(j - SCATTER_LAG)

            loop(pool, 0, SCATTER_LAG, gather, by_hand=4)
            wait(pool, copied, 16 * COPIES)
            loop(pool, SCATTER_LAG, NEG, both)
            wait(pool, s_direct, 16)
            for g in range(DIRECT, NEG):
                wait(pool, x1_done, g + 1)
                for q in range(EQ):
                    pool.indirect_dma_start(
                        out=out[:, :],
                        out_offset=bass.IndirectOffsetOnAxis(ap=direct_sidx[:, g - DIRECT, q:q + 1], axis=0),
                        in_=t.x1[:, g * EG + q * P:g * EG + (q + 1) * P], in_offset=None, bounds_check=N - 1,
                        oob_is_err=False).then_inc(s_direct_scattered, 16)
            wait(pool, s_direct_scattered, 64 * (NEG - DIRECT))
            for i in range(2):
                wait(pool, s_scattered[i], 64 * len(range(i, DIRECT, 2)))

        @block.vector
        def _(dve):
            own = Own(dve, v_step)
            nc.vector.memset(before[:, :], 0.0)
            nc.vector.memset(z[:, :], 0.0)
            nc.vector.memset(h[:, :], 0.0)
            own.step(nc.vector.memset(carry[:, :], 0.0))

            def statistics(e, n):
                if is_group(e):
                    k = e.k % 4
                    for m, tile, s in ((0, xs[k], s_xs[k]), (EQ, xd[k], s_xd[k])):
                        dve.wait_ge(s, e.quarter * 64 + 64)
                        for q in range(EQ):
                            yield nc.vector.bn_stats(stats[:, m + q, :], tile[:, q, :])
                if is_group(n):
                    k, r = n.k % 4, height(n)
                    dve.wait_ge(s_xr[k], n.quarter * 16 + 16)
                    for q in range(DQ):
                        yield nc.vector.bn_stats(stats[0:r, 2 * EQ + q, :], xr[k][0:r, q, :])

            def edge_norm(g, tile, m, done):
                s = tiny[g.k % 2]
                for q in range(EQ):
                    ins = nc.vector.tensor_scalar(xn[g.k % 2][:, m + q, :], tile[:, q, :], s.mean[:, m + q:m + q + 1],
                                                  s.rstd[:, m + q:m + q + 1], ALU.subtract, ALU.mult)
                    if q == EQ - 1:
                        ins.then_inc(done, 1)
                    yield

            def score_scan(g, tiles):
                k = g.k % 2
                dve.wait_ge(s_start[k], g.half * 16 + 16)
                own.step(nc.vector.tensor_tensor(before[:, 0:1], carry[:, :], start[k][:, 0:1], ALU.add), tiles)
                dve.wait_ge(scores, g.g + 1)
                nc.vector.tensor_tensor_scan(before[:, 1:EG], S[:, 0:EG - 1], start[k][:, 1:EG],
                                             before[:, 0:1], ALU.max, ALU.add).then_inc(before_done, 1)
                next(tiles, None)
                dve.wait_ge(before_done, g.g + 1)
                nc.vector.tensor_tensor(gap[:, :], S[:, :], before[:, :], ALU.subtract)
                own.step(nc.vector.tensor_tensor(carry[:, :], S[:, EG - 1:EG], before[:, EG - 1:EG], ALU.max), tiles)
                nc.vector.tensor_scalar(rise[:, :], gap[:, :], 0.0, None, ALU.max)
                nc.vector.tensor_scalar(gap[:, :], gap[:, :], 0.0, None, ALU.min).then_inc(gaps, 1)

            def new_rows(g):
                dve.wait_ge(back, g.g + 1)
                nc.vector.reciprocal(rz[:, :], ZT[:, 0:EG:HEAD_DIM]).then_inc(rz_done, 1)
                yield
                dve.wait_ge(rz_done, g.g + 1)
                nc.vector.scalar_tensor_tensor(
                    msg[:, :].rearrange("p (a c) -> p a c", c=HEAD_DIM),
                    R[:, :].rearrange("p (a c) -> p a c", c=HEAD_DIM), 0.0,
                    rz[:, :].unsqueeze(2).to_broadcast([P, EQ * HEADS, HEAD_DIM]),
                    ALU.max, ALU.mult).then_inc(new_done, 1)
                yield
                dve.wait_ge(new_done, g.g + 1)
                dve.wait_ge(kept, g.g + 1)
                o = t.x1[:, bass.ds(g.times(EG), EG)]
                nc.vector.tensor_tensor(o, msg[:, :], o, ALU.add).then_inc(x1_done, 1)
                yield

            def sum_scan(g):
                dve.wait_ge(exps, g.g + 1)
                nc.vector.tensor_tensor_scan(z[:, :], decay[:, :], weight[:, :], z[:, EG - 1:EG], ALU.mult, ALU.add)
                yield
                dve.wait_ge(g_full, g.g + 1)
                wait(dve, x1_done, g.g)
                nc.vector.scalar_tensor_tensor(msg[:, :], G[:, :], t.b_src[:, 0:1], weight[:, :],
                                               ALU.add, ALU.mult).then_inc(msg_done, 1)
                yield
                dve.wait_ge(msg_done, g.g + 1)
                nc.vector.tensor_tensor_scan(h[:, :], decay[:, :], msg[:, :], h[:, EG - 1:EG],
                                             ALU.mult, ALU.add).then_inc(h_done, 1)
                yield

            def wide(i):
                e = i + 2
                if is_group(e):
                    yield from edge_norm(e, xs[e.k % 4], 0, src_normed)
                if is_group(i - 1):
                    yield from new_rows(i - 1)
                if is_group(i):
                    yield from sum_scan(i)
                if is_group(e):
                    yield from edge_norm(e, xd[e.k % 4], EQ, dst_normed)

            def body(i):
                tiles = statistics(i + 3, i + 2)
                if is_group(i):
                    score_scan(i, tiles)
                ins = None
                for ins in tiles:
                    pass
                rest = wide(i)
                if ins is not None:
                    own.step(ins)
                    lo, hi = 0 if is_group(i + 3) else 2 * EQ, 2 * EQ + DQ if is_group(i + 2) else 2 * EQ
                    r = P if is_group(i + 3) else height(i + 2)
                    s = tiny[(i.k + 1) % 2]
                    wait(dve, node_normed, i.g + 1)
                    norm_scale(nc, own, stats, lo, hi, s, rest, r)
                    c = (slice(0, r), slice(2 * EQ, hi))
                    if hi > 2 * EQ:
                        nc.vector.scalar_tensor_tensor(s.shift[c], s.mean[c], -1.0, s.rstd[c], ALU.mult,
                                                       ALU.mult).then_inc(scaled, 1)
                for _ in rest:
                    pass

            lo, hi, per = 4, 44, NORM_STEPS + 3
            for g in range(-3, lo):
                body(group(g))
            first = own.base + own.k - lo * per
            with dve.Fori(lo // 4, hi // 4) as turn:
                for k in range(4):
                    i = Group(turn, k)
                    own.start(i.times(per, first))
                    body(i)
                    assert own.k == per
            own.start(hi * per + first)
            for g in range(hi, NEG + 1):
                body(group(g))

        @block.tensor
        def _(pe):
            def turn(tile, first, use, r=P, strided=True):
                b, n = use
                wait(pe, tp_free[b], n)
                for q in range(EQ):
                    o = TP[b][:, q:EG:EQ] if strided else TP[b][:, q * r:(q + 1) * r]
                    ins = nc.tensor.transpose(o, tile[0:r, first + q, :], t.ident[0:r, 0:r])
                ins.then_inc(tp_full[b], 1)

            def edge_logits(g):
                uses, k = edge_tp(g), g.k % 2
                pe.wait_ge(s_er[k], g.half * 16 + 16)
                turn(er[k], 0, uses[0])
                pe.wait_ge(src_normed, g.g + 1)
                turn(xn[k], 0, uses[1])
                pe.wait_ge(dst_normed, g.g + 1)
                turn(xn[k], EQ, uses[2])
                wait(pe, y_free, g.times(3, -3))
                for j, W, hT in ((0, t.W_edgeT, eT), (1, t.W_srcT, hsT), (2, t.W_dstT, hdT)):
                    b, n = uses[j]
                    pe.wait_ge(tp_free[b], n + 1)
                    ins = nc.tensor.matmul(T[:, :], W[:, :], hT[:, :], start=j == 0, stop=j == 2)
                ins.then_inc(logits, 1)

            def edge_scores(g):
                pe.wait_ge(signs, g.times(2, 1))
                wait(pe, gaps, g.g)
                nc.tensor.matmul(S[:, :], t.A_pos[:, :], pos[:, :], start=True, stop=False)
                pe.wait_ge(signs, g.times(2, 2))
                nc.tensor.matmul(S[:, :], t.A_neg[:, :], neg[:, :], start=False, stop=True).then_inc(scores, 1)

            def edge_summands(g):
                wait(pe, msg_done, g.g)
                nc.tensor.matmul(G[:, :], t.W_srcT[:, :], hsT[:, :], start=True, stop=False)
                nc.tensor.matmul(G[:, :], t.W_edgeT[:, :], eT[:, :], start=False, stop=True).then_inc(g_full, 1)

            def own_part(g):
                wait(pe, y_free, g.times(3, -1))
                pe.wait_ge(s_last[g.k % 2], g.half * 16 + 16)
                nc.tensor.matmul(Y[:, :], t.W1T[:, :], hdT[:, :], start=True, stop=False)
                nc.tensor.matmul(Y[:, :], t.ones_row_bf[:, :], last[g.k % 2][:, :], start=False,
                                 stop=True).then_inc(y_full, 1)

            def back_rows(g):
                pe.wait_ge(h_done, g.g + 1)
                wait(pe, new_done, g.g)
                for q in range(EQ):
                    nc.tensor.transpose(R[:, q * P:(q + 1) * P], h[:, q:EG:EQ], t.ident[:, :])
                for q in range(EQ):
                    ins = nc.tensor.transpose(ZT[:, q * P:(q + 1) * P], z[:, q:EG:EQ], t.ident[:, :])
                ins.then_inc(back, 1)

            def node_turn(i):
                pe.wait_ge(node_normed, i.g + 1)
                for m, use in enumerate(node_tp(i)):
                    turn(xrn, m * EQ, use, r=height(i), strided=False)

            def node_product(i):
                w = EQ * height(i)
                for m, (b, n) in enumerate(node_tp(i)):
                    pe.wait_ge(tp_free[b], n + 1)
                    if m == 0:
                        pe.wait_ge(y_free, i.times(3, 1))
                    nc.tensor.matmul((Y, T)[m][:, 0:w], t.W1T[:, :], hrT[:, m * w:(m + 1) * w],
                                     start=True, stop=True).then_inc(y_full, 1)

            def body(i):
                e = i + 1
                if is_group(e):
                    edge_logits(group(e.g) if e.known else e)
                if is_group(i):
                    node_turn(i)
                if is_group(e):
                    edge_scores(e)
                if is_group(i):
                    node_product(i)
                if is_group(e):
                    edge_summands(e)
                if is_group(e):
                    own_part(e)
                if is_group(i):
                    back_rows(i)

            unrolled(pe, -1, 4, 44, NEG, body)

        @block.scalar
        def _(act):
            for i in range(2):
                act.sem_inc(s_y0_stored[i], 16)

            def evacuate(o, func, use, w=EG):
                b, n = use
                act.wait_ge(tp_full[b], n + 1)
                nc.scalar.activation(o, TP[b][:, 0:w], func).then_inc(tp_free[b], 1)

            def edge_rows(g):
                for o, func, use in zip((eT, hsT, hdT), (ACT.Copy, ACT.Relu, ACT.Relu), edge_tp(g)):
                    evacuate(o[:, :], func, use)

            def softmax(g):
                act.wait_ge(gaps, g.g + 1)
                nc.scalar.activation(decay[:, :], rise[:, :], ACT.Exp, scale=-1.0)
                nc.scalar.activation(weight[:, :], gap[:, :], ACT.Exp).then_inc(exps, 1)

            def both_signs(g):
                act.wait_ge(logits, g.g + 1)
                nc.scalar.activation(pos[:, :], T[:, :], ACT.Relu, bias=t.b_sum[:, 0:1]).then_inc(signs, 1)
                nc.scalar.activation(neg[:, :], T[:, :], ACT.Relu, bias=t.b_sum_neg[:, 0:1],
                                     scale=-1.0).then_inc(signs, 1)

            def node_rows(i):
                w = EQ * height(i)
                for m, use in enumerate(node_tp(i)):
                    evacuate(hrT[:, m * w:(m + 1) * w], ACT.Relu, use, w)

            def node_hidden(i):
                k, w = i.k % 2, EQ * height(i)
                act.wait_ge(s_y0_stored[k], i.half * 16 + 16)
                for m in range(2):
                    act.wait_ge(y_full, i.times(3, 2 + m))
                    nc.scalar.activation(y0[k][:, m * w:(m + 1) * w], (Y, T)[m][:, 0:w], ACT.Relu, bias=t.b1[:, 0:1],
                                         accum_out=t.col("node", i.times(2, m))).then_inc(y_free, 1)

            def own_hidden(g):
                act.wait_ge(y_full, g.times(3, 1))
                nc.scalar.activation(yd[:, :], Y[:, :], ACT.Relu, bias=t.b1[:, 0:1],
                                     accum_out=t.col("edge_old", g.g)).then_inc(y_free, 1)

            def node_norm(i):
                k, r = i.k % 4, height(i)
                s = tiny[(i.k + 1) % 2]
                act.wait_ge(scaled, i.g + 1)
                act.wait_ge(s_xr[k], i.quarter * 16 + 16)
                for q in range(DQ):
                    m = 2 * EQ + q
                    ins = nc.scalar.activation(xrn[0:r, q, :], xr[k][0:r, q, :], ACT.Identity,
                                               bias=s.shift[0:r, m:m + 1], scale=s.rstd[0:r, m:m + 1])
                ins.then_inc(node_normed, 1)

            def keep_rows(g):
                act.wait_ge(s_xd[g.k % 4], g.quarter * 64 + 64)
                nc.scalar.copy(t.x1[:, bass.ds(g.times(EG), EG)], xd[g.k % 4][:, :, :].rearrange(FLAT)
                               ).then_inc(kept, 1)

            def squares(i):
                e, w = i + 1, DQ * height(i)
                if is_group(e):
                    act.wait_ge(y_free, e.times(3, 1))
                    nc.scalar.activation(yd[:, :], yd[:, :], ACT.Square,
                                         accum_out=t.col("edge_old_sq", e.g)).then_inc(yd_squared, 1)
                if is_group(i):
                    act.wait_ge(y_free, i.times(3, 3))
                    nc.scalar.activation(hrT[:, 0:w], y0[i.k % 2][:, 0:w], ACT.Square,
                                         accum_out=t.col("node_sq", i.g)).then_inc(y0_squared, 1)

            def body(i):
                e = group(i.g + 1) if i.known else i + 1
                if is_group(i + 2):
                    keep_rows(i + 2)
                if is_group(i):
                    softmax(i)
                if is_group(e):
                    edge_rows(e)
                if is_group(i):
                    wait(act, yd_squared, i.g)
                    own_hidden(i)
                squares(i - 1)
                if is_group(e):
                    both_signs(e)
                if is_group(i):
                    wait(act, y0_squared, i.g)
                    node_rows(i)
                if is_group(e):
                    node_norm(e)
                if is_group(i):
                    node_hidden(i)

            unrolled(act, -2, 4, 44, NEG, body)
            squares(group(LAST))


class Ahead:

    def __init__(self, a, d, x):
        self.d = d
        self.xr, self.y0 = ([a.sb(f"{n}{i}", [P, DG]) for i in range(4)] for n in ("xr", "y0"))
        self.y1 = a.sb("y1", [P, (NEG - RESIDENT) * EG])
        self.need, self.where = a.sb("need", [1, NEG], I32), a.sb("where", [P, NEG, EQ], I32)
        self.s_xr, self.s_y0 = ([a.sem(f"{n}{i}") for i in range(4)] for n in ("xr_loaded", "y0_loaded"))
        self.s_need, self.s_where = a.sem("need_loaded"), a.sem("where_loaded")
        self.x_full = x[0:(ND - 1) * DG, :].rearrange("(g p q) f -> g p (q f)", p=P, q=DQ)
        self.x_tail = x[(ND - 1) * DG:N, :].rearrange("(p q) f -> p (q f)", q=DQ)

    def load(self, sp, g):
        k, d = g.k % 4, self.d
        if g.known and g.g == ND - 1:
            sp.dma_start(self.xr[k][0:DTAIL, :], self.x_tail).then_inc(self.s_xr[k], 16)
            sp.dma_start(self.y0[k][:, 0:DTAIL * DQ], d.y0[:, (ND - 1) * DG:N]).then_inc(self.s_y0[k], 16)
        else:
            sp.dma_start(self.xr[k][:, :], rows(self.x_full, g.g)).then_inc(self.s_xr[k], 16)
            sp.dma_start(self.y0[k][:, :], d.y0[:, bass.ds(g.times(DG), DG)]).then_inc(self.s_y0[k], 16)

    def load_ahead(self, sp, g):
        if g >= 0:
            self.load(sp, group(g))
            return
        sp.dma_start(self.need[:, :], self.d.gather[1].rearrange("(g e) -> e g", e=EG)[EG - 1:EG, :],
                     allow_slow_non_contiguous=True).then_inc(self.s_need, 16)
        sp.dma_start(self.where[:, :, :], self.d.scatter.rearrange("(g p q) -> p g q", p=P, q=EQ)
                     ).then_inc(self.s_where, 16)




def aggregation(nc, t, r, d, out):
    with ExitStack() as ctx:
        a = Allocator(nc, ctx, "agg")
        sb, ps, sem = a.sb, a.ps, a.sem

        def sems(name, n=2):
            return [sem(f"{name}{i}") for i in range(n)]

        def two(name, shape, dt=F32):
            return [sb(f"{name}{i}", shape, dt) for i in range(2)]

        idx = [sb(f"idx{i}", [P, EQ], I32) for i in range(4)]
        xs = [sb(f"xs{i}", [P, EQ, P]) for i in range(4)]
        xsn, xdn, hsT, hdT, agg, y = (two("xsn", [P, EQ, P]), two("xdn", [P, EQ, P]), two("hsT", [P, EG]),
                                      two("hdT", [P, EG]), two("agg", [P, EG]), two("y", [P, EG]))
        keep, last, junk = two("keep", [P, EG], BF16), two("last", [1, EG], BF16), sb("junk", [P, EG])
        stats, tiny = sb("stats", [P, 2 * EQ, 6]), [Tiny(a, 2 * EQ, i) for i in range(2)]
        TS, TD, Y = [ps("TS0"), ps("TS1")], [ps("TD0"), ps("TD1")], [ps("Y0"), ps("Y1")]
        s_idx, s_xs, s_keep, s_last, s_stored = sems("idx", 4), sems("xs", 4), sems("keep"), sems("last"), sems("stored")
        var_done, root, scaled, src_normed, dst_normed, turned, hs_done, hd_done, agg_done = (
            sem(n) for n in ("var_done", "root", "scaled", "src_normed", "dst_normed", "turned", "hs_done", "hd_done",
                             "agg_done"))
        y_full, y_done, squared, v_step = (sem(n) for n in ("y_full", "y_done", "squared", "v_step"))
        gather_v = d.gather[0].rearrange("(g p q) -> g p q", p=P, q=EQ)
        block = ctx.enter_context(nc.Block())

        @block.sync
        def _(sp):
            def load_idx(g):
                sp.dma_start(idx[g.k % 4][:, :], rows(gather_v, g.g)).then_inc(s_idx[g.k % 4], 16)

            def load_masks(g):
                k = g.k % 2
                sp.dma_start(keep[k][:, :], d.keep[bass.ds(g.times(EG), EG)].partition_broadcast(P)
                             ).then_inc(s_keep[k], 16)
                sp.dma_start(last[k][:, :], d.last[bass.ds(g.times(EG), EG)].unsqueeze(0)).then_inc(s_last[k], 16)

            def body(i):
                known = i.known
                if not known or i.g + 6 < NEG:
                    j = i + 2
                    wait(sp, s_xs[j.k % 4], j.quarter * 64 + 64)
                    load_idx(i + 6)
                wait(sp, y_done, i.g + 1)
                if not known or i.g + 2 < NEG:
                    load_masks(i + 2)
                if known and 3 <= i.g < 8:
                    r.load_ahead(sp, i.g - 4)
                if not resident(i):
                    sp.dma_start(d.y1[:, bass.ds(i.times(EG), EG)], y[i.k % 2][:, :]).then_inc(s_stored[i.k % 2], 16)

            for g in range(4):
                load_idx(group(g))
            for g in range(2):
                load_masks(group(g))
            for g in range(2):
                wait(sp, s_xs[g], 64)
                load_idx(group(g + 4))
            unrolled(sp, 0, 8, RESIDENT, NEG, body)
            for i in range(2):
                wait(sp, s_stored[i], 16 + 16 * len(range(i, RESIDENT, 2)))

        @block.gpsimd
        def _(pool):
            def gather(j):
                k = j.k % 4
                wait(pool, s_idx[k], j.quarter * 16 + 16)
                wait(pool, src_normed, j.g - 3)
                for q in range(EQ):
                    pool.indirect_dma_start(
                        out=xs[k][:, q, :], out_offset=None, in_=out[:, :],
                        in_offset=bass.IndirectOffsetOnAxis(ap=idx[k][:, q:q + 1], axis=0)).then_inc(s_xs[k], 16)

            loop(pool, 0, NEG, gather, by_hand=4)

        @block.vector
        def _(dve):
            own = Own(dve, v_step)

            def scan(g):
                k = g.k % 2
                dve.wait_ge(s_keep[k], g.half * 16 + 16)
                dve.wait_ge(hs_done, g.g + 1)
                wait(dve, agg_done, g.g)
                nc.vector.tensor_tensor_scan(agg[k][:, :], keep[k][:, :], hsT[k][:, :], agg[1 - k][:, EG - 1:EG],
                                             ALU.mult, ALU.add).then_inc(agg_done, 1)

            def scales(g):
                s = tiny[g.k % 2]
                c = (slice(0, P), slice(EQ, 2 * EQ))
                dve.wait_ge(root, g.g + 1)
                own.step(nc.vector.reciprocal(s.rstd[:, :], s.x[:, :]))
                nc.vector.scalar_tensor_tensor(s.shift[c], s.mean[c], -1.0, s.rstd[c], ALU.mult,
                                               ALU.mult).then_inc(scaled, 1)

            def wide(i):
                if is_group(i):
                    scan(i)
                    yield
                if is_group(i + 1):
                    k = (i + 1).k % 2
                    for q in range(EQ):
                        ins = nc.vector.tensor_scalar(xsn[k][:, q, :], xs[(i + 1).k % 4][:, q, :],
                                                      tiny[k].mean[:, q:q + 1], tiny[k].rstd[:, q:q + 1],
                                                      ALU.subtract, ALU.mult)
                        if q == EQ - 1:
                            ins.then_inc(src_normed, 1)
                        yield

            def body(i):
                e = i + 2
                if is_group(i + 1):
                    scales(i + 1)
                rest = wide(i)
                if is_group(e):
                    for q in range(EQ):
                        nc.vector.bn_stats(stats[:, EQ + q, :], t.x1[:, bass.ds(e.times(EG, q * P), P)])
                    dve.wait_ge(s_xs[e.k % 4], e.quarter * 64 + 64)
                    for q in range(EQ):
                        ins = nc.vector.bn_stats(stats[:, q, :], xs[e.k % 4][:, q, :])
                    own.step(ins, rest)
                    wait(dve, dst_normed, i.g + 1)
                    mean_var(nc, own, stats, 0, 2 * EQ, tiny[i.k % 2], rest).then_inc(var_done, 1)
                for _ in rest:
                    pass

            nc.vector.memset(agg[1][:, :], 0.0)
            lo, hi, per = 4, 44, 4
            for g in range(-2, lo):
                body(group(g))
            first = own.base + own.k - lo * per
            with dve.Fori(lo // 4, hi // 4) as turn:
                for k in range(4):
                    i = Group(turn, k)
                    own.start(i.times(per, first))
                    body(i)
                    assert own.k == per
            own.start(hi * per + first)
            for g in range(hi, NEG):
                body(group(g))

        @block.tensor
        def _(pe):
            def turn(g):
                for rows_, normed, bank in ((xsn, src_normed, TS), (xdn, dst_normed, TD)):
                    pe.wait_ge(normed, g.g + 1)
                    for q in range(EQ):
                        ins = nc.tensor.transpose(bank[g.k % 2][:, q:EG:EQ], rows_[g.k % 2][:, q, :], t.ident[:, :])
                    ins.then_inc(turned, 1)

            def product(g):
                k = g.k % 2
                pe.wait_ge(s_last[k], g.half * 16 + 16)
                pe.wait_ge(hd_done, g.g + 1)
                nc.tensor.matmul(Y[k][:, :], t.W1T[:, :], hdT[k][:, :], start=True, stop=False)
                nc.tensor.matmul(Y[k][:, :], t.ones_row_bf[:, :], last[k][:, :], start=False, stop=False)
                pe.wait_ge(agg_done, g.g + 1)
                nc.tensor.matmul(Y[k][:, :], t.W1T[:, :], agg[k][:, :], start=False, stop=True).then_inc(y_full, 1)

            def body(i):
                if is_group(i):
                    product(i)
                if is_group(i + 1):
                    turn(i + 1)

            unrolled(pe, -1, 4, 44, NEG, body)

        @block.scalar
        def _(act):
            for i in range(2):
                act.sem_inc(s_stored[i], 16)

            def evacuate(g):
                k = g.k % 2
                act.wait_ge(turned, g.times(2, 1))
                nc.scalar.activation(hsT[k][:, :], TS[k][:, :], ACT.Relu).then_inc(hs_done, 1)
                act.wait_ge(turned, g.times(2, 2))
                nc.scalar.activation(hdT[k][:, :], TD[k][:, :], ACT.Relu).then_inc(hd_done, 1)

            def hidden_of(g):
                if resident(g):
                    return r.y1[:, bass.ds(g.times(EG, -RESIDENT * EG), EG)]
                return y[g.k % 2][:, :]

            def hidden(g):
                k = g.k % 2
                if not resident(g):
                    act.wait_ge(s_stored[k], g.half * 16 + 16)
                act.wait_ge(y_full, g.g + 1)
                nc.scalar.activation(hidden_of(g), Y[k][:, :], ACT.Relu, bias=t.b1[:, 0:1],
                                     accum_out=t.col("edge_new", g.g)).then_inc(y_done, 1)

            def dst_norm(g):
                s = tiny[g.k % 2]
                act.wait_ge(scaled, g.g + 1)
                for q in range(EQ):
                    m = EQ + q
                    ins = nc.scalar.activation(xdn[g.k % 2][:, q, :], t.x1[:, bass.ds(g.times(EG, q * P), P)],
                                               ACT.Identity, bias=s.shift[:, m:m + 1], scale=s.rstd[:, m:m + 1])
                ins.then_inc(dst_normed, 1)

            def square(g):
                act.wait_ge(y_done, g.g + 1)
                wait(act, squared, g.g)
                nc.scalar.activation(junk[:, :], hidden_of(g), ACT.Square,
                                     accum_out=t.col("edge_new_sq", g.g)).then_inc(squared, 1)

            def body(i):
                if is_group(i + 1):
                    dst_norm(i + 1)
                if is_group(i + 2):
                    act.wait_ge(var_done, i.g + 3)
                    s = tiny[i.k % 2]
                    nc.scalar.activation(s.x[:, :], s.v[:, :], ACT.Sqrt).then_inc(root, 1)
                if is_group(i + 1):
                    evacuate(i + 1)
                if is_group(i):
                    hidden(i)
                    square(i)

            unrolled(act, -2, 4, RESIDENT, RESIDENT, body)
            unrolled(act, RESIDENT, RESIDENT, 44, NEG, body)




class BatchNorm:

    def __init__(self, nc, a, t):
        self.nc, self.t = nc, t
        self.part, self.tot, self.c = a.sb("bn_part", [P, 6]), a.sb("bn_tot", [P, 2]), a.sb("bn_c", [P, 8])
        self.ones, self.shift, self.bank = a.sb("bn_ones", [P, P]), a.sb("bn_shift", [P, P]), a.ps("bn_bank", (P, P))
        self.v_step, self.var_done, self.root, self.folded, self.product, self.row_done = (
            a.sem(n) for n in ("v_step", "var_done", "root", "folded", "product", "row_done"))

    def vector(self, dve):
        nc, t, part, tot, c, ones, shift = self.nc, self.t, self.part, self.tot, self.c, self.ones, self.shift
        own = Own(dve, self.v_step)
        for i, n in enumerate(("node", "edge_old", "edge_new", "node_sq", "edge_old_sq", "edge_new_sq")):
            o, w = t.cols[n]
            nc.vector.reduce_sum(part[:, i:i + 1], t.sums[:, o:o + w], axis=AX.X)
        own.step(nc.vector.memset(ones[:, :], 1.0))
        for i in range(2):
            ins = nc.vector.tensor_tensor(tot[:, i:i + 1], part[:, 3 * i + 2:3 * i + 3], part[:, 3 * i + 1:3 * i + 2],
                                          ALU.subtract)
        own.step(ins)
        for i in range(2):
            ins = nc.vector.tensor_tensor(tot[:, i:i + 1], tot[:, i:i + 1], part[:, 3 * i:3 * i + 1], ALU.add)
        own.step(ins)
        mean, sq, var, rstd, s, sh = (c[:, i:i + 1] for i in range(6))
        own.step(nc.vector.tensor_scalar(c[:, 0:2], tot[:, 0:2], 1.0 / N, None, ALU.mult))
        own.step(nc.vector.tensor_tensor(var, mean, mean, ALU.mult))
        own.step(nc.vector.tensor_tensor(var, sq, var, ALU.subtract))
        nc.vector.tensor_scalar(var, var, 0.0, EPS, ALU.max, ALU.add).then_inc(self.var_done, 1)
        dve.wait_ge(self.root, 1)
        own.step(nc.vector.reciprocal(rstd, rstd))
        own.step(nc.vector.tensor_tensor(s, rstd, t.gamma[:, :], ALU.mult))
        nc.vector.tensor_scalar(t.W2s[:, :], t.W2T[:, :], s, None, ALU.mult)
        own.step(nc.vector.tensor_tensor(sh, mean, s, ALU.mult))
        own.step(nc.vector.tensor_tensor(sh, t.beta[:, :], sh, ALU.subtract))
        nc.vector.tensor_scalar(shift[:, :], ones[:, :], sh, None, ALU.mult).then_inc(self.folded, 1)
        dve.wait_ge(self.product, 1)
        nc.vector.tensor_copy(t.b_row[:, :], self.bank[:, :]).then_inc(self.row_done, 1)
        dve.wait_ge(self.row_done, 1)

    def scalar(self, act):
        act.wait_ge(self.var_done, 1)
        self.nc.scalar.activation(self.c[:, 3:4], self.c[:, 2:3], ACT.Sqrt).then_inc(self.root, 1)

    def tensor(self, pe):
        nc, t = self.nc, self.t
        pe.wait_ge(self.folded, 1)
        nc.tensor.matmul(self.bank[:, :], self.shift[:, :], t.W2T[:, :], start=True, stop=False)
        nc.tensor.matmul(self.bank[:, :], t.ones_row[:, :], t.b2_row[:, :], start=False,
                         stop=True).then_inc(self.product, 1)




def result(nc, t, r, d, out):
    with ExitStack() as ctx:
        a = Allocator(nc, ctx, "out")
        sb, ps, sem = a.sb, a.ps, a.sem

        def sems(name, n=2):
            return [sem(f"{name}{i}") for i in range(n)]

        xr, y0, s_xr, s_y0, need, where = r.xr, r.y0, r.s_xr, r.s_y0, r.need, r.where
        y1 = [sb(f"y1{i}", [P, EG]) for i in range(4)]
        staged = [sb(f"staged{i}", [P, EG]) for i in range(4)]
        sidx = [sb(f"sidx{i}", [P, EQ], I32) for i in range(4)]
        D, Z = [ps(f"D{i}") for i in range(4)], [ps(f"Z{i}") for i in range(2)]
        s_y1, s_out = sems("y1", 4), sems("stored", 4)
        need_step, need_done = sem("need_step"), sem("need_done")
        s_scattered, s_staged = sems("scattered", 4), sem("staged")
        node_full, edge_full, node_done, edge_done, biased, nodes_written = (
            sem(n) for n in ("node_full", "edge_full", "node_done", "edge_done", "biased", "nodes_written"))
        o_full = out[0:(ND - 1) * DG, :].rearrange("(g p q) f -> g p (q f)", p=P, q=DQ)
        o_tail = out[(ND - 1) * DG:N, :].rearrange("(p q) f -> p (q f)", q=DQ)
        TAIL = group(ND - 1)
        batch_norm = BatchNorm(nc, a, t)
        block = ctx.enter_context(nc.Block())

        @block.sync
        def _(sp):
            def load_y1(g):
                if not resident(g):
                    k = g.k % 4
                    sp.dma_start(y1[k][:, :], d.y1[:, bass.ds(g.times(EG), EG)]).then_inc(s_y1[k], 16)

            def body(i):
                k = i.k % 4
                known = i.known
                wait(sp, node_done, i.g + 1)
                if known and i.g == ND - 1:
                    sp.dma_start(o_tail, xr[k][0:DTAIL, :]).then_inc(s_out[k], 16)
                else:
                    sp.dma_start(rows(o_full, i.g), xr[k][:, :]).then_inc(s_out[k], 16)
                if not known or i.g >= 1:
                    wait(sp, s_out[(i.k - 1) % 4], (i - 1).quarter * 16 + 16)
                    sp.sem_inc(nodes_written, 1)
                    if not known or i.g + 3 < ND:
                        wait(sp, edge_done, i.g)
                        j = group(i.g + 3) if known else i + 3
                        r.load(sp, j)
                        load_y1(j)

            for g in range(4):
                load_y1(group(g))
            unrolled(sp, 0, 4, RESIDENT - 4, ND, body)
            wait(sp, s_out[(ND - 1) % 4], TAIL.quarter * 16 + 16)
            sp.sem_inc(nodes_written, 1)

        @block.vector
        def _(dve):
            batch_norm.vector(dve)
            dve.wait_ge(r.s_need, 16)
            nc.vector.tensor_scalar(need[:, :], need[:, :], DG.bit_length() - 1, None,
                                    ALU.logical_shift_right).then_inc(need_step, 1)
            dve.wait_ge(need_step, 1)
            nc.vector.tensor_scalar(need[:, :], need[:, :], 1.0, None, ALU.add).then_inc(need_done, 1)

            def nodes(i, n=P):
                k, w = i.k % 4, DQ * P // 2
                dve.wait_ge(s_xr[k], i.quarter * 16 + 16)
                v = xr[k][0:n, :].rearrange("p (q f) -> p q f", f=P)
                nc.vector.tensor_tensor(v, v, t.b_row[0:n, :].unsqueeze(1).to_broadcast([n, DQ, P]),
                                        ALU.add).then_inc(biased, 1)
                dve.wait_ge(biased, i.times(2, 1))
                for m in range(2):
                    dve.wait_ge(node_full, i.times(2, m + 1))
                    o = xr[k][0:n, m * w:(m + 1) * w]
                    ins = nc.vector.tensor_tensor(o, D[(2 * i.k + m) % 4][0:n, :], o, ALU.add)
                ins.then_inc(node_done, 1)

            def edges(i):
                o = t.x1[:, bass.ds(i.times(EG), EG)]
                v = o.rearrange("p (q f) -> p q f", f=P)
                nc.vector.tensor_tensor(v, v, t.b_row[:, :].unsqueeze(1).to_broadcast([P, EQ, P]),
                                        ALU.add).then_inc(biased, 1)
                dve.wait_ge(biased, i.times(2, 2))
                dve.wait_ge(edge_full, i.g + 1)
                nc.vector.tensor_tensor(o, Z[i.k % 2][:, :], o, ALU.add).then_inc(edge_done, 1)

            def body(i):
                nodes(i)
                edges(i)

            loop(dve, 0, ND - 1, body)
            nodes(TAIL, DTAIL)
            edges(TAIL)

        @block.tensor
        def _(pe):
            batch_norm.tensor(pe)
            def body(i):
                k, n = i.k % 4, DTAIL if i.known and i.g == ND - 1 else P
                pe.wait_ge(s_y0[k], i.quarter * 16 + 16)
                for m in range(2):
                    wait(pe, node_done, i.g - 1)
                    for q in range(EQ):
                        c = (m * EQ + q) * n
                        ins = nc.tensor.matmul(D[(2 * i.k + m) % 4][0:n, q * P:(q + 1) * P], y0[k][:, c:c + n],
                                               t.W2s[:, :], start=True, stop=True)
                    ins.then_inc(node_full, 1)
                if not resident(i):
                    pe.wait_ge(s_y1[k], i.quarter * 16 + 16)
                wait(pe, edge_done, i.g - 1)
                hidden, o = (r.y1, (i.g - RESIDENT) * EG) if resident(i) else (y1[k], 0)
                for q in range(EQ):
                    ins = nc.tensor.matmul(Z[i.k % 2][:, q * P:(q + 1) * P], hidden[:, o + q:o + EG:EQ], t.W2s[:, :],
                                           start=True, stop=True)
                ins.then_inc(edge_full, 1)

            unrolled(pe, 0, 4, RESIDENT, ND, body)

        @block.scalar
        def _(act):
            batch_norm.scalar(act)
            def stage(g):
                k = g.k % 4
                wait(act, s_scattered[k], g.quarter * 64)
                act.wait_ge(edge_done, g.g + 1)
                nc.scalar.copy(sidx[k][:, :], where[:, bass.ds(g.g, 1), :].rearrange("p a q -> p (a q)"))
                nc.scalar.copy(staged[k][:, :], t.x1[:, bass.ds(g.times(EG), EG)]).then_inc(s_staged, 1)

            act.wait_ge(r.s_where, 16)
            loop(act, 0, NEG, stage, by_hand=4)

        @block.gpsimd
        def _(pool):
            wait(pool, need_done, 1)

            def scatter(g):
                k = g.k % 4
                wait(pool, s_staged, g.g + 1)
                rank = pool.value_load(need[0:1, bass.ds(g.g, 1)], min_val=1, max_val=ND)
                wait(pool, nodes_written, rank)
                for q in range(EQ):
                    pool.indirect_dma_start(
                        out=out[:, :], out_offset=bass.IndirectOffsetOnAxis(ap=sidx[k][:, q:q + 1], axis=0),
                        in_=staged[k][:, q * P:(q + 1) * P], in_offset=None, bounds_check=N - 1, oob_is_err=False
                    ).then_inc(s_scattered[k], 16)

            loop(pool, 0, NEG, scatter)
            for i in range(4):
                wait(pool, s_scattered[i], 64 * len(range(i, NEG, 4)))




class Tiles:

    def __init__(self, a):
        self.x1 = a.sb("x1", [P, EPAD])
        (self.W_srcT, self.W_dstT, self.W_edgeT, self.W1T, self.W2T, self.W2s, self.A_pos, self.A_neg, self.ident,
         self.b_row) = (a.sb(n, [P, P]) for n in ("W_srcT", "W_dstT", "W_edgeT", "W1T", "W2T", "W2s", "A_pos", "A_neg",
                                                  "ident", "b_row"))
        self.unsorted = a.sb("unsorted", [1, 1], I32)
        self.ones_row, self.ones_row_bf, self.b2_row = a.sb("ones_row", [1, P]), a.sb("ones_row_bf", [1, P], BF16), \
            a.sb("b2_row", [1, P])
        (self.b_src, self.b_dst, self.attn, self.b1, self.gamma, self.beta, self.b_sum, self.b_sum_neg) = (
            a.sb(n, [P, 1]) for n in ("b_src", "b_dst", "attn", "b1", "gamma", "beta", "b_sum", "b_sum_neg"))
        self.columns = (("b_src", self.b_src), ("b_dst", self.b_dst), ("attn", self.attn), ("b1", self.b1),
                        ("gamma", self.gamma), ("beta", self.beta), ("b2", self.b2_row))
        self.columns_loaded = a.sem("columns_loaded")
        self.cols, o = {}, 0
        for n, w in (("node", 2 * ND), ("node_sq", ND), ("edge_old", NEG), ("edge_old_sq", NEG),
                     ("edge_new", NEG), ("edge_new_sq", NEG)):
            self.cols[n] = (o, w)
            o += w
        self.sums = a.sb("sums", [P, o])

    def col(self, name, i):
        return self.sums[:, bass.ds(self.cols[name][0] + i, 1)]


class Scratch:

    def __init__(self, nc):
        def dram(name, shape, dt=F32):
            return nc.dram_tensor(name, list(shape), dt, kind="Internal").ap()

        self.src, self.dst = dram("src_sorted", (E, 1), I32), dram("dst_sorted", (E, 1), I32)
        self.attr = dram("edge_attr_sorted", (E, P))
        self.gather = dram("gather_rows", (2, EPAD), I32)
        self.scatter = dram("scatter_rows", (EPAD,), I32)
        self.keep, self.start, self.last = (dram(n, (EPAD,), BF16) for n in ("keep", "start", "last"))
        self.y0 = dram("y_nodes", (P, N))
        self.y1 = dram("y_edges", (P, EPAD))


def program(nc, x, src, dst, edge_attr, W_src, b_src, W_dst, b_dst, W_edge, attn, W1, b1, gamma, beta, W2, b2, out):
    d = Scratch(nc)

    def column(v):
        return v.rearrange("(f o) -> f o", o=1)

    w = {"W_src": W_src, "W_dst": W_dst, "W_edge": W_edge, "W1": W1, "W2": W2, "b_src": column(b_src),
         "b_dst": column(b_dst), "attn": attn.rearrange("h (f o) -> (h f) o", o=1), "b1": column(b1),
         "gamma": column(gamma), "beta": column(beta), "b2": b2.unsqueeze(0)}
    with ExitStack() as ctx:
        t = Tiles(Allocator(nc, ctx, "t"))
        edge_order(nc, t, w, d, src, dst)
        sort_edges(nc, t, d, src, dst, edge_attr)
        tables(nc, t, w, d)
        attention(nc, t, d, x, edge_attr, out)
        r = Ahead(Allocator(nc, ctx, "ahead"), d, x)
        aggregation(nc, t, r, d, out)
        result(nc, t, r, d, out)


_INS = ['x', 'src', 'dst', 'edge_attr_128', 'L0_gnn_W_src', 'L0_gnn_b_src', 'L0_gnn_W_dst', 'L0_gnn_b_dst',
        'L0_gnn_W_edge', 'L0_gnn_attn', 'L1_gnn_W1', 'L1_gnn_b1', 'L1_gnn_gamma', 'L1_gnn_beta', 'L1_gnn_W2',
        'L1_gnn_b2']


def kernel(**inputs):
    import concourse.bacc as _bacc
    from concourse.bass_utils import run_bass_kernel_spmd as _run

    nc = _bacc.Bacc("TRN2", target_bir_lowering=False, num_devices=1)
    arrays, args = {}, []
    for name in _INS:
        v = np.ascontiguousarray(inputs[name])
        arrays[f"in_{name}"] = v
        args.append(nc.dram_tensor(f"in_{name}", v.shape, mybir.dt.from_np(v.dtype), kind="ExternalInput").ap())
    args.append(nc.dram_tensor("out_0", (N, P), F32, kind="ExternalOutput").ap())
    program(nc, *args)
    return _run(nc, [arrays], core_ids=[0]).results[0]["out_0"]
```
